# Optimizing a Trainium2 kernel written in Bass

```python
import numpy as np
import jax
import jax.numpy as jnp

def _softmax(x, axis=-1):
    return jax.nn.softmax(x, axis=axis)

def _gelu(x):
    return jax.nn.gelu(x, approximate=True)

def _silu(x):
    return jax.nn.silu(x)

def _sigmoid(x):
    return jax.nn.sigmoid(x)

def _layernorm(x, axis=-1, eps=1e-05):
    m = jnp.mean(x, axis=axis, keepdims=True)
    v = jnp.var(x, axis=axis, keepdims=True)
    return (x - m) / jnp.sqrt(v + eps)

def _scatter_add(tgt, idx, src, axis=0):
    return tgt.at[idx].add(src)

def _segment_sum(src, seg, n):
    return jax.ops.segment_sum(src, seg, n)
kernel_name = 'mk_gnn_resnorm_d2_gnn_r8_d99752'

def setup_inputs(seed: int=0):
    np.random.seed(seed)
    _w = jnp.asarray

    def _rec_inputs():
        import jax
        import jax.numpy as jnp
        _gk = jax.random.key(seed)
        x = -0.0009044 + 1 * jax.random.normal(jax.random.fold_in(_gk, 1), (12500, 32), jnp.float32)
        _s = jax.random.randint(jax.random.fold_in(_gk, 2), (200000,), 0, 12500, jnp.int32)
        _d = jax.random.randint(jax.random.fold_in(_gk, 3), (200000,), 0, 12500, jnp.int32)
        _loop = jnp.arange(12500, dtype=jnp.int32)
        src = jnp.concatenate([_s, _d, _loop])
        dst = jnp.concatenate([_d, _s, _loop])
        _o = jnp.argsort(dst, stable=True)
        src = src[_o]
        dst = dst[_o]
        edge_attr_32 = 0.000196303 + 1.00016 * jax.random.normal(jax.random.fold_in(_gk, 11), (412500, 32), jnp.float32)
        return (x, src, dst, edge_attr_32)
    x, src, dst, edge_attr_32 = _rec_inputs()

    def _L0_gnn_setup():
        import jax, jax.numpy as jnp
        import numpy as np
        N_NODES = 6250
        N_EDGES = 100000
        X_DIM = 32
        E_DIM = 32
        HID = 64
        OUT = 32
        key = jax.random.key(seed)
        ks = jax.random.split(key, 6)
        x = jax.random.normal(ks[0], (N_NODES, X_DIM), dtype=jnp.float32)
        edge_index = jax.random.randint(ks[1], (2, N_EDGES), 0, N_NODES, dtype=jnp.int64)
        edge_attr = jax.random.normal(ks[2], (N_EDGES, E_DIM), dtype=jnp.float32)
        in_dim = 2 * X_DIM + E_DIM
        W1 = jax.random.normal(ks[3], (in_dim, HID), dtype=jnp.float32) * (1.0 / np.sqrt(in_dim))
        b1 = jnp.zeros((HID,), dtype=jnp.float32)
        W2 = jax.random.normal(ks[4], (HID, OUT), dtype=jnp.float32) * (1.0 / np.sqrt(HID))
        b2 = jnp.zeros((OUT,), dtype=jnp.float32)
        return {'x': x, 'edge_index': edge_index, 'edge_attr': edge_attr, 'W1': W1, 'b1': b1, 'W2': W2, 'b2': b2}
    _L0_gnn_all = _L0_gnn_setup()
    _L0_gnn_in = {k: v for k, v in _L0_gnn_all.items() if k in ('W1', 'b1', 'W2', 'b2')}
    del _L0_gnn_all

    def _L1_gnn_setup():
        import jax, jax.numpy as jnp
        import numpy as np
        N_NODES = 12500
        N_EDGES = 400000
        D = 32

        def _gat(x, edge_index, W, att_s, att_d, bias, heads, ch, neg_slope):
            n = x.shape[0]
            h = (x @ W.T).reshape(n, heads, ch)
            a_s = (h * att_s[None]).sum(-1)
            a_d = (h * att_d[None]).sum(-1)
            src, dst = (edge_index[0], edge_index[1])
            logits = jax.nn.leaky_relu(a_s[src] + a_d[dst], neg_slope)
            m = jax.ops.segment_max(logits, dst, num_segments=n)
            m = jnp.where(jnp.isfinite(m), m, 0.0)
            ex = jnp.exp(logits - m[dst])
            denom = jax.ops.segment_sum(ex, dst, num_segments=n)
            alpha = ex / (denom[dst] + 1e-16)
            out = jax.ops.segment_sum(alpha[:, :, None] * h[src], dst, num_segments=n)
            return out.reshape(n, heads * ch) + bias
        key = jax.random.key(seed)
        ks = jax.random.split(key, 16)
        x = jax.random.normal(ks[0], (N_NODES, D), dtype=jnp.float32)
        edge_index = jax.random.randint(ks[1], (2, N_EDGES), 0, N_NODES, dtype=jnp.int64)
        s = 1.0 / np.sqrt(D)
        return {'x': x, 'edge_index': edge_index, 'W1': jax.random.normal(ks[2], (32, D), dtype=jnp.float32) * s, 'att_s1': jax.random.normal(ks[3], (2, 16), dtype=jnp.float32) * 0.05, 'att_d1': jax.random.normal(ks[4], (2, 16), dtype=jnp.float32) * 0.05, 'b1': jnp.full((32,), 0.1, dtype=jnp.float32), 'ea1': jnp.ones((1,), dtype=jnp.float32), 'W2': jax.random.normal(ks[5], (32, 32), dtype=jnp.float32) * s, 'att_s2': jax.random.normal(ks[6], (2, 16), dtype=jnp.float32) * 0.05, 'att_d2': jax.random.normal(ks[7], (2, 16), dtype=jnp.float32) * 0.05, 'b2': jnp.full((32,), 0.1, dtype=jnp.float32), 'W3': jax.random.normal(ks[8], (32, 32), dtype=jnp.float32) * s, 'att_s3': jax.random.normal(ks[9], (1, 32), dtype=jnp.float32) * 0.05, 'att_d3': jax.random.normal(ks[10], (1, 32), dtype=jnp.float32) * 0.05, 'b3': jnp.full((32,), 0.1, dtype=jnp.float32)}
    _L1_gnn_all = _L1_gnn_setup()
    _L1_gnn_in = {k: v for k, v in _L1_gnn_all.items() if k in ('W1', 'att_s1', 'att_d1', 'b1', 'ea1', 'W2', 'att_s2', 'att_d2', 'b2', 'W3', 'att_s3', 'att_d3', 'b3')}
    del _L1_gnn_all
    return {'x': x, 'src': src, 'dst': dst, 'edge_attr_32': edge_attr_32, 'L0_gnn_W1': _L0_gnn_in['W1'], 'L0_gnn_b1': _L0_gnn_in['b1'], 'L0_gnn_W2': _L0_gnn_in['W2'], 'L0_gnn_b2': _L0_gnn_in['b2'], 'L1_gnn_W1': _L1_gnn_in['W1'], 'L1_gnn_att_s1': _L1_gnn_in['att_s1'], 'L1_gnn_att_d1': _L1_gnn_in['att_d1'], 'L1_gnn_b1': _L1_gnn_in['b1'], 'L1_gnn_ea1': _L1_gnn_in['ea1'], 'L1_gnn_W2': _L1_gnn_in['W2'], 'L1_gnn_att_s2': _L1_gnn_in['att_s2'], 'L1_gnn_att_d2': _L1_gnn_in['att_d2'], 'L1_gnn_b2': _L1_gnn_in['b2'], 'L1_gnn_W3': _L1_gnn_in['W3'], 'L1_gnn_att_s3': _L1_gnn_in['att_s3'], 'L1_gnn_att_d3': _L1_gnn_in['att_d3'], 'L1_gnn_b3': _L1_gnn_in['b3']}

def reference(x, src, dst, edge_attr_32, L0_gnn_W1, L0_gnn_b1, L0_gnn_W2, L0_gnn_b2, L1_gnn_W1, L1_gnn_att_s1, L1_gnn_att_d1, L1_gnn_b1, L1_gnn_ea1, L1_gnn_W2, L1_gnn_att_s2, L1_gnn_att_d2, L1_gnn_b2, L1_gnn_W3, L1_gnn_att_s3, L1_gnn_att_d3, L1_gnn_b3):
    import jax
    import jax.numpy as jnp

    def _L0_gnn_ref(x, edge_index, edge_attr, W1, b1, W2, b2):
        import jax, jax.numpy as jnp
        import numpy as np
        N_NODES = 6250
        N_EDGES = 100000
        X_DIM = 32
        E_DIM = 32
        HID = 64
        OUT = 32
        num_nodes = x.shape[0]
        rol, col = (edge_index[0], edge_index[1])
        e_feat = jnp.concatenate([x[rol], x[col], edge_attr], axis=-1)
        h = jax.nn.relu(e_feat @ W1 + b1)
        v = h @ W2 + b2
        x_cand = jax.ops.segment_max(v, col, num_segments=num_nodes)
        return jnp.maximum(x_cand, x[:, -v.shape[-1]:])

    def _L1_gnn_ref(x, edge_index, W1, att_s1, att_d1, b1, ea1, W2, att_s2, att_d2, b2, W3, att_s3, att_d3, b3):
        import jax, jax.numpy as jnp
        import numpy as np
        N_NODES = 12500
        N_EDGES = 400000
        D = 32

        def _gat(x, edge_index, W, att_s, att_d, bias, heads, ch, neg_slope):
            n = x.shape[0]
            h = (x @ W.T).reshape(n, heads, ch)
            a_s = (h * att_s[None]).sum(-1)
            a_d = (h * att_d[None]).sum(-1)
            src, dst = (edge_index[0], edge_index[1])
            logits = jax.nn.leaky_relu(a_s[src] + a_d[dst], neg_slope)
            m = jax.ops.segment_max(logits, dst, num_segments=n)
            m = jnp.where(jnp.isfinite(m), m, 0.0)
            ex = jnp.exp(logits - m[dst])
            denom = jax.ops.segment_sum(ex, dst, num_segments=n)
            alpha = ex / (denom[dst] + 1e-16)
            out = jax.ops.segment_sum(alpha[:, :, None] * h[src], dst, num_segments=n)
            return out.reshape(n, heads * ch) + bias
        h = _gat(x, edge_index, W1, att_s1, att_d1, b1, heads=2, ch=16, neg_slope=0.01)
        scale = jnp.tanh(ea1)[0]
        scale = jnp.where(scale < 0.1, 1.0, scale)
        h = h * scale
        h = h + 0.05 * jax.lax.stop_gradient(h)
        h = jax.nn.elu(h)
        h = jnp.clip(h, -3.0, 3.0)
        h = _gat(h, edge_index, W2, att_s2, att_d2, b2, heads=2, ch=16, neg_slope=0.2)
        h = jax.nn.elu(h)
        h = jnp.clip(h, -3.0, 3.0)
        out = _gat(h, edge_index, W3, att_s3, att_d3, b3, heads=1, ch=32, neg_slope=0.2)
        return out
    edge_index = jnp.stack([src, dst])
    x = _layernorm(x + _L0_gnn_ref(x, edge_index, edge_attr_32, L0_gnn_W1, L0_gnn_b1, L0_gnn_W2, L0_gnn_b2), axis=-1)
    x = _layernorm(x + _L1_gnn_ref(x, edge_index, L1_gnn_W1, L1_gnn_att_s1, L1_gnn_att_d1, L1_gnn_b1, L1_gnn_ea1, L1_gnn_W2, L1_gnn_att_s2, L1_gnn_att_d2, L1_gnn_b2, L1_gnn_W3, L1_gnn_att_s3, L1_gnn_att_d3, L1_gnn_b3), axis=-1)
    return x

_drawn_inputs = setup_inputs


def setup_inputs(seed=0):
    import zlib

    import numpy as np

    out = dict(_drawn_inputs(seed))
    spreads = {'L0_gnn_b1': (0.0, 0.1),
     'L0_gnn_b2': (0.0, 0.1),
     'L1_gnn_b1': (0.10000000149011612, 0.6),
     'L1_gnn_b2': (0.10000000149011612, 0.6),
     'L1_gnn_b3': (0.10000000149011612, 0.6)}
    factors = {'L1_gnn_att_d1': 200.0,
     'L1_gnn_att_s2': 55.376,
     'L1_gnn_att_d2': 200.0,
     'L1_gnn_att_s3': 200.0,
     'L1_gnn_att_d3': 200.0}
    for name, (base, spread) in spreads.items():
        noise = np.random.default_rng([zlib.crc32(name.encode()), seed]).standard_normal(out[name].shape)
        drawn = base * np.exp(spread * noise) if base else spread * noise
        out[name] = jnp.asarray(drawn.astype(out[name].dtype))
    for name, factor in factors.items():
        out[name] = (out[name] * factor).astype(out[name].dtype)
    return out
```

```python
import concourse.bass as bass
from concourse import mybir
from contextlib import ExitStack

F32 = mybir.dt.float32
BF16 = mybir.dt.bfloat16
I32 = mybir.dt.int32
ALU = mybir.AluOpType
ACT = mybir.ActivationFunctionType
X = mybir.AxisListType.X

P = 128
LOW = -3.0e38
ROUND = 12582912.0


def gnn_program(nc, x, src, dst, edge, w1, b1, w2, b2, gat, ea1, out):
    N, D = x.shape
    E = src.shape[0]
    HID = w1.shape[1]
    COLS = -(-E // P)
    EP = P * COLS
    REAL = E - (P - 1) * COLS
    NCOL = -(-N // P)
    NP = P * NCOL
    NREAL = N - (P - 1) * NCOL
    CB = 64
    NB = COLS // CB
    TAIL = COLS - NB * CB
    ROUNDS = NB // 2
    assert NB == 2 * ROUNDS and 0 < TAIL and REAL > (NB - 1) * CB and REAL < NB * CB
    assert 0 < NREAL < NCOL and EP + NP < 1 << 24
    GW = 4
    GB = CB // GW
    GT = -(-TAIL // GW)
    HW = 18
    ROW = 2 * HW
    KD = ROW + 2
    OH = 16
    OHN = COLS // OH
    OHT = COLS - OHN * OH
    NQ = -(-NCOL // 4)
    ZW = 586
    assert COLS % 11 == 0 and 2 * COLS == 11 * ZW
    LOADS = 5 + 3 * 6
    SLOPES = [0.01, 0.2, 0.2]

    xd_d = nc.dram_tensor("xd_d", (EP + NP, D), F32, kind="Internal").ap()
    ad_d = nc.dram_tensor("ad_d", (EP + NP, 2), F32, kind="Internal").ap()
    scan0_d = nc.dram_tensor("scan0_d", (EP, D), F32, kind="Internal").ap()
    scan_d = nc.dram_tensor("scan_d", (EP, ROW), F32, kind="Internal").ap()
    table_d = nc.dram_tensor("table_d", (NP, ROW), F32, kind="Internal").ap()
    adn_d = nc.dram_tensor("adn_d", (NP, 2), F32, kind="Internal").ap()
    xd_v = xd_d[0:EP, :].rearrange("(p j) f -> p j f", p=P)
    ad_v = ad_d[0:EP, :].rearrange("(p j) h -> p j h", p=P)
    scan0_v = scan0_d.rearrange("(p j) f -> p j f", p=P)
    scan_v = scan_d.rearrange("(p j) f -> p j f", p=P)

    ctx = ExitStack()
    with ctx:
        def sb(name, shape, dt=F32):
            return ctx.enter_context(nc.sbuf_tensor(name, shape, dt))

        def sem(name):
            return ctx.enter_context(nc.semaphore(name))

        src_i = sb("src_i", [P, COLS], I32)
        index = sb("index", [P, 2, CB], I32)
        dst_f = sb("dst_f", [P, COLS])
        same = sb("same", [P, COLS])
        reset = sb("reset", [P, COLS])
        adf = sb("adf", [P, COLS, 2])
        hi_f = adf[:, :, :].rearrange("p j h -> p (j h)")[:, 0:COLS]
        lo_f = adf[:, :, :].rearrange("p j h -> p (j h)")[:, COLS:2 * COLS]
        ring0 = sb("ring0", [P, 2 * 3 * CB * D])
        slot0 = [ring0[:, k * 3 * CB * D:(k + 1) * 3 * CB * D].rearrange("p (j f) -> p j f", f=3 * D)
                 for k in range(2)]
        work = ring0[:, 0:4 * NQ * D].rearrange("p (c f) -> p c f", f=D)
        work2 = ring0[:, 4 * NQ * D:8 * NQ * D].rearrange("p (c f) -> p c f", f=D)
        tab = ring0[:, 8 * NQ * D:8 * NQ * D + 4 * NQ * ROW].rearrange("p (c f) -> p c f", f=ROW)
        ringg = sb("ringg", [P, 2 * CB * ROW])
        slotg = [ringg[:, k * CB * ROW:(k + 1) * CB * ROW].rearrange("p (j f) -> p j f", f=ROW)
                 for k in range(2)]
        spread = [ringg[:, k * CB * D:(k + 1) * CB * D].rearrange("p (j f) -> p j f", f=D) for k in range(2)]
        adf_flat = adf[:, :, :].rearrange("p j h -> p (j h)")
        attr = [adf_flat[:, k * CB * D:(k + 1) * CB * D].rearrange("p (j f) -> p j f", f=D) for k in range(2)]
        zeros = ringg[:, 0:ZW]
        OHB = OH * (P + NCOL)
        onehot = [ringg[:, ZW + k * OHB // 2:ZW + (k + 1) * OHB // 2].bitcast(BF16) for k in range(2)]
        oh_hi = [o[:, 0:OH * P].rearrange("p (j n) -> p j n", n=P) for o in onehot]
        oh_lo = [o[:, OH * P:OHB].rearrange("p (j n) -> p j n", n=NCOL) for o in onehot]
        digits = sb("digits", [P, 2, 2 * OH])
        xt_sb = sb("xt_sb", [P, 2, 512])
        h_sb = sb("h_sb", [HID, 2, 512])
        same_b = sb("same_b", [P, CB])
        reset_b = sb("reset_b", [P, CB])
        fillc = sb("fillc", [P, D])
        maxc = sb("maxc", [P, ROW])
        lg = sb("lg", [P, 2, CB])
        mx = sb("mx", [P, 2, CB + 1])
        ex_in = sb("ex_in", [P, 2, 2, CB])
        ex = sb("ex", [P, 2, 2, CB])
        sumc = sb("sumc", [P, ROW])
        x1 = sb("x1", [P, 4 * NQ, D])
        xn = x1[:, 0:NCOL, :]
        nd = sb("nd", [P, NCOL, ROW])
        adt = sb("adt", [P, 4 * NQ, 2])
        deg = sb("deg", [P, NCOL])
        cum = sb("cum", [P, NCOL])
        has = sb("has", [P, NCOL])
        pen = sb("pen", [P, NCOL])
        nt = sb("nt", [P, 4, NCOL])
        rden = sb("rden", [P, NCOL, 2])
        spare_i = sb("spare_i", [P, NCOL], I32)
        spare = sb("spare", [P, NCOL])
        start_i = sb("start_i", [P, NCOL], I32)
        end_i = sb("end_i", [P, NCOL], I32)
        onesn = sb("onesn", [P, NCOL])
        before = sb("before", [P, 1])
        dst0_i = sb("dst0_i", [P, 1], I32)
        prev_i = sb("prev_i", [P, 1], I32)
        prev_f = sb("prev_f", [P, 1])
        cont = sb("cont", [P, 1])
        cmask = sb("cmask", [P, 1])
        wmask = sb("wmask", [P, ROW])
        pt = sb("pt", [P, 4])
        row0_i = sb("row0_i", [P, 1], I32)
        fe_i = sb("fe_i", [P, 1], I32)
        x0 = sb("x0", [P, D])
        a0 = sb("a0", [P, 2])
        tot = sb("tot", [P, 1])
        mrep = sb("mrep", [P, ROW])
        wm_t = sb("wm_t", [ROW, P])
        m_t = sb("m_t", [ROW, P])
        mi_t = sb("mi_t", [ROW, P + 1])
        si_t = sb("si_t", [ROW, P + 1])
        te_in = sb("te_in", [ROW, 2, P])
        te = sb("te", [ROW, 2, P])
        fix = sb("fix", [P, ROW])
        fo = sb("fo", [P, ROW])
        cs = sb("cs", [P, ROW])
        cm = sb("cm", [P, 2])
        vm = sb("vm", [P, 2])
        fe_in = sb("fe_in", [P, 2, 2])
        fe = sb("fe", [P, 2, 2])
        ident = sb("ident", [P, P])
        upper = sb("upper", [P, P])
        iota_i = sb("iota_i", [P, P], I32)
        iota_b = sb("iota_b", [P, P], BF16)
        w1_sb = sb("w1_sb", [3 * D, HID])
        w2_sb = sb("w2_sb", [HID, D])
        b1_sb = sb("b1_sb", [HID, 1])
        b2_sb = sb("b2_sb", [P, D])
        bg_sb = sb("bg_sb", [P, 3, D])
        gw_sb = sb("gw_sb", [D, 3, D])
        pick = sb("pick", [D, 3, KD])
        wc_sb = sb("wc_sb", [D, 3, KD])
        wd_sb = sb("wd_sb", [P, 3, 4 * KD])
        ea_sb = sb("ea_sb", [P, 1])
        sc = sb("sc", [P, 4])
        sc_out = sb("sc_out", [P, 1])

        psum = ctx.enter_context(nc.psum_tensor("psum", [P, 8 * 512], F32))
        t_ps = [psum[:, k * 512:(k + 1) * 512] for k in range(2)]
        h_ps = [psum[:, (2 + k) * 512:(3 + k) * 512] for k in range(2)]
        v_ps = psum[:, 4 * 512:8 * 512].rearrange("p (j f) -> p j f", f=D)
        count_ps = psum[:, 4 * 512:4 * 512 + NCOL]
        before_ps = psum[:, 5 * 512:5 * 512 + 1]
        wc_ps = psum[0:D, 6 * 512:6 * 512 + 3 * KD].rearrange("p (l k) -> p l k", l=3)

        s_src = sem("s_src")
        s_dst = sem("s_dst")
        s_prev = sem("s_prev")
        s_x = sem("s_x")
        s_w = sem("s_w")
        s_pads = sem("s_pads")
        s_zs = sem("s_zs")
        s_zero = sem("s_zero")
        s_const = sem("s_const")
        s_pool = sem("s_pool")
        s_index = sem("s_index")
        s_begun = sem("s_begun")
        s_wc = sem("s_wc")
        s_wcs = sem("s_wcs")
        s_wd = sem("s_wd")
        s_wz = sem("s_wz")
        s_v = sem("s_v")
        s_oh = sem("s_oh")
        s_ohd = sem("s_ohd")
        s_b0 = sem("s_b0")
        s_own = sem("s_own")
        s_cnt = sem("s_cnt")
        s_tot = sem("s_tot")
        s_bef = sem("s_bef")
        s_idx = sem("s_idx")
        s_xs = [sem(f"s_xs{k}") for k in range(2)]
        s_xd = [sem(f"s_xd{k}") for k in range(2)]
        s_ed = [sem(f"s_ed{k}") for k in range(2)]
        s_st0 = [sem(f"s_st_max{k}") for k in range(2)]
        s_xscat = sem("s_xscat")
        s_x0 = sem("s_x0")
        s_xrow = sem("s_xrow")
        s_fill = sem("s_fill")
        s_t = sem("s_t")
        s_tc = sem("s_tc")
        s_h = sem("s_h")
        s_hr = sem("s_hr")
        s_vp = sem("s_vp")
        s_max = sem("s_max")
        s_g = [[sem(f"s_g{l}_{k}") for k in range(2)] for l in range(3)]
        s_st = [[sem(f"s_st{l}_{k}") for k in range(2)] for l in range(3)]
        s_exin = sem("s_exin")
        s_ex = sem("s_ex")
        s_sum = sem("s_sum")
        s_tail = sem("s_tail")
        s_tailt = sem("s_tailt")
        s_tein = sem("s_tein")
        s_te = sem("s_te")
        s_car = sem("s_car")
        s_cart = sem("s_cart")
        s_fein = sem("s_fein")
        s_fe = sem("s_fe")
        s_fixg = sem("s_fixg")
        s_fixv = sem("s_fixv")
        s_fixs = sem("s_fixs")
        s_nd = sem("s_nd")
        s_ain = sem("s_ain")
        s_aout = sem("s_aout")
        s_node = sem("s_node")
        s_nt = sem("s_nt")
        s_ntc = sem("s_ntc")
        s_np = sem("s_np")
        s_npc = sem("s_npc")
        s_tab = sem("s_tab")
        s_tabd = sem("s_tabd")
        s_ascat = sem("s_ascat")
        s_a0 = sem("s_a0")
        s_arow = sem("s_arow")
        s_adf = sem("s_adf")
        s_fin = sem("s_fin")
        s_out = sem("s_out")

        block = ctx.enter_context(nc.Block())

        def split_rows(ap, per, real):
            whole = ap[0:(P - 1) * per].rearrange("(p j) -> p j", j=per)
            last = ap[(P - 1) * per:(P - 1) * per + real].rearrange("(p j) -> p j", p=1)
            return ((slice(0, 112), per, whole[0:112, :]), (slice(112, P - 1), per, whole[112:P - 1, :]),
                    (slice(P - 1, P), real, last))

        @block.sync
        def _(sp):
            sp.wait_ge(s_pads, 1)
            for rows, n, part in split_rows(dst, COLS, REAL):
                sp.dma_start(hi_f.bitcast(I32)[rows, 0:n], part).then_inc(s_dst, 16)
            for rows, n, part in split_rows(src, COLS, REAL):
                sp.dma_start(src_i[rows, 0:n], part).then_inc(s_src, 16)
            sp.dma_start(prev_i[1:P, :], dst[COLS - 1:E:COLS].unsqueeze(1),
                         allow_slow_non_contiguous=True).then_inc(s_prev, 16)
            xn_flat = xn.rearrange("p c f -> p (c f)")
            for rows, n, part in split_rows(x.rearrange("n f -> (n f)"), NCOL * D, NREAL * D):
                sp.dma_start(xn_flat[rows, 0:n], part).then_inc(s_x, 16)
            sp.wait_ge(s_wcs, 1)
            sp.wait_ge(s_wz, 1)
            for l in range(3):
                for q in range(4):
                    sp.dma_start(wd_sb[q * D:(q + 1) * D, l, q * KD:(q + 1) * KD], wc_sb[:, l, :]).then_inc(s_wd, 16)

            def load_edges(b, k, j0):
                n = CB if b < NB else TAIL
                for rows in (slice(0, 112), slice(112, P - 1)):
                    flat = edge[0:(P - 1) * COLS, :].rearrange("(p j) f -> p j f", j=COLS)
                    sp.dma_start(attr[k][rows, 0:n, :], flat[rows, j0:j0 + n, :]).then_inc(s_ed[k], 16)
                real = min(max(REAL - j0, 0), n)
                if real:
                    first = (P - 1) * COLS + j0
                    sp.dma_start(attr[k][P - 1:P, 0:real, :],
                                 edge[first:first + real, :].rearrange("(p j) f -> p j f", p=1)).then_inc(s_ed[k], 16)

            def load_spread(k, j0, n):
                sp.dma_start(spread[k][:, 0:n, :], xd_v[:, bass.ds(j0, n), :]).then_inc(s_xd[k], 16)

            edge_v = bass.AP(tensor=edge.tensor, offset=0, ap=[[COLS * D, P], [D, (NB - 1) * CB], [1, D]])

            def load_whole(k, j0):
                sp.dma_start(attr[k], edge_v[:, bass.ds(j0, CB), :]).then_inc(s_ed[k], 16)

            def store_max(k, j0, n, done):
                sp.wait_ge(s_max, done)
                sp.dma_start(scan0_v[:, bass.ds(j0, n), :], spread[k][:, 0:n, :]).then_inc(s_st0[k], 16)

            sp.wait_ge(s_idx, 1)
            load_whole(0, 0)
            load_whole(1, CB)
            sp.wait_ge(s_xscat, 16 * NCOL)
            sp.wait_ge(s_x0, 16)
            sp.dma_start(xd_v[:, 0, :], x0[:, :]).then_inc(s_xrow, 16)
            sp.wait_ge(s_xrow, 16)
            load_spread(0, 0, CB)
            load_spread(1, CB, CB)
            store_max(0, 0, CB, 1)
            with sp.Fori(1, ROUNDS - 1) as r:
                for k in range(2):
                    sp.wait_ge(s_fill, r * 2 + (k - 1))
                    load_whole(k, r * (2 * CB) + k * CB)
                    sp.wait_ge(s_st0[k], r * 16)
                    load_spread(k, r * (2 * CB) + k * CB, CB)
                    store_max(1 - k, r * (2 * CB) + (k - 1) * CB, CB, r * 2 + k)
            for b in range(NB - 2, NB + 1):
                k = b % 2
                n = CB if b < NB else TAIL
                sp.wait_ge(s_fill, b - 1)
                if b == NB - 2:
                    load_whole(k, b * CB)
                else:
                    load_edges(b, k, b * CB)
                sp.wait_ge(s_st0[k], b // 2 * 16)
                load_spread(k, b * CB, n)
                store_max(1 - k, (b - 1) * CB, CB, b)
            store_max(NB % 2, NB * CB, TAIL, NB + 1)

            for l in range(3):
                sp.wait_ge(s_tab, l + 1)
                sp.dma_start(table_d.rearrange("(p c) f -> p c f", p=P), tab[:, 0:NCOL, :]).then_inc(s_tabd, 16)
                sp.dma_start(adn_d.rearrange("(p c) f -> p c f", p=P), adt[:, 0:NCOL, :]).then_inc(s_tabd, 16)
                sp.wait_ge(s_ascat, 16 * NCOL * (l + 1))
                sp.wait_ge(s_a0, 16 * (l + 1))
                sp.dma_start(ad_v[:, 0, :], a0[:, :]).then_inc(s_arow, 16)
                sp.wait_ge(s_arow, 16 * (l + 1))
                sp.dma_start(adf[:, :, :], ad_v).then_inc(s_adf, 16)

                done = l * (NB + 1)

                def store_sum(k, j0, n, blocks):
                    sp.wait_ge(s_sum, blocks)
                    sp.dma_start(scan_v[:, bass.ds(j0, n), :], slotg[k][:, 0:n, :]).then_inc(s_st[l][k], 16)

                with sp.Fori(0, ROUNDS) as r:
                    for k in range(2):
                        store_sum(k, r * (2 * CB) + k * CB, CB, r * 2 + (done + k + 1))
                store_sum(NB % 2, NB * CB, TAIL, done + NB + 1)
            sp.wait_ge(s_fin, 1)
            o_flat = work2[:, 0:NCOL, :].rearrange("p c f -> p (c f)")
            for rows, n, part in split_rows(out.rearrange("n f -> (n f)"), NCOL * D, NREAL * D):
                sp.dma_start(part, o_flat[rows, 0:n]).then_inc(s_out, 16)
            sp.wait_ge(s_out, 48)

        @block.gpsimd
        def _(pool):
            steps = [0]

            def step(ins):
                steps[0] += 1
                ins.then_inc(s_pool, 1)
                pool.wait_ge(s_pool, steps[0])

            step(pool.memset(ident[:, :], 0.0))
            step(pool.affine_select(out=ident[:, :], in_=ident[:, :], compare_op=ALU.not_equal, fill=1.0,
                                    base=0, pattern=[[-1, P]], channel_multiplier=1))
            step(pool.memset(upper[:, :], 1.0))
            step(pool.affine_select(out=upper[:, :], in_=upper[:, :], compare_op=ALU.is_gt, fill=0.0,
                                    base=0, pattern=[[1, P]], channel_multiplier=-1))
            step(pool.iota(iota_i[:, :], pattern=[[1, P]], base=0, channel_multiplier=0))
            step(pool.iota(spare_i[:, :], pattern=[[1, NCOL]], base=EP, channel_multiplier=NCOL))
            step(pool.iota(row0_i[:, :], pattern=[[1, 1]], base=0, channel_multiplier=COLS))
            step(pool.memset(pick[:, :, :], 0.0))
            for l in range(3):
                for h in range(2):
                    part = pick[:, l, h * HW:h * HW + 16]
                    step(pool.affine_select(out=part, in_=part, compare_op=ALU.not_equal, fill=1.0,
                                            base=-16 * h, pattern=[[-1, 16]], channel_multiplier=1))
            pool.memset(wd_sb[:, :, :], 0.0).then_inc(s_wz, 1)
            pool.engine_nop().then_inc(s_const, 1)

            def gather(table, k, j0, n, blocks, row, signal):
                pool.tensor_copy(index[:, k, 0:n], src_i[:, bass.ds(j0, n)]).then_inc(s_index, 1)
                pool.wait_ge(s_index, blocks + 1)
                pool.sem_inc(s_begun, 1)
                for j in range(n):
                    gather_one(row(j), table, index[:, k, j:j + 1], signal)

            def gather_one(rows, table, index, signal):
                pool.indirect_dma_start(out=rows, out_offset=None, in_=table,
                                        in_offset=bass.IndirectOffsetOnAxis(ap=index, axis=0)).then_inc(signal, 16)

            def scatter_one(table, index, rows, signal):
                pool.indirect_dma_start(out=table, out_offset=bass.IndirectOffsetOnAxis(ap=index, axis=0),
                                        in_=rows, in_offset=None).then_inc(signal, 16)

            def join_and_fetch(n_fix, scanned, width):
                gather_one(fix[:, 0:width], scanned, fe_i[:, :], s_fixg)
                pool.wait_ge(s_fixv, n_fix)
                scatter_one(scanned, fe_i[:, :], fo[:, 0:width], s_fixs)
                pool.wait_ge(s_fixs, 16 * n_fix)
                for c in range(NCOL):
                    gather_one(nd[:, c, 0:width], scanned, end_i[:, c:c + 1], s_nd)

            pool.wait_ge(s_src, 48)
            for k in range(2):
                gather(x, k, k * CB, CB, k, lambda j: slot0[k][:, j, 0:D], s_xs[k])
            pool.wait_ge(s_x, 48)
            pool.wait_ge(s_idx, 1)
            pool.wait_ge(s_zero, 32)
            for c in range(NCOL):
                scatter_one(xd_d, start_i[:, c:c + 1], xn[:, c, :], s_xscat)
            gather_one(x0[:, :], x, dst0_i[:, :], s_x0)
            with pool.Fori(1, ROUNDS) as r:
                for k in range(2):
                    pool.wait_ge(s_t, (r * 2 + (k - 1)) * GB)
                    gather(x, k, r * (2 * CB) + k * CB, CB, r * 2 + k, lambda j: slot0[k][:, j, 0:D], s_xs[k])
            pool.wait_ge(s_t, (NB - 1) * GB)
            gather(x, 0, NB * CB, TAIL, NB, lambda j: slot0[0][:, j, 0:D], s_xs[0])
            pool.wait_ge(s_st0[0], 16 * (ROUNDS + 1))
            pool.wait_ge(s_st0[1], 16 * ROUNDS)
            join_and_fetch(1, scan0_d, D)

            for l in range(3):
                done = (l + 1) * (NB + 1)
                pool.wait_ge(s_tabd, 32 * (l + 1))
                for k in range(2):
                    gather(table_d, k, k * CB, CB, done + k, lambda j: slotg[k][:, j, :], s_g[l][k])
                for c in range(NCOL):
                    scatter_one(ad_d, start_i[:, c:c + 1], adt[:, c, :], s_ascat)
                gather_one(a0[:, :], adn_d, dst0_i[:, :], s_a0)
                with pool.Fori(1, ROUNDS) as r:
                    for k in range(2):
                        pool.wait_ge(s_st[l][k], r * 16)
                        gather(table_d, k, r * (2 * CB) + k * CB, CB, r * 2 + (done + k),
                               lambda j: slotg[k][:, j, :], s_g[l][k])
                pool.wait_ge(s_st[l][0], 16 * ROUNDS)
                gather(table_d, 0, NB * CB, TAIL, done + NB, lambda j: slotg[0][:, j, :], s_g[l][0])
                pool.wait_ge(s_st[l][0], 16 * (ROUNDS + 1))
                pool.wait_ge(s_st[l][1], 16 * ROUNDS)
                join_and_fetch(l + 2, scan_d, ROW)

        @block.tensor
        def _(pe):
            pe.wait_ge(s_const, 1)
            pe.wait_ge(s_w, 16 * LOADS)
            for l in range(3):
                last = pe.matmul(wc_ps[:, l, :], gw_sb[:, l, :], pick[:, l, :], start=True, stop=True)
            last.then_inc(s_wc, 1)
            def count(m, k, n, first=False, final=False):
                pe.wait_ge(s_oh, m)
                for j in range(n):
                    last = pe.matmul(count_ps, oh_hi[k][:, j, :], oh_lo[k][:, j, :],
                                     start=first and j == 0, stop=final and j == n - 1, skip_group_check=True)
                last.then_inc(s_cnt, 1)

            count(1, 0, OH, first=True)
            count(2, 1, OH)
            with pe.Fori(1, OHN // 2) as r:
                for k in range(2):
                    count(r * 2 + (k + 1), k, OH)
            for m in range(OHN - OHN % 2, OHN):
                count(m + 1, m % 2, OH)
            count(OHN + 1, OHN % 2, OHT, final=True)
            pe.wait_ge(s_tot, 1)
            pe.matmul(before_ps, upper[:, :], tot[:, :], start=True, stop=True).then_inc(s_bef, 1)

            def block0(k, use, base, blocks, n):
                groups = -(-n // GW)
                pe.wait_ge(s_xs[k], use)
                pe.wait_ge(s_fill, blocks + 1)
                for i in range(groups + 2):
                    if i < groups:
                        if base is not None:
                            pe.wait_ge(s_tc, base + (i - 1))
                        elif i >= 2:
                            pe.wait_ge(s_tc, i - 1)
                        for j in range(GW * i, min(GW * i + GW, n)):
                            q = j - GW * i
                            last = pe.transpose(t_ps[i % 2][0:3 * D, q * P:(q + 1) * P],
                                                slot0[k][:, j, :], ident[:, :])
                        last.then_inc(s_t, 1)
                    if 1 <= i <= groups:
                        g = i - 1
                        w = P * (min(GW * g + GW, n) - GW * g)
                        pe.wait_ge(s_tc, (0 if base is None else base) + (g + 1))
                        if base is not None:
                            pe.wait_ge(s_hr, base + (g - 1))
                        elif g >= 2:
                            pe.wait_ge(s_hr, g - 1)
                        pe.matmul(h_ps[g % 2][0:HID, 0:w], w1_sb[:, :], xt_sb[0:3 * D, g % 2, 0:w],
                                  start=True, stop=True).then_inc(s_h, 1)
                    if i >= 2:
                        g = i - 2
                        pe.wait_ge(s_hr, (0 if base is None else base) + (g + 1))
                        if g == 0 and base is not None:
                            pe.wait_ge(s_max, blocks)
                        for j in range(GW * g, min(GW * g + GW, n)):
                            q = j - GW * g
                            last = pe.matmul(v_ps[:, j, :], h_sb[:, g % 2, q * P:(q + 1) * P], w2_sb[:, :],
                                             start=True, stop=True)
                        last.then_inc(s_vp, 1)

            block0(0, 16 * CB, None, 0, CB)
            block0(1, 16 * CB, GB, 1, CB)
            with pe.Fori(1, ROUNDS) as r:
                for k in range(2):
                    block0(k, (r + 1) * (16 * CB), r * (2 * GB) + k * GB, r * 2 + k, CB)
            block0(0, ROUNDS * 16 * CB + 16 * TAIL, NB * GB, NB, TAIL)

            def tails(n):
                pe.wait_ge(s_tail, n)
                pe.transpose(t_ps[0][0:ROW, 0:P], (maxc if n == 1 else sumc)[:, :], ident[:, :])
                last = pe.transpose(t_ps[0][0:ROW, P:2 * P], wmask[:, :], ident[:, :])
                if n > 1:
                    last = pe.transpose(t_ps[0][0:ROW, 2 * P:3 * P], mrep[:, :], ident[:, :])
                last.then_inc(s_tailt, 1)
                pe.wait_ge(s_car, n)
                last = pe.transpose(t_ps[1][:, 0:ROW], si_t[:, 0:P], ident[0:ROW, 0:ROW])
                if n > 1:
                    last = pe.transpose(t_ps[1][:, 64:64 + ROW], mi_t[:, 0:P], ident[0:ROW, 0:ROW])
                last.then_inc(s_cart, 1)

            def table(l):
                feats = x1 if l == 0 else work
                pe.wait_ge(s_node, l + 1)
                for i in range(NQ + 1):
                    if i < NQ:
                        if i >= 2:
                            pe.wait_ge(s_ntc, l * NQ + i - 1)
                        pe.transpose(t_ps[i % 2][:, 0:P], feats[:, 4 * i:4 * i + 4, :], ident[:, :]).then_inc(s_nt, 1)
                    if i >= 1:
                        g = i - 1
                        pe.wait_ge(s_ntc, l * NQ + g + 1)
                        if g >= 2:
                            pe.wait_ge(s_npc, l * NQ + g - 1)
                        pe.matmul(h_ps[g % 2][:, 0:4 * KD], xt_sb[:, g % 2, 0:P], wd_sb[:, l, :],
                                  start=True, stop=True).then_inc(s_np, 1)

            tails(1)
            pe.wait_ge(s_wd, 16 * 12)
            for l in range(3):
                table(l)
                tails(l + 2)

        @block.scalar
        def _(act):
            act.wait_ge(s_wz, 1)
            act.wait_ge(s_const, 1)
            act.dma_start(w1_sb[:, :], w1).then_inc(s_w, 16)
            act.dma_start(w2_sb[:, :], w2).then_inc(s_w, 16)
            act.dma_start(b1_sb[:, :], b1.unsqueeze(1), allow_slow_non_contiguous=True).then_inc(s_w, 16)
            act.dma_start(b2_sb[:, :], b2.partition_broadcast(P)).then_inc(s_w, 16)
            act.dma_start(ea_sb[:, :], ea1.partition_broadcast(P)).then_inc(s_w, 16)
            for l, (w, att_s, att_d, b) in enumerate(gat):
                act.dma_start(gw_sb[:, l, :], w).then_inc(s_w, 16)
                act.dma_start(bg_sb[:, l, :], b.partition_broadcast(P)).then_inc(s_w, 16)
                heads = att_s.shape[0]
                for h in range(2):
                    rows = slice(16 * h, 16 * h + 16) if heads == 2 else slice(0, D)
                    head = h if heads == 2 else 0
                    for column, att in ((h * HW + HW - 1, att_s), (ROW + h, att_d)):
                        act.dma_start(pick[rows, l, column:column + 1], att[head, :].unsqueeze(1),
                                          allow_slow_non_contiguous=True).then_inc(s_w, 16)
            act.wait_ge(s_zs, 1)
            act.dma_start(xd_v.rearrange("p (a j) f -> p a (j f)", j=11),
                          zeros[:, 0:11 * D].unsqueeze(1).broadcast_to([P, COLS // 11, 11 * D])).then_inc(s_zero, 16)
            act.dma_start(ad_v.rearrange("p j h -> p (j h)").rearrange("p (a z) -> p a z", z=ZW),
                          zeros.unsqueeze(1).broadcast_to([P, 11, ZW])).then_inc(s_zero, 16)

            def block0(base, n):
                groups = -(-n // GW)
                for i in range(groups + 1):
                    if i < groups:
                        w = P * (min(GW * i + GW, n) - GW * i)
                        act.wait_ge(s_t, (0 if base is None else base) + (i + 1))
                        if base is not None:
                            act.wait_ge(s_h, base + (i - 1))
                        elif i >= 2:
                            act.wait_ge(s_h, i - 1)
                        act.activation(xt_sb[0:3 * D, i % 2, 0:w], t_ps[i % 2][0:3 * D, 0:w], ACT.Copy).then_inc(s_tc, 1)
                    if i >= 1:
                        g = i - 1
                        w = P * (min(GW * g + GW, n) - GW * g)
                        act.wait_ge(s_h, (0 if base is None else base) + (g + 1))
                        if base is not None:
                            act.wait_ge(s_vp, base + (g - 1))
                        elif g >= 2:
                            act.wait_ge(s_vp, g - 1)
                        act.activation(h_sb[:, g % 2, 0:w], h_ps[g % 2][0:HID, 0:w], ACT.Relu,
                                       bias=b1_sb[:, 0:1]).then_inc(s_hr, 1)

            act.wait_ge(s_w, 16 * LOADS)
            act.activation(sc_out[:, :], ea_sb[:, :], ACT.Tanh).then_inc(s_te, 1)
            block0(None, CB)
            block0(GB, CB)
            with act.Fori(1, ROUNDS) as r:
                for k in range(2):
                    block0(r * (2 * GB) + k * GB, CB)
            block0(NB * GB, TAIL)

            asked = [0]

            def serve(out_ap, in_ap, what):
                asked[0] += 1
                act.wait_ge(s_ain, asked[0])
                act.activation(out_ap, in_ap, what).then_inc(s_aout, 1)

            def norm_parts():
                serve(work[:, 0:NCOL, :], work2[:, 0:NCOL, :], ACT.Square)
                serve(nt[:, 2, :], nt[:, 1, :], ACT.Sqrt)

            norm_parts()
            for l in range(3):
                for i in range(NQ):
                    act.wait_ge(s_nt, l * NQ + i + 1)
                    if i >= 2:
                        act.wait_ge(s_np, l * NQ + i - 1)
                    act.activation(xt_sb[:, i % 2, 0:P], t_ps[i % 2][:, 0:P], ACT.Copy).then_inc(s_ntc, 1)
                done = l * (NB + 1)

                def exps(blocks, n):
                    act.wait_ge(s_exin, blocks)
                    act.activation(ex[:, :, :, 0:n], ex_in[:, :, :, 0:n], ACT.Exp).then_inc(s_ex, 1)

                with act.Fori(0, ROUNDS) as r:
                    for k in range(2):
                        exps(r * 2 + (done + k + 1), CB)
                exps(done + NB + 1, TAIL)
                act.wait_ge(s_tein, l + 1)
                act.activation(te[:, :, :], te_in[:, :, :], ACT.Exp).then_inc(s_te, 1)
                act.wait_ge(s_fein, l + 1)
                act.activation(fe[:, :, :], fe_in[:, :, :], ACT.Exp).then_inc(s_fe, 1)
                if l < 2:
                    serve(work2[:, 0:NCOL, :], work2[:, 0:NCOL, :], ACT.Exp)
                else:
                    norm_parts()

        @block.vector
        def _(dve):
            count = [0]

            def mark(ins):
                count[0] += 1
                ins.then_inc(s_v, 1)

            def link(ins):
                mark(ins)
                dve.wait_ge(s_v, count[0])

            tt, ts, stt = dve.tensor_tensor, dve.tensor_scalar, dve.scalar_tensor_tensor

            hi_i = hi_f.bitcast(I32)
            link(dve.memset(hi_i[96:P, REAL:COLS], N))
            link(dve.memset(src_i[96:P, REAL:COLS], 0))
            link(dve.memset(xn[96:P, NREAL:NCOL, :], 0.0))
            dve.memset(prev_i[:, :], -1).then_inc(s_pads, 1)
            dve.memset(zeros, 0.0).then_inc(s_zs, 1)
            mark(dve.memset(onesn[:, :], 1.0))
            mark(dve.memset(x1[:, NCOL:4 * NQ, :], 0.0))
            mark(dve.memset(same[:, 0:1], 0.0))
            mark(dve.memset(fillc[:, :], 0.0))
            mark(dve.memset(maxc[:, :], 0.0))
            mark(dve.memset(si_t[:, 0:1], 0.0))
            mark(dve.memset(mi_t[:, 0:1], 0.0))

            dve.wait_ge(s_dst, 48)
            mark(dve.tensor_copy(dst0_i[:, :], hi_i[:, 0:1]))
            link(dve.tensor_copy(dst_f[:, :], hi_i))
            link(ts(hi_f, dst_f[:, :], 0.5, 1.0 / NCOL, ALU.add, ALU.mult))
            link(ts(hi_f, hi_f, -0.5, None, ALU.add))
            link(ts(hi_f, hi_f, ROUND, None, ALU.add))
            link(ts(hi_f, hi_f, -ROUND, None, ALU.add))
            link(stt(lo_f, hi_f, -float(NCOL), dst_f[:, :], ALU.mult, ALU.add))
            dve.wait_ge(s_const, 1)
            link(dve.tensor_copy(iota_b[:, :], iota_i[:, :]))

            ohc = [0]

            def onehots(m, k, j0, n, wait):
                if wait is not None:
                    dve.wait_ge(s_cnt, wait)
                dve.tensor_copy(digits[:, 0, 0:n], hi_f[:, bass.ds(j0, n)])
                dve.tensor_copy(digits[:, 1, 0:n], lo_f[:, bass.ds(j0, n)]).then_inc(s_ohd, 1)
                dve.wait_ge(s_ohd, m)
                for j in range(n):
                    ts(oh_hi[k][:, j, :], iota_b[:, :], digits[:, 0, j:j + 1], None, ALU.is_equal)
                    last = ts(oh_lo[k][:, j, :], iota_b[:, 0:NCOL], digits[:, 1, j:j + 1], None, ALU.is_equal)
                last.then_inc(s_oh, 1)
                dve.wait_ge(s_oh, m)

            onehots(1, 0, 0, OH, None)
            onehots(2, 1, OH, OH, None)
            with dve.Fori(1, OHN // 2) as r:
                for k in range(2):
                    onehots(r * 2 + (k + 1), k, r * (2 * OH) + k * OH, OH, r * 2 + (k - 1))
            for m in range(OHN - OHN % 2, OHN + 1):
                onehots(m + 1, m % 2, m * OH, OH if m < OHN else OHT, m - 1)

            dve.wait_ge(s_cnt, OHN + 1)
            link(dve.tensor_copy(deg[:, :], count_ps))
            link(dve.tensor_tensor_scan(cum[:, :], onesn[:, :], deg[:, :], 0.0, ALU.mult, ALU.add))
            dve.tensor_copy(tot[:, :], cum[:, NCOL - 1:NCOL]).then_inc(s_tot, 1)
            mark(ts(has[:, :], deg[:, :], 0.5, None, ALU.is_gt))
            link(dve.tensor_copy(spare[:, :], spare_i[:, :]))
            link(ts(pen[:, :], has[:, :], -1.0, -LOW, ALU.add, ALU.mult))
            dve.wait_ge(s_bef, 1)
            link(dve.tensor_copy(before[:, :], before_ps))
            link(ts(cum[:, :], cum[:, :], before[:, 0:1], None, ALU.add))
            link(tt(nt[:, 0, :], cum[:, :], deg[:, :], ALU.subtract))
            link(tt(nt[:, 0, :], nt[:, 0, :], spare[:, :], ALU.subtract))
            link(tt(nt[:, 0, :], nt[:, 0, :], has[:, :], ALU.mult))
            link(tt(nt[:, 0, :], nt[:, 0, :], spare[:, :], ALU.add))
            mark(dve.tensor_copy(start_i[:, :], nt[:, 0, :]))
            link(ts(nt[:, 1, :], cum[:, :], -1.0, 0.0, ALU.add, ALU.max))
            link(dve.tensor_copy(end_i[:, :], nt[:, 1, :]))

            link(tt(same[:, 1:COLS], dst_f[:, 1:COLS], dst_f[:, 0:COLS - 1], ALU.is_equal))
            link(ts(reset[:, :], same[:, :], -1.0, -LOW, ALU.add, ALU.mult))
            dve.wait_ge(s_prev, 16)
            link(dve.tensor_copy(prev_f[:, :], prev_i[:, :]))
            link(tt(cont[:, :], prev_f[:, :], dst_f[:, 0:1], ALU.is_equal))
            link(ts(cmask[:, :], cont[:, :], -1.0, -LOW, ALU.add, ALU.mult))
            link(tt(pt[:, 0:1], dst_f[:, 0:1], dst_f[:, COLS - 1:COLS], ALU.is_equal))
            link(tt(pt[:, 0:1], pt[:, 0:1], cont[:, :], ALU.mult))
            link(ts(pt[:, 0:1], pt[:, 0:1], -1.0, -LOW, ALU.add, ALU.mult))
            link(dve.tensor_copy(wmask[:, :], pt[:, 0:1].broadcast_to([P, ROW])))
            link(ts(hi_f, dst_f[:, :], dst_f[:, 0:1], None, ALU.is_equal))
            link(dve.reduce_sum(pt[:, 1:2], hi_f, X))
            link(dve.tensor_copy(pt[:, 2:3], row0_i[:, :]))
            link(tt(pt[:, 1:2], pt[:, 1:2], pt[:, 2:3], ALU.add))
            link(ts(pt[:, 1:2], pt[:, 1:2], -1.0, None, ALU.add))
            dve.tensor_copy(fe_i[:, :], pt[:, 1:2]).then_inc(s_idx, 1)
            dve.wait_ge(s_wc, 1)
            dve.tensor_copy(wc_sb[:, :, :], wc_ps).then_inc(s_wcs, 1)
            dve.wait_ge(s_te, 1)
            link(ts(sc[:, 0:1], sc_out[:, :], 0.1, None, ALU.is_lt))
            link(ts(sc[:, 1:2], sc[:, 0:1], -1.0, 1.0, ALU.mult, ALU.add))
            link(tt(sc[:, 2:3], sc_out[:, :], sc[:, 1:2], ALU.mult))
            link(tt(sc[:, 2:3], sc[:, 2:3], sc[:, 0:1], ALU.add))

            def block0(k, j0, n, use, attrs, groups, blocks):
                dve.wait_ge(s_xd[k], use)
                dve.tensor_copy(same_b[:, 0:n], same[:, bass.ds(j0, n)])
                dve.tensor_copy(reset_b[:, 0:n], reset[:, bass.ds(j0, n)]).then_inc(s_b0, 1)
                dve.wait_ge(s_b0, blocks * 3 + 1)
                for f in range(D):
                    dve.tensor_tensor_scan(slot0[k][:, 0:n, D + f], same_b[:, 0:n], spread[k][:, 0:n, f],
                                           fillc[:, f:f + 1], ALU.mult, ALU.add)
                dve.wait_ge(s_ed[k], attrs)
                dve.tensor_copy(slot0[k][:, 0:n, 2 * D:3 * D], attr[k][:, 0:n, :]).then_inc(s_fill, 1)
                dve.wait_ge(s_fill, blocks + 1)
                dve.tensor_copy(fillc[:, :], slot0[k][:, n - 1, D:2 * D]).then_inc(s_b0, 1)
                dve.wait_ge(s_vp, groups)
                for f in range(D):
                    last = dve.tensor_tensor_scan(spread[k][:, 0:n, f], reset_b[:, 0:n], v_ps[:, 0:n, f],
                                                  maxc[:, f:f + 1], ALU.add, ALU.max)
                last.then_inc(s_b0, 1)
                dve.wait_ge(s_b0, blocks * 3 + 3)
                dve.tensor_copy(maxc[:, 0:D], spread[k][:, n - 1, :]).then_inc(s_max, 1)
                dve.wait_ge(s_max, blocks + 1)

            with dve.Fori(0, ROUNDS - 1) as r:
                for k in range(2):
                    block0(k, r * (2 * CB) + k * CB, CB, (r + 1) * 16, (r + 1) * 16,
                           r * (2 * GB) + (k + 1) * GB, r * 2 + k)
            block0(0, (NB - 2) * CB, CB, ROUNDS * 16, ROUNDS * 16, (NB - 1) * GB, NB - 2)
            block0(1, (NB - 1) * CB, CB, ROUNDS * 16, (ROUNDS - 1) * 16 + 48, NB * GB, NB - 1)
            block0(0, NB * CB, TAIL, (ROUNDS + 1) * 16, ROUNDS * 16 + 32, NB * GB + GT, NB)

            dve.engine_nop().then_inc(s_tail, 1)
            dve.wait_ge(s_tailt, 1)
            link(dve.tensor_copy(wm_t[:, :], t_ps[0][0:ROW, P:2 * P]))
            link(dve.tensor_tensor_scan(si_t[:, 1:P + 1], wm_t[:, :], t_ps[0][0:ROW, 0:P], 0.0, ALU.add, ALU.max))
            dve.engine_nop().then_inc(s_car, 1)
            dve.wait_ge(s_cart, 1)
            link(ts(cs[:, :], t_ps[1][:, 0:ROW], cmask[:, 0:1], None, ALU.add))
            dve.wait_ge(s_fixg, 16)
            tt(fo[:, 0:D], fix[:, 0:D], cs[:, 0:D], ALU.max).then_inc(s_fixv, 1)

            def per_node(v, f=D):
                return v.unsqueeze(2).broadcast_to([P, NCOL, f])

            def per_feature(v):
                return v.unsqueeze(1).broadcast_to([P, NCOL, D])

            asked = [0]

            def ask(ins):
                asked[0] += 1
                ins.then_inc(s_ain, 1)
                dve.wait_ge(s_aout, asked[0])

            def norm(y, result):
                link(dve.reduce_sum(nt[:, 0, :], y, X))
                link(ts(nt[:, 0, :], nt[:, 0, :], 1.0 / D, None, ALU.mult))
                ask(tt(work2[:, 0:NCOL, :], y, per_node(nt[:, 0, :]), ALU.subtract))
                link(dve.reduce_sum(nt[:, 1, :], work[:, 0:NCOL, :], X))
                ask(ts(nt[:, 1, :], nt[:, 1, :], 1.0 / D, 1e-5, ALU.mult, ALU.add))
                link(dve.reciprocal(nt[:, 3, :], nt[:, 2, :]))
                return tt(result, work2[:, 0:NCOL, :], per_node(nt[:, 3, :]), ALU.mult)

            wk = work[:, 0:NCOL, :]
            dve.wait_ge(s_nd, 16 * NCOL)
            link(tt(wk, nd[:, :, 0:D], per_feature(b2_sb[:, :]), ALU.add))
            link(tt(wk, wk, per_node(pen[:, :]), ALU.add))
            link(tt(wk, wk, xn, ALU.max))
            link(tt(wk, wk, xn, ALU.add))
            norm(wk, x1[:, 0:NCOL, :]).then_inc(s_node, 1)

            for l in range(3):
                for g in range(NQ):
                    dve.wait_ge(s_np, l * NQ + g + 1)
                    prod = h_ps[g % 2][:, 0:4 * KD].rearrange("p (c k) -> p c k", k=KD)
                    dve.tensor_copy(tab[:, 4 * g:4 * g + 4, :], prod[:, :, 0:ROW])
                    dve.tensor_copy(adt[:, 4 * g:4 * g + 4, :], prod[:, :, ROW:KD]).then_inc(s_npc, 1)
                dve.wait_ge(s_npc, (l + 1) * NQ)
                dve.memset(tab[:, :, 16:ROW:HW], 1.0).then_inc(s_tab, 1)
                mark(dve.memset(mx[:, :, 0:1], 0.0))
                link(dve.memset(sumc[:, :], 0.0))

                dve.wait_ge(s_adf, 16 * (l + 1))
                for h in range(2):
                    mark(dve.tensor_tensor_scan(adf[:, :, h], same[:, :], adf[:, :, h], 0.0, ALU.mult, ALU.add))
                dve.wait_ge(s_v, count[0])
                done = l * (NB + 1)
                STEPS = 7

                def blockg(k, j0, n, use, blocks):
                    own = [0]

                    def chain(ins):
                        own[0] += 1
                        ins.then_inc(s_own, 1)
                        dve.wait_ge(s_own, blocks * STEPS + own[0])

                    rows = slotg[k][:, 0:n, :]
                    logit = rows[:, :, HW - 1:ROW:HW].rearrange("p j h -> p h j")
                    dve.wait_ge(s_g[l][k], use)
                    chain(tt(lg[:, :, 0:n], logit, adf[:, bass.ds(j0, n), :].rearrange("p j h -> p h j"), ALU.add))
                    chain(stt(lg[:, :, 0:n], lg[:, :, 0:n], SLOPES[l], lg[:, :, 0:n], ALU.mult, ALU.max))
                    dve.tensor_copy(reset_b[:, 0:n], reset[:, bass.ds(j0, n)]).then_inc(s_own, 1)
                    own[0] += 1
                    dve.wait_ge(s_own, blocks * STEPS + own[0])
                    for h in range(2):
                        last = dve.tensor_tensor_scan(mx[:, h, 1:n + 1], reset_b[:, 0:n], lg[:, h, 0:n],
                                                      mx[:, h, 0:1], ALU.add, ALU.max)
                    chain(last)
                    tt(ex_in[:, 1, :, 0:n], lg[:, :, 0:n], mx[:, :, 1:n + 1], ALU.subtract)
                    dve.tensor_copy(rows[:, :, HW - 1:ROW:HW].rearrange("p j h -> p h j"), mx[:, :, 1:n + 1])
                    chain(tt(ex_in[:, 0, :, 0:n], mx[:, :, 0:n],
                             reset_b[:, 0:n].unsqueeze(1).broadcast_to([P, 2, n]), ALU.add))
                    tt(ex_in[:, 0, :, 0:n], ex_in[:, 0, :, 0:n], mx[:, :, 1:n + 1], ALU.subtract).then_inc(s_exin, 1)
                    dve.wait_ge(s_ex, blocks + 1)
                    parts = rows.rearrange("p j (h k) -> p j h k", h=2)[:, :, :, 0:HW - 1]
                    weights = ex[:, 1, :, 0:n].rearrange("p h j -> p j h").unsqueeze(3).broadcast_to([P, n, 2, HW - 1])
                    chain(tt(parts, parts, weights, ALU.mult))
                    for h in range(2):
                        for c in range(h * HW, h * HW + HW - 1):
                            last = dve.tensor_tensor_scan(rows[:, :, c], ex[:, 0, h, 0:n], rows[:, :, c],
                                                          sumc[:, c:c + 1], ALU.mult, ALU.add)
                    chain(last)
                    assert own[0] == STEPS
                    dve.tensor_copy(mx[:, :, 0:1], mx[:, :, n:n + 1])
                    dve.tensor_copy(sumc[:, :], rows[:, n - 1, :]).then_inc(s_sum, 1)
                    dve.wait_ge(s_sum, blocks + 1)

                with dve.Fori(0, ROUNDS) as r:
                    for k in range(2):
                        blockg(k, r * (2 * CB) + k * CB, CB, (r + 1) * (16 * CB), r * 2 + (done + k))
                blockg(0, NB * CB, TAIL, ROUNDS * 16 * CB + 16 * TAIL, done + NB)

                dve.tensor_copy(mrep[:, :].rearrange("p (h k) -> p h k", h=2),
                                sumc[:, HW - 1:ROW:HW].unsqueeze(2).broadcast_to([P, 2, HW])).then_inc(s_tail, 1)
                dve.wait_ge(s_tailt, l + 2)
                mark(dve.tensor_copy(wm_t[:, :], t_ps[0][0:ROW, P:2 * P]))
                link(dve.tensor_copy(m_t[:, :], t_ps[0][0:ROW, 2 * P:3 * P]))
                link(dve.tensor_tensor_scan(mi_t[:, 1:P + 1], wm_t[:, :], m_t[:, :], 0.0, ALU.add, ALU.max))
                mark(tt(te_in[:, 0, :], mi_t[:, 0:P], wm_t[:, :], ALU.add))
                link(tt(te_in[:, 1, :], m_t[:, :], mi_t[:, 1:P + 1], ALU.subtract))
                tt(te_in[:, 0, :], te_in[:, 0, :], mi_t[:, 1:P + 1], ALU.subtract).then_inc(s_tein, 1)
                dve.wait_ge(s_te, l + 2)
                link(tt(m_t[:, :], te[:, 1, :], t_ps[0][0:ROW, 0:P], ALU.mult))
                dve.tensor_tensor_scan(si_t[:, 1:P + 1], te[:, 0, :], m_t[:, :], 0.0, ALU.mult, ALU.add).then_inc(s_car, 1)
                dve.wait_ge(s_cart, l + 2)
                dve.wait_ge(s_fixg, 16 * (l + 2))
                mark(dve.tensor_copy(cs[:, :], t_ps[1][:, 0:ROW]))
                link(ts(cm[:, :], t_ps[1][:, 64 + HW - 1:64 + ROW:HW], cmask[:, 0:1], None, ALU.add))
                link(tt(vm[:, :], cm[:, :], fix[:, HW - 1:ROW:HW], ALU.max))
                mark(tt(fe_in[:, 0, :], fix[:, HW - 1:ROW:HW], vm[:, :], ALU.subtract))
                tt(fe_in[:, 1, :], cm[:, :], vm[:, :], ALU.subtract).then_inc(s_fein, 1)
                dve.wait_ge(s_fe, l + 1)
                both = [t[:, :].rearrange("p (h k) -> p h k", h=2) for t in (fix, cs, fo)]
                mark(tt(both[0], both[0], fe[:, 0, :].unsqueeze(2).broadcast_to([P, 2, HW]), ALU.mult))
                link(tt(both[1], both[1], fe[:, 1, :].unsqueeze(2).broadcast_to([P, 2, HW]), ALU.mult))
                tt(both[2], both[0], both[1], ALU.add).then_inc(s_fixv, 1)

                dve.wait_ge(s_nd, 16 * NCOL * (l + 2))
                link(ts(rden[:, :, :], nd[:, :, 16:ROW:HW], 1e-16, None, ALU.add))
                link(dve.reciprocal(rden[:, :, :], rden[:, :, :]))
                link(tt(rden[:, :, :], rden[:, :, :], per_node(has[:, :], 2), ALU.mult))
                link(tt(wk.rearrange("p c (h k) -> p c h k", h=2),
                        nd[:, :, :].rearrange("p c (h k) -> p c h k", h=2)[:, :, :, 0:16],
                        rden[:, :, :].unsqueeze(3).broadcast_to([P, NCOL, 2, 16]), ALU.mult))
                link(tt(wk, wk, per_feature(bg_sb[:, l, :]), ALU.add))
                if l == 0:
                    link(ts(wk, wk, sc[:, 2:3], None, ALU.mult))
                    link(stt(wk, wk, 0.05, wk, ALU.mult, ALU.add))
                if l < 2:
                    ask(ts(work2[:, 0:NCOL, :], wk, 0.0, None, ALU.min))
                    link(ts(wk, wk, 0.0, None, ALU.max))
                    link(stt(wk, work2[:, 0:NCOL, :], -1.0, wk, ALU.add, ALU.add))
                    mark(dve.memset(work[:, NCOL:4 * NQ, :], 0.0))
                    ts(wk, wk, -3.0, 3.0, ALU.max, ALU.min).then_inc(s_node, 1)
                else:
                    link(tt(wk, wk, x1[:, 0:NCOL, :], ALU.add))
                    norm(wk, work2[:, 0:NCOL, :]).then_inc(s_fin, 1)


_INS = ['x', 'src', 'dst', 'edge_attr_32', 'L0_gnn_W1', 'L0_gnn_b1', 'L0_gnn_W2', 'L0_gnn_b2', 'L1_gnn_W1',
        'L1_gnn_att_s1', 'L1_gnn_att_d1', 'L1_gnn_b1', 'L1_gnn_ea1', 'L1_gnn_W2', 'L1_gnn_att_s2',
        'L1_gnn_att_d2', 'L1_gnn_b2', 'L1_gnn_W3', 'L1_gnn_att_s3', 'L1_gnn_att_d3', 'L1_gnn_b3']


def kernel(**inputs):
    import numpy as _np
    import concourse.bacc as _bacc
    from concourse import mybir as _mybir
    from concourse.bass_utils import run_bass_kernel_spmd as _run

    nc = _bacc.Bacc("TRN2", target_bir_lowering=False, num_devices=1)
    arrays, a = {}, {}
    for name in _INS:
        v = _np.ascontiguousarray(inputs[name])
        arrays[f"in_{name}"] = v
        a[name] = nc.dram_tensor(f"in_{name}", v.shape, _mybir.dt.from_np(v.dtype), kind="ExternalInput").ap()
    out = nc.dram_tensor("out_0", a['x'].shape, _mybir.dt.float32, kind="ExternalOutput").ap()
    gat = [tuple(a[f'L1_gnn_{n}{i}'] for n in ('W', 'att_s', 'att_d', 'b')) for i in (1, 2, 3)]
    gnn_program(nc, a['x'], a['src'], a['dst'], a['edge_attr_32'], a['L0_gnn_W1'], a['L0_gnn_b1'],
                a['L0_gnn_W2'], a['L0_gnn_b2'], gat, a['L1_gnn_ea1'], out)
    r = _run(nc, [arrays], core_ids=[0])
    return r.results[0]["out_0"]
```

```python
import concourse.bass as bass
from concourse import mybir
from contextlib import ExitStack

F32 = mybir.dt.float32
BF16 = mybir.dt.bfloat16
F16 = mybir.dt.float16
I32 = mybir.dt.int32
ALU = mybir.AluOpType
ACT = mybir.ActivationFunctionType
X = mybir.AxisListType.X

P = 128
LOW = -3.0e38
ROUND = 12582912.0


def gnn_program(nc, x, src, dst, edge, w1, b1, w2, b2, gat, ea1, out):
    N, D = x.shape
    E = src.shape[0]
    HID = w1.shape[1]
    COLS = -(-E // P)
    EP = P * COLS
    REAL = E - (P - 1) * COLS
    NCOL = -(-N // P)
    NP = P * NCOL
    NREAL = N - (P - 1) * NCOL
    CB = 64
    NB = COLS // CB
    TAIL = COLS - NB * CB
    ROUNDS = NB // 2
    assert NB == 2 * ROUNDS and 0 < TAIL and REAL > (NB - 1) * CB and REAL < NB * CB
    assert 0 < NREAL < NCOL and EP + NP < 1 << 24
    GW = 4
    GB = CB // GW
    GT = -(-TAIL // GW)
    HW = 18
    ROW = 2 * HW
    KD = ROW + 2
    KG = 10
    PG = CB - KG
    C1 = 14
    C2 = NCOL // C1
    assert NCOL == C1 * C2 and C1 * ROW <= 512 and C2 * P <= 1024 and 2 * KG % 4 == 0
    OH = 16
    OHN = COLS // OH
    OHT = COLS - OHN * OH
    NQ = -(-NCOL // 4)
    QUARTERS = [(0, 28), (28, 56), (56, 84), (84, NCOL)]
    EARLY = 16
    ZW = 586
    assert EARLY % 2 == 0 and all(c0 % 4 == 0 for c0, _ in QUARTERS)
    assert COLS % 11 == 0 and 2 * COLS == 11 * ZW
    LOADS = 7 + 3 * 6
    SLOPES = [0.01, 0.2, 0.2]

    xd_d = nc.dram_tensor("xd_d", (EP + NP, D), F32, kind="Internal").ap()
    xs_d = nc.dram_tensor("xs_d", (EP, D), F32, kind="Internal").ap()
    ad_d = nc.dram_tensor("ad_d", (EP + NP, 2), F32, kind="Internal").ap()
    scan0_d = nc.dram_tensor("scan0_d", (EP, D), F32, kind="Internal").ap()
    scan_d = nc.dram_tensor("scan_d", (EP, ROW), F32, kind="Internal").ap()
    table_d = nc.dram_tensor("table_d", (NP, ROW), F32, kind="Internal").ap()
    adn_d = nc.dram_tensor("adn_d", (NP, 2), F32, kind="Internal").ap()
    xd_v = xd_d[0:EP, :].rearrange("(p j) f -> p j f", p=P)
    ad_v = ad_d[0:EP, :].rearrange("(p j) h -> p j h", p=P)
    recs_d = [nc.dram_tensor(f"recs{i}_d", (EP, 3), F32, kind="Internal").ap() for i in range(3)]
    edge_s = nc.dram_tensor("edge_s", (EP, D), F32, kind="Internal").ap()
    xs_v = xs_d.rearrange("(p j) f -> p j f", p=P)
    scan0_v = scan0_d.rearrange("(p j) f -> p j f", p=P)
    scan_v = scan_d.rearrange("(p j) f -> p j f", p=P)

    ctx = ExitStack()
    with ctx:
        def sb(name, shape, dt=F32):
            return ctx.enter_context(nc.sbuf_tensor(name, shape, dt))

        def sem(name):
            return ctx.enter_context(nc.semaphore(name))

        src_i = sb("src_i", [P, COLS], I32)
        dst_f = sb("dst_f", [P, COLS])
        onehot_e = [dst_f[:, i * C2 * P // 2:(i + 1) * C2 * P // 2].bitcast(BF16) for i in range(4)]
        onehot_t = [dst_f[:, (4 + i) * C2 * P // 2:(5 + i) * C2 * P // 2].bitcast(BF16) for i in range(2)]
        keys = sb("keys", [P, NB, KG])
        c1s = sb("c1s", [P, NB, KG])
        key_b = sb("key_b", [P, KG])
        onehot_c1 = sb("onehot_c1", [P, KG, C1])
        iota_key = sb("iota_key", [P, C2 * P], F16)
        iota_c1 = sb("iota_c1", [P, C1])
        ident_b = sb("ident_b", [P, P], BF16)
        index = sb("index", [P, 2, CB], I32)
        same = sb("same", [P, COLS])
        reset = sb("reset", [P, COLS])
        adf = sb("adf", [P, COLS, 2])
        hi_f = adf[:, :, :].rearrange("p j h -> p (j h)")[:, 0:COLS]
        lo_f = adf[:, :, :].rearrange("p j h -> p (j h)")[:, COLS:2 * COLS]
        ring0 = sb("ring0", [P, 2 * 3 * CB * D])
        slot0 = [ring0[:, k * 3 * CB * D:(k + 1) * 3 * CB * D].rearrange("p (j f) -> p j f", f=3 * D)
                 for k in range(2)]
        work = ring0[:, 0:4 * NQ * D].rearrange("p (c f) -> p c f", f=D)
        work2 = ring0[:, 4 * NQ * D:8 * NQ * D].rearrange("p (c f) -> p c f", f=D)
        tab = ring0[:, 8 * NQ * D:8 * NQ * D + 4 * NQ * ROW].rearrange("p (c f) -> p c f", f=ROW)
        part_mem = ring0[:, 0:8 * NQ * D].bitcast(BF16)
        parts = [part_mem[:, i * NCOL * ROW:(i + 1) * NCOL * ROW] for i in range(3)]
        ringg = sb("ringg", [P, 2 * CB * ROW])
        slotg = [ringg[:, k * CB * ROW:(k + 1) * CB * ROW].rearrange("p (j f) -> p j f", f=ROW)
                 for k in range(2)]
        spread = [ringg[:, k * CB * D:(k + 1) * CB * D].rearrange("p (j f) -> p j f", f=D) for k in range(2)]
        adf_flat = adf[:, :, :].rearrange("p j h -> p (j h)")
        attr = [adf_flat[:, k * CB * D:(k + 1) * CB * D].rearrange("p (j f) -> p j f", f=D) for k in range(2)]
        zeros = ringg[:, 0:ZW]
        OHB = OH * (P + NCOL)
        onehot = [ringg[:, ZW + k * OHB // 2:ZW + (k + 1) * OHB // 2].bitcast(BF16) for k in range(2)]
        oh_hi = [o[:, 0:OH * P].rearrange("p (j n) -> p j n", n=P) for o in onehot]
        oh_lo = [o[:, OH * P:OHB].rearrange("p (j n) -> p j n", n=NCOL) for o in onehot]
        recs = ring0[:, 0:3 * COLS].rearrange("p (j r) -> p j r", r=3)
        sort_mem = ringg[:, ZW:ZW + 4 * P + 3 * P + D + 8]
        base, cnt = (sort_mem[:, i * 2 * P:(i + 1) * 2 * P].rearrange("p (m d) -> p m d", m=2) for i in range(2))
        oh_s, upper_b, ones_b = (sort_mem[:, (8 + i) * P // 2:(9 + i) * P // 2].bitcast(BF16) for i in range(3))
        places = sort_mem[:, 11 * P // 2:13 * P // 2]
        erow = sort_mem[:, 7 * P:7 * P + D]
        key = sort_mem[:, 7 * P + D:7 * P + D + 8]
        ones_f = sb("ones_f", [P, P])
        rec = sb("rec", [P, 3])
        pos_i = sb("pos_i", [P, 1], I32)
        flag_i = sb("flag_i", [1, 1], I32)
        digits = sb("digits", [P, 2, 2 * OH])
        xt_sb = sb("xt_sb", [P, 2, 512])
        h_sb = sb("h_sb", [2 * HID, 2, 256])
        iota_ki = xt_sb[:, :, :].rearrange("p a n -> p (a n)").bitcast(I32)[:, 0:C2 * P]
        same_b = sb("same_b", [P, CB])
        reset_b = sb("reset_b", [P, CB])
        fillc = sb("fillc", [P, D])
        maxc = sb("maxc", [P, ROW])
        lg = sb("lg", [P, 2, CB])
        mx = sb("mx", [P, 2, CB + 1])
        ex_in = sb("ex_in", [P, 2, 2, CB])
        ex = sb("ex", [P, 2, 2, CB])
        sumc = sb("sumc", [P, ROW])
        x1 = sb("x1", [P, 4 * NQ, D])
        xn = x1[:, 0:NCOL, :]
        nd_all = sb("nd_all", [P, 2 * CB * D])
        nd = nd_all[:, 0:NCOL * ROW].rearrange("p (c f) -> p c f", f=ROW)
        rest = nd_all[:, 0:NCOL * ROW]
        picked = [nd_all[:, i * C1 * ROW:(i + 1) * C1 * ROW].rearrange("p (c f) -> p c f", f=ROW) for i in range(2)]
        stage = [nd_all[:, k * CB * D:(k + 1) * CB * D].rearrange("p (j f) -> p j f", f=D) for k in range(2)]
        adt = sb("adt", [P, 4 * NQ, 2])
        deg = sb("deg", [P, NCOL])
        cum = sb("cum", [P, NCOL])
        has = sb("has", [P, NCOL])
        pen = sb("pen", [P, NCOL])
        nt = sb("nt", [P, 4, NCOL])
        rden = sb("rden", [P, NCOL, 2])
        spare_i = sb("spare_i", [P, NCOL], I32)
        spare = sb("spare", [P, NCOL])
        start_i = sb("start_i", [P, NCOL], I32)
        end_i = sb("end_i", [P, NCOL], I32)
        onesn = sb("onesn", [P, NCOL])
        before = sb("before", [P, 1])
        dst0_i = sb("dst0_i", [P, 1], I32)
        prev_i = sb("prev_i", [P, 1], I32)
        prev_f = sb("prev_f", [P, 1])
        cont = sb("cont", [P, 1])
        cmask = sb("cmask", [P, 1])
        wmask = sb("wmask", [P, ROW])
        pt = sb("pt", [P, 4])
        row0_i = sb("row0_i", [P, 1], I32)
        fe_i = sb("fe_i", [P, 1], I32)
        x0 = sb("x0", [P, D])
        a0 = sb("a0", [P, 2])
        tot = sb("tot", [P, 1])
        viol = sb("viol", [P, 1])
        mrep = sb("mrep", [P, ROW])
        wm_t = sb("wm_t", [ROW, P])
        m_t = sb("m_t", [ROW, P])
        mi_t = sb("mi_t", [ROW, P + 1])
        si_t = sb("si_t", [ROW, P + 1])
        te_in = sb("te_in", [ROW, 2, P])
        te = sb("te", [ROW, 2, P])
        fix = sb("fix", [P, ROW])
        fo = sb("fo", [P, ROW])
        cs = sb("cs", [P, ROW])
        cm = sb("cm", [P, 2])
        vm = sb("vm", [P, 2])
        fe_in = sb("fe_in", [P, 2, 2])
        fe = sb("fe", [P, 2, 2])
        ident = sb("ident", [P, P])
        upper = sb("upper", [P, P])
        iota_i = sb("iota_i", [P, P], I32)
        iota_b = sb("iota_b", [P, P], BF16)
        w1_sb = sb("w1_sb", [3 * D, HID])
        w2_sb = sb("w2_sb", [2 * HID, 2 * D])
        b1_sb = sb("b1_sb", [2 * HID, 1])
        b2_sb = sb("b2_sb", [P, D])
        bg_sb = sb("bg_sb", [P, 3, D])
        gw_sb = sb("gw_sb", [D, 3, D])
        pick = sb("pick", [D, 3, KD])
        wc_sb = sb("wc_sb", [D, 3, KD])
        wd_sb = sb("wd_sb", [P, 3, 4 * KD])
        ea_sb = sb("ea_sb", [P, 1])
        sc = sb("sc", [P, 4])
        sc_out = sb("sc_out", [P, 1])

        psum = ctx.enter_context(nc.psum_tensor("psum", [P, 8 * 512], F32))
        t_ps = [psum[:, k * 512:(k + 1) * 512] for k in range(2)]
        h_ps = [psum[:, (2 + k) * 512:(3 + k) * 512] for k in range(2)]
        v_ps = psum[:, 4 * 512:8 * 512].rearrange("p (j f) -> p j f", f=D)
        count_ps = psum[:, 4 * 512:4 * 512 + NCOL]
        before_ps = psum[:, 5 * 512:5 * 512 + 1]
        sel_ps = [psum[:, (2 + i) * 512:(2 + i) * 512 + C1 * ROW] for i in range(4)]
        oht_ps = [psum[:, (6 + i) * 512:(7 + i) * 512].bitcast(BF16)[:, 0:C2 * P] for i in range(2)]
        flag_ps = psum[0:1, 5 * 512 + 8:5 * 512 + 9]
        total_ps = psum[:, 0:2 * P]
        rank_ps = psum[:, 512:512 + P]
        add_ps = psum[:, 1024:1024 + P]
        wc_ps = psum[0:D, 6 * 512:6 * 512 + 3 * KD].rearrange("p (l k) -> p l k", l=3)

        s_src = sem("s_src")
        s_dst = sem("s_dst")
        s_prev = sem("s_prev")
        s_viol = sem("s_viol")
        s_violp = sem("s_violp")
        s_flag = sem("s_flag")
        s_srt = sem("s_srt")
        s_dig = sem("s_dig")
        s_srp = [sem(f"s_srp{m}") for m in range(2)]
        s_recs = sem("s_recs")
        s_recd = sem("s_recd")
        s_cntd = sem("s_cntd")
        s_totd = sem("s_totd")
        s_rec = [sem(f"s_rec{m}") for m in range(3)]
        s_ohs = sem("s_ohs")
        s_rank = sem("s_rank")
        s_pos = sem("s_pos")
        s_put = [sem(f"s_put{m}") for m in range(2)]
        s_eid = sem("s_eid")
        s_erow = sem("s_erow")
        s_erowd = sem("s_erowd")
        s_back = sem("s_back")
        s_sorted = sem("s_sorted")
        s_sbegun = sem("s_sbegun")
        s_past = sem("s_past")
        s_x = sem("s_x")
        s_w = sem("s_w")
        s_pads = sem("s_pads")
        s_zs = sem("s_zs")
        s_zero = sem("s_zero")
        s_const = sem("s_const")
        s_pool = sem("s_pool")
        s_index = sem("s_index")
        s_begun = sem("s_begun")
        s_wc = sem("s_wc")
        s_wcs = sem("s_wcs")
        s_wd = sem("s_wd")
        s_wz = sem("s_wz")
        s_v = sem("s_v")
        s_oh = sem("s_oh")
        s_ohd = sem("s_ohd")
        s_fs = sem("s_fs")
        s_ms = sem("s_ms")
        s_own = sem("s_own")
        s_cnt = sem("s_cnt")
        s_tot = sem("s_tot")
        s_bef = sem("s_bef")
        s_idx = sem("s_idx")
        s_xs = [sem(f"s_xs{k}") for k in range(2)]
        s_xst = [sem(f"s_xst{k}") for k in range(2)]
        s_xl = [sem(f"s_xl{k}") for k in range(2)]
        s_xd = [sem(f"s_xd{k}") for k in range(2)]
        s_ed = [sem(f"s_ed{k}") for k in range(2)]
        s_st0 = [sem(f"s_st_max{k}") for k in range(2)]
        s_xscat = sem("s_xscat")
        s_x0 = sem("s_x0")
        s_xrow = sem("s_xrow")
        s_fill = sem("s_fill")
        s_t = sem("s_t")
        s_tc = sem("s_tc")
        s_h = sem("s_h")
        s_hr = sem("s_hr")
        s_vp = sem("s_vp")
        s_max = sem("s_max")
        s_g = [[sem(f"s_g{l}_{k}") for k in range(2)] for l in range(3)]
        s_st = [[sem(f"s_st{l}_{k}") for k in range(2)] for l in range(3)]
        s_exin = sem("s_exin")
        s_ex = sem("s_ex")
        s_sum = sem("s_sum")
        s_keys = sem("s_keys")
        s_ohe = sem("s_ohe")
        s_oht = sem("s_oht")
        s_ohc = sem("s_ohc")
        s_sel = sem("s_sel")
        s_pick = sem("s_pick")
        s_row = sem("s_row")
        s_tail = sem("s_tail")
        s_tailt = sem("s_tailt")
        s_tein = sem("s_tein")
        s_te = sem("s_te")
        s_car = sem("s_car")
        s_cart = sem("s_cart")
        s_fein = sem("s_fein")
        s_fe = sem("s_fe")
        s_fixg = sem("s_fixg")
        s_fixv = sem("s_fixv")
        s_fixs = sem("s_fixs")
        s_nd = [sem(f"s_nd{q}") for q in range(len(QUARTERS))]
        s_ain = sem("s_ain")
        s_aout = sem("s_aout")
        s_node = sem("s_node")
        s_nt = sem("s_nt")
        s_ntc = sem("s_ntc")
        s_np = sem("s_np")
        s_npc = sem("s_npc")
        s_tab = sem("s_tab")
        s_tabd = sem("s_tabd")
        s_adnd = sem("s_adnd")
        s_ascat = sem("s_ascat")
        s_a0 = sem("s_a0")
        s_arow = sem("s_arow")
        s_adf = sem("s_adf")
        s_fin = sem("s_fin")
        s_out = sem("s_out")

        block = ctx.enter_context(nc.Block())

        def split_rows(ap, per, real):
            whole = ap[0:(P - 1) * per].rearrange("(p j) -> p j", j=per)
            last = ap[(P - 1) * per:(P - 1) * per + real].rearrange("(p j) -> p j", p=1)
            return ((slice(0, 112), per, whole[0:112, :]), (slice(112, P - 1), per, whole[112:P - 1, :]),
                    (slice(P - 1, P), real, last))

        @block.sync
        def _(sp):
            sp.wait_ge(s_pads, 1)
            for rows, n, part in split_rows(dst, COLS, REAL):
                sp.dma_start(hi_f.bitcast(I32)[rows, 0:n], part).then_inc(s_dst, 16)
            for rows, n, part in split_rows(src, COLS, REAL):
                sp.dma_start(src_i[rows, 0:n], part).then_inc(s_src, 16)
            sp.dma_start(prev_i[1:P, :], dst[COLS - 1:E:COLS].unsqueeze(1),
                         allow_slow_non_contiguous=True).then_inc(s_prev, 16)
            xn_flat = xn.rearrange("p c f -> p (c f)")
            for rows, n, part in split_rows(x.rearrange("n f -> (n f)"), NCOL * D, NREAL * D):
                sp.dma_start(xn_flat[rows, 0:n], part).then_inc(s_x, 16)
            sp.wait_ge(s_flag, 1)
            unsorted = sp.value_load(flag_i[0:1, 0:1], min_val=0, max_val=1)
            with sp.If(unsorted > 0):
                sp.wait_ge(s_recs, 2)
                sp.dma_start(recs_d[0].rearrange("(p j) r -> p j r", p=P), recs).then_inc(s_recd, 16)
                sp.wait_ge(s_recd, 16)
                for m in range(2):
                    with sp.Fori(0, COLS) as t:
                        sp.dma_start(rec[:, :], recs_d[m][bass.ds(t * P, P), :]).then_inc(s_rec[m], 16)
                        sp.wait_ge(s_put[m], (t + 1) * 16)
                        sp.sem_inc(s_past, 1)
                with sp.Fori(0, COLS) as t:
                    sp.dma_start(rec[:, :], recs_d[2][bass.ds(t * P, P), :]).then_inc(s_rec[2], 16)
                    sp.wait_ge(s_erow, (t + 1) * 16)
                    sp.dma_start(edge_s[bass.ds(t * P, P), :], erow).then_inc(s_erowd, 16)
                    sp.wait_ge(s_erowd, (t + 1) * 16)
                    sp.sem_inc(s_past, 1)
                sp.dma_start(recs, recs_d[2].rearrange("(p j) r -> p j r", p=P)).then_inc(s_back, 16)
                sp.dma_start(prev_f[1:P, :], recs_d[2][COLS - 1:EP - 1:COLS, 0:1],
                             allow_slow_non_contiguous=True).then_inc(s_back, 16)
                sp.wait_ge(s_sorted, 1)

            sp.wait_ge(s_wcs, 1)
            sp.wait_ge(s_wz, 1)
            for l in range(3):
                for q in range(4):
                    sp.dma_start(wd_sb[q * D:(q + 1) * D, l, q * KD:(q + 1) * KD], wc_sb[:, l, :]).then_inc(s_wd, 16)

            def from_edges(load):
                with sp.If(unsorted > 0):
                    load(edge_s)
                with sp.If(unsorted < 1):
                    load(edge)

            def load_edges(b, k, j0):
                from_edges(lambda table: load_parts(table, b, k, j0))

            def load_parts(edge, b, k, j0):
                n = CB if b < NB else TAIL
                for rows in (slice(0, 112), slice(112, P - 1)):
                    flat = edge[0:(P - 1) * COLS, :].rearrange("(p j) f -> p j f", j=COLS)
                    sp.dma_start(attr[k][rows, 0:n, :], flat[rows, j0:j0 + n, :]).then_inc(s_ed[k], 16)
                real = min(max(REAL - j0, 0), n)
                if real:
                    first = (P - 1) * COLS + j0
                    sp.dma_start(attr[k][P - 1:P, 0:real, :],
                                 edge[first:first + real, :].rearrange("(p j) f -> p j f", p=1)).then_inc(s_ed[k], 16)

            def load_spread(k, j0, n):
                sp.dma_start(spread[k][:, 0:n, :], xd_v[:, bass.ds(j0, n), :]).then_inc(s_xd[k], 16)

            def load_sources(k, j0, n, groups, stored):
                if groups is not None:
                    sp.wait_ge(s_t, groups)
                sp.wait_ge(s_xst[k], stored)
                sp.dma_start(slot0[k][:, 0:n, 0:D], xs_v[:, bass.ds(j0, n), :]).then_inc(s_xl[k], 16)

            def whole_columns(table):
                return bass.AP(tensor=table.tensor, offset=0, ap=[[COLS * D, P], [D, (NB - 1) * CB], [1, D]])

            def load_whole(k, j0):
                from_edges(lambda table: sp.dma_start(attr[k], whole_columns(table)[:, bass.ds(j0, CB), :])
                           .then_inc(s_ed[k], 16))

            def store_max(k, j0, n, done):
                sp.wait_ge(s_max, done)
                sp.dma_start(scan0_v[:, bass.ds(j0, n), :], spread[k][:, 0:n, :]).then_inc(s_st0[k], 16)

            sp.wait_ge(s_idx, 1)
            load_whole(0, 0)
            load_whole(1, CB)
            sp.wait_ge(s_xscat, 16 * NCOL)
            sp.wait_ge(s_x0, 16)
            sp.dma_start(xd_v[:, 0, :], x0[:, :]).then_inc(s_xrow, 16)
            sp.wait_ge(s_xrow, 16)
            for k in range(2):
                load_spread(k, k * CB, CB)
                load_sources(k, k * CB, CB, None, 16)
            store_max(0, 0, CB, 1)
            with sp.Fori(1, ROUNDS - 1) as r:
                for k in range(2):
                    sp.wait_ge(s_fill, r * 2 + (k - 1))
                    sp.sem_inc(s_past, 1)
                    load_whole(k, r * (2 * CB) + k * CB)
                    sp.wait_ge(s_st0[k], r * 16)
                    load_spread(k, r * (2 * CB) + k * CB, CB)
                    load_sources(k, r * (2 * CB) + k * CB, CB, (r * 2 + (k - 1)) * GB, (r + 1) * 16)
                    store_max(1 - k, r * (2 * CB) + (k - 1) * CB, CB, r * 2 + k)
            for b in range(NB - 2, NB + 1):
                k = b % 2
                n = CB if b < NB else TAIL
                sp.wait_ge(s_fill, b - 1)
                if b == NB - 2:
                    load_whole(k, b * CB)
                else:
                    load_edges(b, k, b * CB)
                sp.wait_ge(s_st0[k], b // 2 * 16)
                load_spread(k, b * CB, n)
                load_sources(k, b * CB, n, (b - 1) * GB, (b // 2 + 1) * 16)
                store_max(1 - k, (b - 1) * CB, CB, b)
            store_max(NB % 2, NB * CB, TAIL, NB + 1)

            for l in range(3):
                for q, (c0, c1) in enumerate(QUARTERS):
                    sp.wait_ge(s_tab, l * len(QUARTERS) + q + 1)
                    sp.dma_start(table_d.rearrange("(p c) f -> p c f", p=P)[:, c0:c1, :],
                                 tab[:, c0:c1, :]).then_inc(s_tabd, 16)
                    sp.dma_start(adn_d.rearrange("(p c) f -> p c f", p=P)[:, c0:c1, :],
                                 adt[:, c0:c1, :]).then_inc(s_adnd, 16)
                sp.wait_ge(s_ascat, 16 * NCOL * (l + 1))
                sp.wait_ge(s_a0, 16 * (l + 1))
                sp.dma_start(ad_v[:, 0, :], a0[:, :]).then_inc(s_arow, 16)
                sp.wait_ge(s_arow, 16 * (l + 1))
                sp.dma_start(adf[:, :, :], ad_v).then_inc(s_adf, 16)

                done = l * (NB + 1)

                def store_sum(k, j0, n, blocks):
                    sp.wait_ge(s_sum, blocks)
                    sp.dma_start(scan_v[:, bass.ds(j0, n), :], slotg[k][:, 0:n, :]).then_inc(s_st[l][k], 16)

                with sp.Fori(0, ROUNDS) as r:
                    for k in range(2):
                        store_sum(k, r * (2 * CB) + k * CB, CB, r * 2 + (done + k + 1))
                store_sum(NB % 2, NB * CB, TAIL, done + NB + 1)
            sp.wait_ge(s_fin, len(QUARTERS))
            o_flat = work2[:, 0:NCOL, :].rearrange("p c f -> p (c f)")
            for rows, n, part in split_rows(out.rearrange("n f -> (n f)"), NCOL * D, NREAL * D):
                sp.dma_start(part, o_flat[rows, 0:n]).then_inc(s_out, 16)
            sp.wait_ge(s_out, 48)

        @block.gpsimd
        def _(pool):
            steps = [0]

            def step(ins):
                steps[0] += 1
                ins.then_inc(s_pool, 1)
                pool.wait_ge(s_pool, steps[0])

            step(pool.memset(ident[:, :], 0.0))
            step(pool.affine_select(out=ident[:, :], in_=ident[:, :], compare_op=ALU.not_equal, fill=1.0,
                                    base=0, pattern=[[-1, P]], channel_multiplier=1))
            step(pool.memset(upper[:, :], 1.0))
            step(pool.affine_select(out=upper[:, :], in_=upper[:, :], compare_op=ALU.is_gt, fill=0.0,
                                    base=0, pattern=[[1, P]], channel_multiplier=-1))
            step(pool.iota(iota_i[:, :], pattern=[[1, P]], base=0, channel_multiplier=0))
            step(pool.iota(spare_i[:, :], pattern=[[1, NCOL]], base=EP, channel_multiplier=NCOL))
            step(pool.iota(iota_ki, pattern=[[1, C2 * P]], base=0, channel_multiplier=0))
            step(pool.iota(row0_i[:, :], pattern=[[1, 1]], base=0, channel_multiplier=COLS))
            step(pool.memset(pick[:, :, :], 0.0))
            step(pool.memset(w2_sb[:, :], 0.0))
            for l in range(3):
                for h in range(2):
                    part = pick[:, l, h * HW:h * HW + 16]
                    step(pool.affine_select(out=part, in_=part, compare_op=ALU.not_equal, fill=1.0,
                                            base=-16 * h, pattern=[[-1, 16]], channel_multiplier=1))
            pool.memset(wd_sb[:, :, :], 0.0).then_inc(s_wz, 1)
            pool.engine_nop().then_inc(s_const, 1)

            step(pool.memset(ones_f[:, :], 1.0))
            pool.wait_ge(s_flag, 1)
            unsorted = pool.value_load(flag_i[0:1, 0:1], min_val=0, max_val=1)
            with pool.If(unsorted > 0):
                pool.iota(lo_f.bitcast(I32), pattern=[[1, COLS]], base=0, channel_multiplier=COLS).then_inc(s_recs, 1)
                for m in range(2):
                    with pool.Fori(0, COLS) as t:
                        pool.wait_ge(s_pos, t + (m * COLS + 1))
                        pool.sem_inc(s_sbegun, 1)
                        pool.indirect_dma_start(
                            out=recs_d[m + 1], out_offset=bass.IndirectOffsetOnAxis(ap=pos_i[:, :], axis=0),
                            in_=rec[:, :], in_offset=None).then_inc(s_put[m], 16)
                with pool.Fori(0, COLS) as t:
                    pool.wait_ge(s_eid, t + 1)
                    pool.sem_inc(s_sbegun, 1)
                    pool.indirect_dma_start(
                        out=erow, out_offset=None, in_=edge,
                        in_offset=bass.IndirectOffsetOnAxis(ap=pos_i[:, :], axis=0)).then_inc(s_erow, 16)
                pool.wait_ge(s_sorted, 1)

            def gather(table, k, j0, n, blocks, row, signal):
                pool.tensor_copy(index[:, k, 0:n], src_i[:, bass.ds(j0, n)]).then_inc(s_index, 1)
                pool.wait_ge(s_index, blocks + 1)
                pool.sem_inc(s_begun, 1)
                for j in range(n):
                    gather_one(row(j), table, index[:, k, j:j + 1], signal)

            def gather_one(rows, table, index, signal):
                pool.indirect_dma_start(out=rows, out_offset=None, in_=table,
                                        in_offset=bass.IndirectOffsetOnAxis(ap=index, axis=0)).then_inc(signal, 16)

            def scatter_one(table, index, rows, signal):
                pool.indirect_dma_start(out=table, out_offset=bass.IndirectOffsetOnAxis(ap=index, axis=0),
                                        in_=rows, in_offset=None).then_inc(signal, 16)

            def join_and_fetch(n_fix, scanned, width):
                gather_one(fix[:, 0:width], scanned, fe_i[:, :], s_fixg)
                pool.wait_ge(s_fixv, n_fix)
                scatter_one(scanned, fe_i[:, :], fo[:, 0:width], s_fixs)
                pool.wait_ge(s_fixs, 16 * n_fix)
                for q, (c0, c1) in enumerate(QUARTERS):
                    for c in range(c0, c1):
                        gather_one(nd[:, c, 0:width], scanned, end_i[:, c:c + 1], s_nd[q])

            def put_away(k, j0, n, gathered):
                pool.wait_ge(s_xs[k], gathered)
                pool.sem_inc(s_begun, 1)
                pool.dma_start(xs_v[:, bass.ds(j0, n), :], stage[k][:, 0:n, :]).then_inc(s_xst[k], 16)

            def fetch(k, j0, n, blocks, gathered, stored):
                if stored is not None:
                    pool.wait_ge(s_xst[k], stored)
                gather(x, k, j0, n, blocks, lambda j: stage[k][:, j, :], s_xs[k])
                if gathered is not None:
                    put_away(1 - k, j0 - CB, CB, gathered)

            pool.wait_ge(s_src, 48)
            fetch(0, 0, CB, 0, None, None)
            fetch(1, CB, CB, 1, 16 * CB, None)

            def rounds(first, last):
                with pool.Fori(first, last) as r:
                    fetch(0, r * (2 * CB), CB, r * 2, r * (16 * CB), r * 16)
                    fetch(1, r * (2 * CB) + CB, CB, r * 2 + 1, (r + 1) * (16 * CB), r * 16)

            rounds(1, EARLY // 2)
            pool.wait_ge(s_x, 48)
            pool.wait_ge(s_idx, 1)
            pool.wait_ge(s_zero, 32)
            for c in range(NCOL):
                scatter_one(xd_d, start_i[:, c:c + 1], xn[:, c, :], s_xscat)
            gather_one(x0[:, :], x, dst0_i[:, :], s_x0)
            rounds(EARLY // 2, ROUNDS)
            fetch(0, NB * CB, TAIL, NB, ROUNDS * 16 * CB, ROUNDS * 16)
            put_away(0, NB * CB, TAIL, ROUNDS * 16 * CB + 16 * TAIL)
            pool.wait_ge(s_st0[0], 16 * (ROUNDS + 1))
            pool.wait_ge(s_st0[1], 16 * ROUNDS)
            join_and_fetch(1, scan0_d, D)

            for l in range(3):
                done = (l + 1) * (NB + 1)
                for q, (c0, c1) in enumerate(QUARTERS):
                    pool.wait_ge(s_tab, l * len(QUARTERS) + q + 1)
                    for c in range(c0, c1):
                        scatter_one(ad_d, start_i[:, c:c + 1], adt[:, c, :], s_ascat)
                pool.wait_ge(s_adnd, 16 * len(QUARTERS) * (l + 1))
                gather_one(a0[:, :], adn_d, dst0_i[:, :], s_a0)
                pool.wait_ge(s_tabd, 16 * len(QUARTERS) * (l + 1))
                for k in range(2):
                    gather(table_d, k, k * CB, PG, done + k, lambda j: slotg[k][:, j, :], s_g[l][k])
                with pool.Fori(1, ROUNDS) as r:
                    for k in range(2):
                        pool.wait_ge(s_st[l][k], r * 16)
                        gather(table_d, k, r * (2 * CB) + k * CB, PG, r * 2 + (done + k),
                               lambda j: slotg[k][:, j, :], s_g[l][k])
                pool.wait_ge(s_st[l][0], 16 * ROUNDS)
                gather(table_d, 0, NB * CB, TAIL, done + NB, lambda j: slotg[0][:, j, :], s_g[l][0])
                pool.wait_ge(s_st[l][0], 16 * (ROUNDS + 1))
                pool.wait_ge(s_st[l][1], 16 * ROUNDS)
                join_and_fetch(l + 2, scan_d, ROW)

        @block.tensor
        def _(pe):
            pe.wait_ge(s_const, 1)
            pe.wait_ge(s_viol, 1)
            pe.matmul(flag_ps, viol[:, :], onesn[:, 0:1], start=True, stop=True).then_inc(s_violp, 1)
            pe.wait_ge(s_flag, 1)
            unsorted = pe.value_load(flag_i[0:1, 0:1], min_val=0, max_val=1)
            with pe.If(unsorted > 0):
                pe.wait_ge(s_cntd, 1)
                pe.matmul(total_ps, ones_f[:, :], cnt, start=True, stop=True).then_inc(s_totd, 1)
                for m in range(2):
                    with pe.Fori(0, COLS) as t:
                        pe.wait_ge(s_ohs, t + (m * COLS + 1))
                        pe.matmul(rank_ps, upper_b, oh_s, start=True, stop=True)
                        pe.matmul(add_ps, ones_b, oh_s, start=True, stop=True).then_inc(s_rank, 1)
            pe.wait_ge(s_w, 16 * LOADS)
            for l in range(3):
                last = pe.matmul(wc_ps[:, l, :], gw_sb[:, l, :], pick[:, l, :], start=True, stop=True)
            last.then_inc(s_wc, 1)
            def count(m, k, n, first=False, final=False):
                pe.wait_ge(s_oh, m)
                for j in range(n):
                    last = pe.matmul(count_ps, oh_hi[k][:, j, :], oh_lo[k][:, j, :],
                                     start=first and j == 0, stop=final and j == n - 1, skip_group_check=True)
                last.then_inc(s_cnt, 1)

            count(1, 0, OH, first=True)
            count(2, 1, OH)
            with pe.Fori(1, OHN // 2) as r:
                for k in range(2):
                    count(r * 2 + (k + 1), k, OH)
            for m in range(OHN - OHN % 2, OHN):
                count(m + 1, m % 2, OH)
            count(OHN + 1, OHN % 2, OHT, final=True)
            pe.wait_ge(s_tot, 1)
            pe.matmul(before_ps, upper[:, :], tot[:, :], start=True, stop=True).then_inc(s_bef, 1)

            def block0(k, use, base, blocks, n):
                groups = -(-n // GW)
                pe.wait_ge(s_xl[k], use)
                pe.wait_ge(s_fill, blocks + 1)
                for i in range(groups + 2):
                    if i < groups:
                        if base is not None:
                            pe.wait_ge(s_tc, base + (i - 1))
                        elif i >= 2:
                            pe.wait_ge(s_tc, i - 1)
                        for q, j in enumerate((0, 2, 1, 3)):
                            last = pe.transpose(t_ps[i % 2][0:3 * D, q * P:(q + 1) * P],
                                                slot0[k][:, GW * i + j, :], ident[:, :])
                        last.then_inc(s_t, 1)
                    if 1 <= i <= groups:
                        g = i - 1
                        pe.wait_ge(s_tc, (0 if base is None else base) + (g + 1))
                        if base is not None:
                            pe.wait_ge(s_hr, base + (g - 1))
                        elif g >= 2:
                            pe.wait_ge(s_hr, g - 1)
                        for h in range(2):
                            last = pe.matmul(h_ps[g % 2][h * HID:(h + 1) * HID, 0:2 * P], w1_sb[:, :],
                                             xt_sb[0:3 * D, g % 2, 2 * h * P:2 * (h + 1) * P], start=True, stop=True)
                        last.then_inc(s_h, 1)
                    if i >= 2:
                        g = i - 2
                        pe.wait_ge(s_hr, (0 if base is None else base) + (g + 1))
                        if g == 0 and base is not None:
                            pe.wait_ge(s_max, blocks)
                        for q in range(2):
                            j = GW * g + 2 * q
                            last = pe.matmul(v_ps[:, j:j + 2, :], h_sb[:, g % 2, q * P:(q + 1) * P], w2_sb[:, :],
                                             start=True, stop=True)
                        last.then_inc(s_vp, 1)

            block0(0, 16, None, 0, CB)
            block0(1, 16, GB, 1, CB)
            with pe.Fori(1, ROUNDS) as r:
                for k in range(2):
                    block0(k, (r + 1) * 16, r * (2 * GB) + k * GB, r * 2 + k, CB)
            block0(0, (ROUNDS + 1) * 16, NB * GB, NB, TAIL)

            def tails(n):
                pe.wait_ge(s_tail, n)
                pe.transpose(t_ps[0][0:ROW, 0:P], (maxc if n == 1 else sumc)[:, :], ident[:, :])
                last = pe.transpose(t_ps[0][0:ROW, P:2 * P], wmask[:, :], ident[:, :])
                if n > 1:
                    last = pe.transpose(t_ps[0][0:ROW, 2 * P:3 * P], mrep[:, :], ident[:, :])
                last.then_inc(s_tailt, 1)
                pe.wait_ge(s_car, n)
                last = pe.transpose(t_ps[1][:, 0:ROW], si_t[:, 0:P], ident[0:ROW, 0:ROW])
                if n > 1:
                    last = pe.transpose(t_ps[1][:, 64:64 + ROW], mi_t[:, 0:P], ident[0:ROW, 0:ROW])
                last.then_inc(s_cart, 1)

            def table(l, q):
                feats = x1 if l == 0 else work
                pe.wait_ge(s_node, l * len(QUARTERS) + q + 1)
                c0, c1 = QUARTERS[q]
                groups = range(c0 // 4, -(-c1 // 4))
                for i in [*groups, groups[-1] + 1]:
                    n = l * NQ + i
                    if i in groups:
                        if n >= 2:
                            pe.wait_ge(s_ntc, n - 1)
                        pe.transpose(t_ps[n % 2][:, 0:P], feats[:, 4 * i:4 * i + 4, :], ident[:, :]).then_inc(s_nt, 1)
                    if i - 1 in groups:
                        n -= 1
                        pe.wait_ge(s_ntc, n + 1)
                        if n >= 2:
                            pe.wait_ge(s_npc, n - 1)
                        pe.matmul(h_ps[n % 2][:, 0:4 * KD], xt_sb[:, n % 2, 0:P], wd_sb[:, l, :],
                                  start=True, stop=True).then_inc(s_np, 1)

            def fetch_block(n0):
                def transposes(i):
                    pe.wait_ge(s_ohe, n0 + (i + 1))
                    if not isinstance(n0, int) or n0 + i >= 2:
                        pe.wait_ge(s_ohc, n0 + (i - 1))
                    for c in range(C2):
                        last = pe.transpose(oht_ps[i % 2][:, c * P:(c + 1) * P],
                                            onehot_e[(off + i) % 4][:, c * P:(c + 1) * P], ident_b[:, :])
                    last.then_inc(s_oht, 1)

                off = fetch_off[0]
                transposes(0)
                for i in range(KG):
                    if i + 1 < KG:
                        transposes(i + 1)
                    pe.wait_ge(s_ohc, n0 + (i + 1))
                    if not isinstance(n0, int) or n0 + i >= 4:
                        pe.wait_ge(s_pick, n0 + (i - 3))
                    for c in range(C2):
                        for part in parts:
                            last = pe.matmul(sel_ps[(off + i) % 4], onehot_t[i % 2][:, c * P:(c + 1) * P],
                                             part[:, c * C1 * ROW:(c + 1) * C1 * ROW],
                                             start=c == 0 and part is parts[0],
                                             stop=c == C2 - 1 and part is parts[2])
                    last.then_inc(s_sel, 1)
                fetch_off[0] = (off + KG) % 4

            fetch_off = [0]
            tails(1)
            pe.wait_ge(s_wd, 16 * 12)
            for l in range(3):
                for q in range(len(QUARTERS)):
                    table(l, q)
                first = l * NB * KG
                fetch_block(first)
                fetch_block(first + KG)
                with pe.Fori(1, ROUNDS) as r:
                    for k in range(2):
                        fetch_block(r * (2 * KG) + (first + k * KG))
                tails(l + 2)

        @block.scalar
        def _(act):
            act.wait_ge(s_wz, 1)
            act.wait_ge(s_const, 1)
            act.dma_start(w1_sb[:, :], w1).then_inc(s_w, 16)
            for h in range(2):
                half = slice(h * HID, (h + 1) * HID)
                act.dma_start(w2_sb[half, h * D:(h + 1) * D], w2).then_inc(s_w, 16)
                act.dma_start(b1_sb[half, :], b1.unsqueeze(1), allow_slow_non_contiguous=True).then_inc(s_w, 16)
            act.dma_start(b2_sb[:, :], b2.partition_broadcast(P)).then_inc(s_w, 16)
            act.dma_start(ea_sb[:, :], ea1.partition_broadcast(P)).then_inc(s_w, 16)
            for l, (w, att_s, att_d, b) in enumerate(gat):
                act.dma_start(gw_sb[:, l, :], w).then_inc(s_w, 16)
                act.dma_start(bg_sb[:, l, :], b.partition_broadcast(P)).then_inc(s_w, 16)
                heads = att_s.shape[0]
                for h in range(2):
                    rows = slice(16 * h, 16 * h + 16) if heads == 2 else slice(0, D)
                    head = h if heads == 2 else 0
                    for column, att in ((h * HW + HW - 1, att_s), (ROW + h, att_d)):
                        act.dma_start(pick[rows, l, column:column + 1], att[head, :].unsqueeze(1),
                                          allow_slow_non_contiguous=True).then_inc(s_w, 16)
            act.wait_ge(s_zs, 1)
            act.dma_start(xd_v.rearrange("p (a j) f -> p a (j f)", j=11),
                          zeros[:, 0:11 * D].unsqueeze(1).broadcast_to([P, COLS // 11, 11 * D])).then_inc(s_zero, 16)
            act.dma_start(ad_v.rearrange("p j h -> p (j h)").rearrange("p (a z) -> p a z", z=ZW),
                          zeros.unsqueeze(1).broadcast_to([P, 11, ZW])).then_inc(s_zero, 16)

            def block0(base, n):
                groups = -(-n // GW)
                for i in range(groups + 1):
                    if i < groups:
                        act.wait_ge(s_t, (0 if base is None else base) + (i + 1))
                        if base is not None:
                            act.wait_ge(s_h, base + (i - 1))
                        elif i >= 2:
                            act.wait_ge(s_h, i - 1)
                        act.activation(xt_sb[0:3 * D, i % 2, :], t_ps[i % 2][0:3 * D, :], ACT.Copy).then_inc(s_tc, 1)
                    if i >= 1:
                        g = i - 1
                        act.wait_ge(s_h, (0 if base is None else base) + (g + 1))
                        if base is not None:
                            act.wait_ge(s_vp, base + (g - 1))
                        elif g >= 2:
                            act.wait_ge(s_vp, g - 1)
                        act.activation(h_sb[:, g % 2, :], h_ps[g % 2][:, 0:2 * P], ACT.Relu,
                                       bias=b1_sb[:, 0:1]).then_inc(s_hr, 1)

            act.wait_ge(s_w, 16 * LOADS)
            act.activation(sc_out[:, :], ea_sb[:, :], ACT.Tanh).then_inc(s_te, 1)
            block0(None, CB)
            block0(GB, CB)
            with act.Fori(1, ROUNDS) as r:
                for k in range(2):
                    block0(r * (2 * GB) + k * GB, CB)
            block0(NB * GB, TAIL)

            asked = [0]

            def serve(out_ap, in_ap, what):
                asked[0] += 1
                act.wait_ge(s_ain, asked[0])
                act.activation(out_ap, in_ap, what).then_inc(s_aout, 1)

            def norm_parts(c0, c1):
                serve(work[:, c0:c1, :], work2[:, c0:c1, :], ACT.Square)
                serve(nt[:, 2, c0:c1], nt[:, 1, c0:c1], ACT.Sqrt)

            def copy_nodes(l, q):
                c0, c1 = QUARTERS[q]
                for i in range(c0 // 4, -(-c1 // 4)):
                    n = l * NQ + i
                    act.wait_ge(s_nt, n + 1)
                    if n >= 2:
                        act.wait_ge(s_np, n - 1)
                    act.activation(xt_sb[:, n % 2, 0:P], t_ps[n % 2][:, 0:P], ACT.Copy).then_inc(s_ntc, 1)

            for l in range(3):
                for q, (c0, c1) in enumerate(QUARTERS):
                    if l == 0:
                        norm_parts(c0, c1)
                    else:
                        serve(work2[:, c0:c1, :], work2[:, c0:c1, :], ACT.Exp)
                    if q:
                        copy_nodes(l, q - 1)
                copy_nodes(l, len(QUARTERS) - 1)
                done = l * (NB + 1)

                def exps(blocks, n):
                    act.wait_ge(s_exin, blocks)
                    act.activation(ex[:, :, :, 0:n], ex_in[:, :, :, 0:n], ACT.Exp).then_inc(s_ex, 1)

                def copies(n0, columns):
                    for i in columns:
                        act.wait_ge(s_oht, n0 + (i + 1))
                        if not isinstance(n0, int) or n0 + i >= 2:
                            act.wait_ge(s_sel, n0 + (i - 1))
                        act.activation(onehot_t[i % 2], oht_ps[i % 2], ACT.Copy).then_inc(s_ohc, 1)

                first = l * NB * KG
                copies(first, range(KG))
                for b in range(2):
                    copies(first + (b + 1) * KG, range(2))
                    exps(done + b + 1, CB)
                    copies(first + (b + 1) * KG, range(2, KG))
                with act.Fori(1, ROUNDS - 1) as r:
                    for k in range(2):
                        copies(r * (2 * KG) + (first + (k + 1) * KG), range(2))
                        exps(r * 2 + (done + k + 1), CB)
                        copies(r * (2 * KG) + (first + (k + 1) * KG), range(2, KG))
                copies(first + (NB - 1) * KG, range(2))
                exps(done + NB - 1, CB)
                copies(first + (NB - 1) * KG, range(2, KG))
                exps(done + NB, CB)
                exps(done + NB + 1, TAIL)
                act.wait_ge(s_tein, l + 1)
                act.activation(te[:, :, :], te_in[:, :, :], ACT.Exp).then_inc(s_te, 1)
                act.wait_ge(s_fein, l + 1)
                act.activation(fe[:, :, :], fe_in[:, :, :], ACT.Exp).then_inc(s_fe, 1)
            for c0, c1 in QUARTERS:
                norm_parts(c0, c1)

        @block.vector
        def _(dve):
            count = [0]

            def mark(ins):
                count[0] += 1
                ins.then_inc(s_v, 1)

            def link(ins):
                mark(ins)
                dve.wait_ge(s_v, count[0])

            tt, ts, stt = dve.tensor_tensor, dve.tensor_scalar, dve.scalar_tensor_tensor

            hi_i = hi_f.bitcast(I32)
            link(dve.memset(hi_i[96:P, REAL:COLS], N))
            link(dve.memset(src_i[96:P, REAL:COLS], 0))
            link(dve.memset(xn[96:P, NREAL:NCOL, :], 0.0))
            dve.memset(prev_i[:, :], -1).then_inc(s_pads, 1)
            dve.memset(zeros, 0.0).then_inc(s_zs, 1)
            mark(dve.memset(onesn[:, :], 1.0))
            mark(dve.memset(x1[:, NCOL:4 * NQ, :], 0.0))
            mark(dve.memset(fillc[:, :], 0.0))
            mark(dve.memset(maxc[:, :], 0.0))
            mark(dve.memset(si_t[:, 0:1], 0.0))
            mark(dve.memset(mi_t[:, 0:1], 0.0))

            dve.wait_ge(s_dst, 48)
            dve.wait_ge(s_prev, 16)
            mark(dve.tensor_copy(prev_f[:, :], prev_i[:, :]))
            link(dve.tensor_copy(dst_f[:, :], hi_i))
            mark(tt(same[:, 1:COLS], dst_f[:, 1:COLS], dst_f[:, 0:COLS - 1], ALU.is_lt))
            link(tt(same[:, 0:1], dst_f[:, 0:1], prev_f[:, :], ALU.is_lt))
            dve.reduce_sum(viol[:, :], same[:, :], X).then_inc(s_viol, 1)
            dve.wait_ge(s_violp, 1)
            ts(flag_i[:, :], flag_ps, 1.0, None, ALU.min).then_inc(s_flag, 1)
            dve.wait_ge(s_flag, 1)
            unsorted = dve.value_load(flag_i[0:1, 0:1], min_val=0, max_val=1)
            dve.wait_ge(s_const, 1)
            link(dve.tensor_copy(iota_b[:, :], iota_i[:, :]))

            own_s = [0]

            def srt(ins):
                own_s[0] += 1
                ins.then_inc(s_srt, 1)
                dve.wait_ge(s_srt, own_s[0])

            def digit(out_hi, out_lo, values, run, radix=NCOL):
                run(ts(out_hi, values, 0.5, 1.0 / radix, ALU.add, ALU.mult))
                run(ts(out_hi, out_hi, -0.5, None, ALU.add))
                run(ts(out_hi, out_hi, ROUND, None, ALU.add))
                run(ts(out_hi, out_hi, -ROUND, None, ALU.add))
                run(stt(out_lo, out_hi, -float(radix), values, ALU.mult, ALU.add))

            with dve.If(unsorted > 0):
                dve.wait_ge(s_src, 48)
                srt(dve.tensor_copy(recs[:, :, 0], dst_f[:, :]))
                srt(dve.tensor_copy(recs[:, :, 1], src_i[:, :]))
                dve.wait_ge(s_recs, 1)
                srt(dve.tensor_copy(reset[:, :], lo_f.bitcast(I32)))
                ts(recs[:, :, 2], reset[:, :], float(E - 1), None, ALU.min).then_inc(s_recs, 1)
                dve.wait_ge(s_recs, 2)
                srt(dve.memset(cnt, 0.0))
                srt(dve.tensor_copy(upper_b, upper[:, :]))
                srt(dve.memset(ones_b, 1.0))
                digit(hi_f, lo_f, dst_f[:, :], srt)
                for m, (digits_m, values) in enumerate(((lo_f, NCOL), (hi_f, P))):
                    with dve.Fori(0, values) as d:
                        dve.tensor_copy(key[:, 0:1], iota_b[:, bass.ds(d, 1)]).then_inc(s_dig, 1)
                        dve.wait_ge(s_dig, d * 3 + (m * NCOL * 3 + 1))
                        ts(reset[:, :], digits_m, key[:, 0:1], None, ALU.is_equal).then_inc(s_dig, 1)
                        dve.wait_ge(s_dig, d * 3 + (m * NCOL * 3 + 2))
                        dve.reduce_sum(cnt[:, m, bass.ds(d, 1)], reset[:, :], X).then_inc(s_dig, 1)
                        dve.wait_ge(s_dig, d * 3 + (m * NCOL * 3 + 3))
                dve.engine_nop().then_inc(s_cntd, 1)
                dve.wait_ge(s_totd, 1)
                srt(dve.tensor_copy(cnt, total_ps.rearrange("p (m d) -> p m d", m=2)))
                for m in range(2):
                    srt(dve.tensor_tensor_scan(base[:, m, :], ones_f[:, :], cnt[:, m, :], 0.0, ALU.mult, ALU.add))
                srt(tt(base, base, cnt, ALU.subtract))
                STEP = 9
                for m in range(2):
                    with dve.Fori(0, COLS) as t:
                        own = [0]

                        def run(ins):
                            own[0] += 1
                            ins.then_inc(s_srp[m], 1)
                            dve.wait_ge(s_srp[m], t * STEP + own[0])

                        dve.wait_ge(s_rec[m], (t + 1) * 16)
                        digit(key[:, 0:1], key[:, 1:2], rec[:, 0:1], run)
                        of = key[:, 1:2] if m == 0 else key[:, 0:1]
                        ts(oh_s, iota_b[:, :], of, None, ALU.is_equal).then_inc(s_ohs, 1)
                        dve.wait_ge(s_rank, t + (m * COLS + 1))
                        run(tt(places, rank_ps, base[:, m, :], ALU.add))
                        run(tt(places, places, oh_s, ALU.mult))
                        run(dve.reduce_sum(key[:, 2:3], places, X))
                        run(tt(base[:, m, :], base[:, m, :], add_ps, ALU.add))
                        assert own[0] == STEP
                        dve.tensor_copy(pos_i[:, :], key[:, 2:3]).then_inc(s_pos, 1)
                with dve.Fori(0, COLS) as t:
                    dve.wait_ge(s_rec[2], (t + 1) * 16)
                    dve.tensor_copy(pos_i[:, :], rec[:, 2:3]).then_inc(s_eid, 1)
                dve.wait_ge(s_back, 32)
                srt(dve.tensor_copy(dst_f[:, :], recs[:, :, 0]))
                srt(dve.tensor_copy(src_i[:, :], recs[:, :, 1]))
                dve.engine_nop().then_inc(s_sorted, 1)

            mark(dve.memset(same[:, 0:1], 0.0))
            mark(dve.tensor_copy(dst0_i[:, :], dst_f[:, 0:1]))
            digit(hi_f, lo_f, dst_f[:, :], link)
            def onehots(m, k, j0, n, wait):
                if wait is not None:
                    dve.wait_ge(s_cnt, wait)
                dve.tensor_copy(digits[:, 0, 0:n], hi_f[:, bass.ds(j0, n)])
                dve.tensor_copy(digits[:, 1, 0:n], lo_f[:, bass.ds(j0, n)]).then_inc(s_ohd, 1)
                dve.wait_ge(s_ohd, m)
                for j in range(n):
                    ts(oh_hi[k][:, j, :], iota_b[:, :], digits[:, 0, j:j + 1], None, ALU.is_equal)
                    last = ts(oh_lo[k][:, j, :], iota_b[:, 0:NCOL], digits[:, 1, j:j + 1], None, ALU.is_equal)
                last.then_inc(s_oh, 1)
                dve.wait_ge(s_oh, m)

            onehots(1, 0, 0, OH, None)
            onehots(2, 1, OH, OH, None)
            with dve.Fori(1, OHN // 2) as r:
                for k in range(2):
                    onehots(r * 2 + (k + 1), k, r * (2 * OH) + k * OH, OH, r * 2 + (k - 1))
            for m in range(OHN - OHN % 2, OHN + 1):
                onehots(m + 1, m % 2, m * OH, OH if m < OHN else OHT, m - 1)

            dve.wait_ge(s_cnt, OHN + 1)
            link(dve.tensor_copy(deg[:, :], count_ps))
            link(dve.tensor_tensor_scan(cum[:, :], onesn[:, :], deg[:, :], 0.0, ALU.mult, ALU.add))
            dve.tensor_copy(tot[:, :], cum[:, NCOL - 1:NCOL]).then_inc(s_tot, 1)
            mark(ts(has[:, :], deg[:, :], 0.5, None, ALU.is_gt))
            link(dve.tensor_copy(spare[:, :], spare_i[:, :]))
            link(ts(pen[:, :], has[:, :], -1.0, -LOW, ALU.add, ALU.mult))
            dve.wait_ge(s_bef, 1)
            link(dve.tensor_copy(before[:, :], before_ps))
            link(ts(cum[:, :], cum[:, :], before[:, 0:1], None, ALU.add))
            link(tt(nt[:, 0, :], cum[:, :], deg[:, :], ALU.subtract))
            link(tt(nt[:, 0, :], nt[:, 0, :], spare[:, :], ALU.subtract))
            link(tt(nt[:, 0, :], nt[:, 0, :], has[:, :], ALU.mult))
            link(tt(nt[:, 0, :], nt[:, 0, :], spare[:, :], ALU.add))
            mark(dve.tensor_copy(start_i[:, :], nt[:, 0, :]))
            link(ts(nt[:, 1, :], cum[:, :], -1.0, 0.0, ALU.add, ALU.max))
            link(dve.tensor_copy(end_i[:, :], nt[:, 1, :]))

            link(tt(same[:, 1:COLS], dst_f[:, 1:COLS], dst_f[:, 0:COLS - 1], ALU.is_equal))
            link(ts(reset[:, :], same[:, :], -1.0, -LOW, ALU.add, ALU.mult))
            link(tt(cont[:, :], prev_f[:, :], dst_f[:, 0:1], ALU.is_equal))
            link(ts(cmask[:, :], cont[:, :], -1.0, -LOW, ALU.add, ALU.mult))
            link(tt(pt[:, 0:1], dst_f[:, 0:1], dst_f[:, COLS - 1:COLS], ALU.is_equal))
            link(tt(pt[:, 0:1], pt[:, 0:1], cont[:, :], ALU.mult))
            link(ts(pt[:, 0:1], pt[:, 0:1], -1.0, -LOW, ALU.add, ALU.mult))
            link(dve.tensor_copy(wmask[:, :], pt[:, 0:1].broadcast_to([P, ROW])))
            link(ts(hi_f, dst_f[:, :], dst_f[:, 0:1], None, ALU.is_equal))
            link(dve.reduce_sum(pt[:, 1:2], hi_f, X))
            link(dve.tensor_copy(pt[:, 2:3], row0_i[:, :]))
            link(tt(pt[:, 1:2], pt[:, 1:2], pt[:, 2:3], ALU.add))
            link(ts(pt[:, 1:2], pt[:, 1:2], -1.0, None, ALU.add))
            dve.tensor_copy(fe_i[:, :], pt[:, 1:2]).then_inc(s_idx, 1)
            dve.wait_ge(s_src, 48)
            flat = [dst_f[:, i * NB * KG:(i + 1) * NB * KG] for i in range(4)]
            src_v = src_i[:, 0:NB * CB].rearrange("p (b j) -> p b j", j=CB)[:, :, PG:CB]
            link(dve.tensor_copy(flat[0].rearrange("p (b j) -> p b j", j=KG), src_v))
            digit(flat[1], flat[2], flat[0], link)
            digit(flat[3], c1s[:, :, :].rearrange("p b j -> p (b j)"), flat[2], link, C1)
            link(stt(keys[:, :, :].rearrange("p b j -> p (b j)"), flat[3], float(P), flat[1], ALU.mult, ALU.add))
            mark(dve.tensor_copy(iota_key[:, :], iota_ki))
            mark(dve.tensor_copy(iota_c1[:, :], iota_i[:, 0:C1]))
            mark(dve.tensor_copy(ident_b[:, :], ident[:, :]))
            dve.wait_ge(s_wc, 1)
            dve.tensor_copy(wc_sb[:, :, :], wc_ps).then_inc(s_wcs, 1)
            dve.wait_ge(s_te, 1)
            link(ts(sc[:, 0:1], sc_out[:, :], 0.1, None, ALU.is_lt))
            link(ts(sc[:, 1:2], sc[:, 0:1], -1.0, 1.0, ALU.mult, ALU.add))
            link(tt(sc[:, 2:3], sc_out[:, :], sc[:, 1:2], ALU.mult))
            link(tt(sc[:, 2:3], sc[:, 2:3], sc[:, 0:1], ALU.add))

            def fill(k, j0, n, use, attrs, blocks):
                dve.wait_ge(s_xd[k], use)
                dve.tensor_copy(same_b[:, 0:n], same[:, bass.ds(j0, n)]).then_inc(s_fs, 1)
                dve.wait_ge(s_fs, blocks * 2 + 1)
                for f in range(D):
                    dve.tensor_tensor_scan(slot0[k][:, 0:n, D + f], same_b[:, 0:n], spread[k][:, 0:n, f],
                                           fillc[:, f:f + 1], ALU.mult, ALU.add)
                dve.wait_ge(s_ed[k], attrs)
                dve.tensor_copy(slot0[k][:, 0:n, 2 * D:3 * D], attr[k][:, 0:n, :]).then_inc(s_fill, 1)
                dve.wait_ge(s_fill, blocks + 1)
                dve.tensor_copy(fillc[:, :], slot0[k][:, n - 1, D:2 * D]).then_inc(s_fs, 1)
                dve.wait_ge(s_fs, blocks * 2 + 2)

            def maxima(k, j0, n, groups, blocks):
                dve.tensor_copy(reset_b[:, 0:n], reset[:, bass.ds(j0, n)]).then_inc(s_ms, 1)
                dve.wait_ge(s_ms, blocks * 2 + 1)
                dve.wait_ge(s_vp, groups)
                for f in range(D):
                    last = dve.tensor_tensor_scan(spread[k][:, 0:n, f], reset_b[:, 0:n], v_ps[:, 0:n, f],
                                                  maxc[:, f:f + 1], ALU.add, ALU.max)
                last.then_inc(s_ms, 1)
                dve.wait_ge(s_ms, blocks * 2 + 2)
                dve.tensor_copy(maxc[:, 0:D], spread[k][:, n - 1, :]).then_inc(s_max, 1)
                dve.wait_ge(s_max, blocks + 1)

            fill(0, 0, CB, 16, 16, 0)
            with dve.Fori(0, ROUNDS - 1) as r:
                for k in range(2):
                    fill(1 - k, r * (2 * CB) + (k + 1) * CB, CB, (r + (k + 1)) * 16, (r + (k + 1)) * 16, r * 2 + (k + 1))
                    maxima(k, r * (2 * CB) + k * CB, CB, r * (2 * GB) + (k + 1) * GB, r * 2 + k)
            fill(1, (NB - 1) * CB, CB, ROUNDS * 16, (ROUNDS - 1) * 16 + 48, NB - 1)
            maxima(0, (NB - 2) * CB, CB, (NB - 1) * GB, NB - 2)
            fill(0, NB * CB, TAIL, (ROUNDS + 1) * 16, ROUNDS * 16 + 32, NB)
            maxima(1, (NB - 1) * CB, CB, NB * GB, NB - 1)
            maxima(0, NB * CB, TAIL, NB * GB + GT, NB)

            dve.engine_nop().then_inc(s_tail, 1)
            dve.wait_ge(s_tailt, 1)
            link(dve.tensor_copy(wm_t[:, :], t_ps[0][0:ROW, P:2 * P]))
            link(dve.tensor_tensor_scan(si_t[:, 1:P + 1], wm_t[:, :], t_ps[0][0:ROW, 0:P], 0.0, ALU.add, ALU.max))
            dve.engine_nop().then_inc(s_car, 1)
            dve.wait_ge(s_cart, 1)
            link(ts(cs[:, :], t_ps[1][:, 0:ROW], cmask[:, 0:1], None, ALU.add))
            dve.wait_ge(s_fixg, 16)
            tt(fo[:, 0:D], fix[:, 0:D], cs[:, 0:D], ALU.max).then_inc(s_fixv, 1)

            def per_node(v, f=D):
                return v.unsqueeze(2).broadcast_to([P, v.shape[1], f])

            def per_feature(v, n):
                return v.unsqueeze(1).broadcast_to([P, n, D])

            asked = [0]

            def ask(ins):
                asked[0] += 1
                ins.then_inc(s_ain, 1)
                dve.wait_ge(s_aout, asked[0])

            def norm(c0, c1, result):
                wk, wk2 = work[:, c0:c1, :], work2[:, c0:c1, :]
                mean, var, sd, inv = (nt[:, i, c0:c1] for i in range(4))
                link(dve.reduce_sum(mean, wk, X))
                link(ts(mean, mean, 1.0 / D, None, ALU.mult))
                ask(tt(wk2, wk, per_node(mean), ALU.subtract))
                link(dve.reduce_sum(var, wk, X))
                ask(ts(var, var, 1.0 / D, 1e-5, ALU.mult, ALU.add))
                link(dve.reciprocal(inv, sd))
                return tt(result[:, c0:c1, :], wk2, per_node(inv), ALU.mult)

            def finish0(q):
                c0, c1 = QUARTERS[q]
                wk = work[:, c0:c1, :]
                dve.wait_ge(s_nd[q], 16 * (c1 - c0))
                link(tt(wk, nd[:, c0:c1, 0:D], per_feature(b2_sb[:, :], c1 - c0), ALU.add))
                link(tt(wk, wk, per_node(pen[:, c0:c1]), ALU.add))
                link(tt(wk, wk, x1[:, c0:c1, :], ALU.max))
                link(tt(wk, wk, x1[:, c0:c1, :], ALU.add))
                norm(c0, c1, x1).then_inc(s_node, 1)

            def finish(l, q):
                c0, c1 = QUARTERS[q]
                n = c1 - c0
                wk, wk2, rd = work[:, c0:c1, :], work2[:, c0:c1, :], rden[:, c0:c1, :]
                dve.wait_ge(s_nd[q], 16 * n * (l + 2))
                link(ts(rd, nd[:, c0:c1, 16:ROW:HW], 1e-16, None, ALU.add))
                link(dve.reciprocal(rd, rd))
                link(tt(rd, rd, per_node(has[:, c0:c1], 2), ALU.mult))
                link(tt(wk.rearrange("p c (h k) -> p c h k", h=2),
                        nd[:, c0:c1, :].rearrange("p c (h k) -> p c h k", h=2)[:, :, :, 0:16],
                        rd.unsqueeze(3).broadcast_to([P, n, 2, 16]), ALU.mult))
                link(tt(wk, wk, per_feature(bg_sb[:, l, :], n), ALU.add))
                if l == 0:
                    link(ts(wk, wk, sc[:, 2:3], None, ALU.mult))
                    link(stt(wk, wk, 0.05, wk, ALU.mult, ALU.add))
                if l < 2:
                    ask(ts(wk2, wk, 0.0, None, ALU.min))
                    link(ts(wk, wk, 0.0, None, ALU.max))
                    link(stt(wk, wk2, -1.0, wk, ALU.add, ALU.add))
                    if c1 == NCOL:
                        mark(dve.memset(work[:, NCOL:4 * NQ, :], 0.0))
                    ts(wk, wk, -3.0, 3.0, ALU.max, ALU.min).then_inc(s_node, 1)
                else:
                    link(tt(wk, wk, x1[:, c0:c1, :], ALU.add))
                    norm(c0, c1, work2).then_inc(s_fin, 1)

            def take_table(l, q):
                c0, c1 = QUARTERS[q]
                for g in range(c0 // 4, -(-c1 // 4)):
                    n = l * NQ + g
                    dve.wait_ge(s_np, n + 1)
                    prod = h_ps[n % 2][:, 0:4 * KD].rearrange("p (c k) -> p c k", k=KD)
                    dve.tensor_copy(tab[:, 4 * g:4 * g + 4, :], prod[:, :, 0:ROW])
                    dve.tensor_copy(adt[:, 4 * g:4 * g + 4, :], prod[:, :, ROW:KD]).then_inc(s_npc, 1)
                dve.wait_ge(s_npc, n + 1)
                dve.memset(tab[:, c0:c1, 16:ROW:HW], 1.0).then_inc(s_tab, 1)

            for l in range(3):
                for q in range(len(QUARTERS)):
                    if l == 0:
                        finish0(q)
                    else:
                        finish(l - 1, q)
                    if q:
                        take_table(l, q - 1)
                take_table(l, len(QUARTERS) - 1)
                mark(dve.memset(mx[:, :, 0:1], 0.0))
                link(dve.memset(sumc[:, :], 0.0))

                tab_flat = tab[:, 0:NCOL, :].rearrange("p c f -> p (c f)")
                link(dve.tensor_copy(parts[0], tab_flat))
                link(tt(rest, tab_flat, parts[0], ALU.subtract))
                link(dve.tensor_copy(parts[1], rest))
                link(tt(rest, rest, parts[1], ALU.subtract))
                link(dve.tensor_copy(parts[2], rest))

                dve.wait_ge(s_adf, 16 * (l + 1))
                for h in range(2):
                    mark(dve.tensor_tensor_scan(adf[:, :, h], same[:, :], adf[:, :, h], 0.0, ALU.mult, ALU.add))
                dve.wait_ge(s_v, count[0])
                done = l * (NB + 1)
                STEPS = 7

                first = l * NB * KG
                def ohe(n0, i, slot):
                    if not isinstance(n0, int) or n0 + i >= 4:
                        dve.wait_ge(s_oht, n0 + (i - 3))
                    ts(onehot_e[slot], iota_key[:, :], key_b[:, i:i + 1], None, ALU.is_equal).then_inc(s_ohe, 1)

                def begin_fetch(b, n0, k):
                    dve.tensor_copy(key_b[:, :], one_block(keys, b)).then_inc(s_keys, 1)
                    tt(onehot_c1[:, :, :], iota_c1[:, :].unsqueeze(1).broadcast_to([P, KG, C1]),
                       one_block(c1s, b).unsqueeze(2).broadcast_to([P, KG, C1]), ALU.is_equal).then_inc(s_keys, 1)
                    dve.wait_ge(s_keys, (b + l * NB) * 2 + 2)
                    for i in range(4):
                        ohe(n0, i, (k * KG + i) % 4)

                def one_block(v, b):
                    if isinstance(b, int):
                        return v[:, b, :]
                    return v[:, bass.ds(b, 1), :].rearrange("p b j -> p (b j)")

                def end_fetch(n0, k, stored):
                    if stored is not None:
                        dve.wait_ge(s_st[l][k], stored)
                    for i in range(KG):
                        dve.wait_ge(s_sel, n0 + (i + 1))
                        if not isinstance(n0, int) or n0 + i >= 2:
                            dve.wait_ge(s_row, n0 + (i - 1))
                        prod = sel_ps[(k * KG + i) % 4].rearrange("p (c f) -> p c f", f=ROW)
                        tt(picked[i % 2], prod, onehot_c1[:, i, :].unsqueeze(2).broadcast_to([P, C1, ROW]),
                           ALU.mult).then_inc(s_pick, 1)
                        if i + 4 < KG:
                            ohe(n0, i + 4, (k * KG + i) % 4)
                        dve.wait_ge(s_pick, n0 + (i + 1))
                        dve.reduce_sum(slotg[k][:, PG + i, :], picked[i % 2].rearrange("p c f -> p f c"),
                                       X).then_inc(s_row, 1)

                def blockg(k, j0, n, use, blocks, rows_in=None):
                    own = [0]

                    def chain(ins):
                        own[0] += 1
                        ins.then_inc(s_own, 1)
                        dve.wait_ge(s_own, blocks * STEPS + own[0])

                    rows = slotg[k][:, 0:n, :]
                    logit = rows[:, :, HW - 1:ROW:HW].rearrange("p j h -> p h j")
                    dve.wait_ge(s_g[l][k], use)
                    if rows_in is not None:
                        dve.wait_ge(s_row, rows_in)
                    chain(tt(lg[:, :, 0:n], logit, adf[:, bass.ds(j0, n), :].rearrange("p j h -> p h j"), ALU.add))
                    chain(stt(lg[:, :, 0:n], lg[:, :, 0:n], SLOPES[l], lg[:, :, 0:n], ALU.mult, ALU.max))
                    dve.tensor_copy(reset_b[:, 0:n], reset[:, bass.ds(j0, n)]).then_inc(s_own, 1)
                    own[0] += 1
                    dve.wait_ge(s_own, blocks * STEPS + own[0])
                    for h in range(2):
                        last = dve.tensor_tensor_scan(mx[:, h, 1:n + 1], reset_b[:, 0:n], lg[:, h, 0:n],
                                                      mx[:, h, 0:1], ALU.add, ALU.max)
                    chain(last)
                    tt(ex_in[:, 1, :, 0:n], lg[:, :, 0:n], mx[:, :, 1:n + 1], ALU.subtract)
                    dve.tensor_copy(rows[:, :, HW - 1:ROW:HW].rearrange("p j h -> p h j"), mx[:, :, 1:n + 1])
                    chain(tt(ex_in[:, 0, :, 0:n], mx[:, :, 0:n],
                             reset_b[:, 0:n].unsqueeze(1).broadcast_to([P, 2, n]), ALU.add))
                    tt(ex_in[:, 0, :, 0:n], ex_in[:, 0, :, 0:n], mx[:, :, 1:n + 1], ALU.subtract).then_inc(s_exin, 1)
                    dve.wait_ge(s_ex, blocks + 1)
                    parts = rows.rearrange("p j (h k) -> p j h k", h=2)[:, :, :, 0:HW - 1]
                    weights = ex[:, 1, :, 0:n].rearrange("p h j -> p j h").unsqueeze(3).broadcast_to([P, n, 2, HW - 1])
                    chain(tt(parts, parts, weights, ALU.mult))
                    for h in range(2):
                        for c in range(h * HW, h * HW + HW - 1):
                            last = dve.tensor_tensor_scan(rows[:, :, c], ex[:, 0, h, 0:n], rows[:, :, c],
                                                          sumc[:, c:c + 1], ALU.mult, ALU.add)
                    chain(last)
                    assert own[0] == STEPS
                    dve.tensor_copy(mx[:, :, 0:1], mx[:, :, n:n + 1])
                    dve.tensor_copy(sumc[:, :], rows[:, n - 1, :]).then_inc(s_sum, 1)
                    dve.wait_ge(s_sum, blocks + 1)

                def window(r, k):
                    n1 = r * (2 * KG) + (first + (k + 1) * KG)
                    begin_fetch(r * 2 + (k + 1), n1, k + 1)
                    blockg(k, r * (2 * CB) + k * CB, CB, (r + 1) * (16 * PG), r * 2 + (done + k), n1)
                    end_fetch(n1, 1 - k, (r + k) * 16 if not (isinstance(r, int) and r + k == 0) else None)

                begin_fetch(0, first, 0)
                end_fetch(first, 0, None)
                window(0, 0)
                window(0, 1)
                with dve.Fori(1, ROUNDS - 1) as r:
                    for k in range(2):
                        window(r, k)
                window(ROUNDS - 1, 0)
                blockg(1, (NB - 1) * CB, CB, ROUNDS * 16 * PG, done + NB - 1, first + NB * KG)
                blockg(0, NB * CB, TAIL, ROUNDS * 16 * PG + 16 * TAIL, done + NB)

                dve.tensor_copy(mrep[:, :].rearrange("p (h k) -> p h k", h=2),
                                sumc[:, HW - 1:ROW:HW].unsqueeze(2).broadcast_to([P, 2, HW])).then_inc(s_tail, 1)
                dve.wait_ge(s_tailt, l + 2)
                mark(dve.tensor_copy(wm_t[:, :], t_ps[0][0:ROW, P:2 * P]))
                link(dve.tensor_copy(m_t[:, :], t_ps[0][0:ROW, 2 * P:3 * P]))
                link(dve.tensor_tensor_scan(mi_t[:, 1:P + 1], wm_t[:, :], m_t[:, :], 0.0, ALU.add, ALU.max))
                mark(tt(te_in[:, 0, :], mi_t[:, 0:P], wm_t[:, :], ALU.add))
                link(tt(te_in[:, 1, :], m_t[:, :], mi_t[:, 1:P + 1], ALU.subtract))
                tt(te_in[:, 0, :], te_in[:, 0, :], mi_t[:, 1:P + 1], ALU.subtract).then_inc(s_tein, 1)
                dve.wait_ge(s_te, l + 2)
                link(tt(m_t[:, :], te[:, 1, :], t_ps[0][0:ROW, 0:P], ALU.mult))
                dve.tensor_tensor_scan(si_t[:, 1:P + 1], te[:, 0, :], m_t[:, :], 0.0, ALU.mult, ALU.add).then_inc(s_car, 1)
                dve.wait_ge(s_cart, l + 2)
                dve.wait_ge(s_fixg, 16 * (l + 2))
                mark(dve.tensor_copy(cs[:, :], t_ps[1][:, 0:ROW]))
                link(ts(cm[:, :], t_ps[1][:, 64 + HW - 1:64 + ROW:HW], cmask[:, 0:1], None, ALU.add))
                link(tt(vm[:, :], cm[:, :], fix[:, HW - 1:ROW:HW], ALU.max))
                mark(tt(fe_in[:, 0, :], fix[:, HW - 1:ROW:HW], vm[:, :], ALU.subtract))
                tt(fe_in[:, 1, :], cm[:, :], vm[:, :], ALU.subtract).then_inc(s_fein, 1)
                dve.wait_ge(s_fe, l + 1)
                both = [t[:, :].rearrange("p (h k) -> p h k", h=2) for t in (fix, cs, fo)]
                mark(tt(both[0], both[0], fe[:, 0, :].unsqueeze(2).broadcast_to([P, 2, HW]), ALU.mult))
                link(tt(both[1], both[1], fe[:, 1, :].unsqueeze(2).broadcast_to([P, 2, HW]), ALU.mult))
                tt(both[2], both[0], both[1], ALU.add).then_inc(s_fixv, 1)

            for q in range(len(QUARTERS)):
                finish(2, q)


_INS = ['x', 'src', 'dst', 'edge_attr_32', 'L0_gnn_W1', 'L0_gnn_b1', 'L0_gnn_W2', 'L0_gnn_b2', 'L1_gnn_W1',
        'L1_gnn_att_s1', 'L1_gnn_att_d1', 'L1_gnn_b1', 'L1_gnn_ea1', 'L1_gnn_W2', 'L1_gnn_att_s2',
        'L1_gnn_att_d2', 'L1_gnn_b2', 'L1_gnn_W3', 'L1_gnn_att_s3', 'L1_gnn_att_d3', 'L1_gnn_b3']


def kernel(**inputs):
    import numpy as _np
    import concourse.bacc as _bacc
    from concourse import mybir as _mybir
    from concourse.bass_utils import run_bass_kernel_spmd as _run

    nc = _bacc.Bacc("TRN2", target_bir_lowering=False, num_devices=1)
    arrays, a = {}, {}
    for name in _INS:
        v = _np.ascontiguousarray(inputs[name])
        arrays[f"in_{name}"] = v
        a[name] = nc.dram_tensor(f"in_{name}", v.shape, _mybir.dt.from_np(v.dtype), kind="ExternalInput").ap()
    out = nc.dram_tensor("out_0", a['x'].shape, _mybir.dt.float32, kind="ExternalOutput").ap()
    gat = [tuple(a[f'L1_gnn_{n}{i}'] for n in ('W', 'att_s', 'att_d', 'b')) for i in (1, 2, 3)]
    gnn_program(nc, a['x'], a['src'], a['dst'], a['edge_attr_32'], a['L0_gnn_W1'], a['L0_gnn_b1'],
                a['L0_gnn_W2'], a['L0_gnn_b2'], gat, a['L1_gnn_ea1'], out)
    r = _run(nc, [arrays], core_ids=[0])
    return r.results[0]["out_0"]
```

```python
import concourse.bass as bass
from concourse import mybir
from contextlib import ExitStack

F32 = mybir.dt.float32
BF16 = mybir.dt.bfloat16
F16 = mybir.dt.float16
F32R = mybir.dt.float32r
I32 = mybir.dt.int32
ALU = mybir.AluOpType
ACT = mybir.ActivationFunctionType
X = mybir.AxisListType.X

P = 128
LOW = -3.0e38
ROUND = 12582912.0


def gnn_program(nc, x, src, dst, edge, w1, b1, w2, b2, gat, ea1, out):
    N, D = x.shape
    E = src.shape[0]
    HID = w1.shape[1]
    COLS = -(-E // P)
    EP = P * COLS
    REAL = E - (P - 1) * COLS
    NCOL = -(-N // P)
    NP = P * NCOL
    NREAL = N - (P - 1) * NCOL
    CB = 64
    NB = COLS // CB
    TAIL = COLS - NB * CB
    ROUNDS = NB // 2
    assert NB == 2 * ROUNDS and 0 < TAIL and REAL > (NB - 1) * CB and REAL < NB * CB
    assert 0 < NREAL < NCOL and EP + NP < 1 << 24
    GW = 4
    GB = CB // GW
    GT = -(-TAIL // GW)
    HW = 18
    ROW = 2 * HW
    KD = ROW + 2
    KG = 15
    PG = CB - KG
    C1 = 14
    C2 = NCOL // C1
    FG = 2 * (HW - 1)
    RE, RT, RS = 4, 2, 4
    assert NCOL == C1 * C2 and C1 * FG <= 512 and C2 * P <= 1024 and KG >= RS

    def before_reuse(i, n0, ring):
        if i < ring:
            if isinstance(n0, int) and n0 == 0:
                return None
            last = i + ring * ((KG - 1 - i) // ring)
            return n0 - (KG - 1 - last)
        return n0 + (i - ring + 1)

    OH = 16
    OHN = COLS // OH
    OHT = COLS - OHN * OH
    NQ = -(-NCOL // 4)
    QUARTERS = [(0, 28), (28, 56), (56, 84), (84, NCOL)]
    EARLY = 14
    ZW = 586
    assert EARLY % 2 == 0 and all(c0 % 4 == 0 for c0, _ in QUARTERS)
    assert COLS % 11 == 0 and 2 * COLS == 11 * ZW
    LOADS = 7 + 3 * 6
    SLOPES = [0.01, 0.2, 0.2]

    xd_d = nc.dram_tensor("xd_d", (EP + NP, D), F32, kind="Internal").ap()
    xs_d = nc.dram_tensor("xs_d", (EP, D), F32, kind="Internal").ap()
    ad_d = nc.dram_tensor("ad_d", (EP + NP, 2), F32, kind="Internal").ap()
    scan0_d = nc.dram_tensor("scan0_d", (EP, D), F32, kind="Internal").ap()
    scan_d = nc.dram_tensor("scan_d", (EP, ROW), F32, kind="Internal").ap()
    table_d = nc.dram_tensor("table_d", (NP, ROW), F32, kind="Internal").ap()
    adn_d = nc.dram_tensor("adn_d", (NP, 2), F32, kind="Internal").ap()
    xd_v = xd_d[0:EP, :].rearrange("(p j) f -> p j f", p=P)
    ad_v = ad_d[0:EP, :].rearrange("(p j) h -> p j h", p=P)
    recs_d = [nc.dram_tensor(f"recs{i}_d", (EP, 3), F32, kind="Internal").ap() for i in range(3)]
    edge_s = nc.dram_tensor("edge_s", (EP, D), F32, kind="Internal").ap()
    xs_v = xs_d.rearrange("(p j) f -> p j f", p=P)
    scan0_v = scan0_d.rearrange("(p j) f -> p j f", p=P)
    scan_v = scan_d.rearrange("(p j) f -> p j f", p=P)

    ctx = ExitStack()
    with ctx:
        def sb(name, shape, dt=F32):
            return ctx.enter_context(nc.sbuf_tensor(name, shape, dt))

        def sem(name):
            return ctx.enter_context(nc.semaphore(name))

        src_i = sb("src_i", [P, COLS], I32)
        def over(name, tensor_at, shape, dt):
            return nc.alloc_sbuf_tensor_at(name, shape, dt, offset=tensor_at)

        dst_at = -(-nc.sbuf_base // 32) * 32
        dst_f = sb("dst_f", [P, COLS])
        onehot_e = [dst_f[:, i * C2 * P // 2:(i + 1) * C2 * P // 2].bitcast(BF16) for i in range(RE - 1)]
        onehot_e.append(sb("onehot_e3", [P, C2 * P], BF16)[:, :])
        oht = over("onehot_t", dst_at + (RE - 1) * C2 * P * 2, [P, RT, C2 * P], F32R)
        onehot_t = [oht[:, i, :] for i in range(RT)]
        assert (RE - 1) * C2 * P * 2 + RT * C2 * P * 4 <= COLS * 4
        keys = sb("keys", [P, NB, KG], F16)
        c1s = sb("c1s", [P, NB, KG], F16)
        key_b = sb("key_b", [P, 2, KG])
        iota_key = sb("iota_key", [P, C2 * P], F16)
        iota_c1 = sb("iota_c1", [P, C1], F16)
        ident_b = sb("ident_b", [P, P], BF16)
        index = sb("index", [P, 2, CB], I32)
        same = sb("same", [P, COLS])
        reset = sb("reset", [P, COLS])
        adf = sb("adf", [P, COLS, 2])
        hi_f = adf[:, :, :].rearrange("p j h -> p (j h)")[:, 0:COLS]
        lo_f = adf[:, :, :].rearrange("p j h -> p (j h)")[:, COLS:2 * COLS]
        ring0_at = -(-nc.sbuf_base // 32) * 32
        ring0 = sb("ring0", [P, 2 * 3 * CB * D])
        slot0 = [ring0[:, k * 3 * CB * D:(k + 1) * 3 * CB * D].rearrange("p (j f) -> p j f", f=3 * D)
                 for k in range(2)]
        work = ring0[:, 0:4 * NQ * D].rearrange("p (c f) -> p c f", f=D)
        work2 = ring0[:, 4 * NQ * D:8 * NQ * D].rearrange("p (c f) -> p c f", f=D)
        tab = ring0[:, 2 * NCOL * FG:2 * NCOL * FG + 4 * NQ * ROW].rearrange("p (c f) -> p c f", f=ROW)
        assert 8 * NQ * D <= 2 * NCOL * FG and 2 * NCOL * FG + 4 * NQ * ROW <= 6 * CB * D
        parts = over("parts", ring0_at, [P, 2, NCOL * FG], F32R)
        ringg = sb("ringg", [P, 2 * CB * ROW])
        slotg = [ringg[:, k * CB * ROW:(k + 1) * CB * ROW].rearrange("p (j f) -> p j f", f=ROW)
                 for k in range(2)]
        spread = [ringg[:, k * CB * D:(k + 1) * CB * D].rearrange("p (j f) -> p j f", f=D) for k in range(2)]
        zeros = ringg[:, 0:ZW]
        OHB = OH * (P + NCOL)
        onehot = [ringg[:, ZW + k * OHB // 2:ZW + (k + 1) * OHB // 2].bitcast(BF16) for k in range(2)]
        oh_hi = [o[:, 0:OH * P].rearrange("p (j n) -> p j n", n=P) for o in onehot]
        oh_lo = [o[:, OH * P:OHB].rearrange("p (j n) -> p j n", n=NCOL) for o in onehot]
        recs = ring0[:, 0:3 * COLS].rearrange("p (j r) -> p j r", r=3)
        sort_mem = ringg[:, ZW:ZW + 4 * P + 3 * P + D + 8]
        base, cnt = (sort_mem[:, i * 2 * P:(i + 1) * 2 * P].rearrange("p (m d) -> p m d", m=2) for i in range(2))
        oh_s, upper_b, ones_b = (sort_mem[:, (8 + i) * P // 2:(9 + i) * P // 2].bitcast(BF16) for i in range(3))
        places = sort_mem[:, 11 * P // 2:13 * P // 2]
        erow = sort_mem[:, 7 * P:7 * P + D]
        key = sort_mem[:, 7 * P + D:7 * P + D + 8]
        ones_f = sb("ones_f", [P, P])
        rec = sb("rec", [P, 3])
        pos_i = sb("pos_i", [P, 1], I32)
        flag_i = sb("flag_i", [1, 1], I32)
        digits = sb("digits", [P, 2, OH], BF16)
        xt_sb = sb("xt_sb", [P, 2, 512])
        picked = xt_sb[:, :, :].rearrange("p a n -> p (a n)")[:, 0:2 * C1 * FG].rearrange("p (a n) -> p a n", a=2)
        h_sb = sb("h_sb", [2 * HID, 2, 256])
        onehot_c1 = h_sb[:, :, :].rearrange("p a n -> p (a n)")[:, 0:2 * KG * C1].rearrange(
            "p (a i c) -> p a i c", a=2, c=C1)
        iota_ki = xt_sb[:, :, :].rearrange("p a n -> p (a n)").bitcast(I32)[:, 0:C2 * P]
        same_b = sb("same_b", [P, CB])
        reset_b = sb("reset_b", [P, CB])
        fillc = sb("fillc", [P, D])
        maxc = sb("maxc", [P, ROW])
        lg = sb("lg", [P, 2, CB])
        mx = sb("mx", [P, 2, CB + 1])
        ex_in = sb("ex_in", [P, 2, 2, CB])
        ex = sb("ex", [P, 2, 2, CB])
        sumc = sb("sumc", [P, ROW])
        x1 = sb("x1", [P, 4 * NQ, D])
        xn = x1[:, 0:NCOL, :]
        nd_all = sb("nd_all", [P, 2 * CB * D])
        nd = nd_all[:, 0:NCOL * ROW].rearrange("p (c f) -> p c f", f=ROW)
        stage = [nd_all[:, k * CB * D:(k + 1) * CB * D].rearrange("p (j f) -> p j f", f=D) for k in range(2)]
        adt = sb("adt", [P, 4 * NQ, 2])
        deg = sb("deg", [P, NCOL])
        cum = sb("cum", [P, NCOL])
        has = sb("has", [P, NCOL])
        pen = sb("pen", [P, NCOL])
        nt = sb("nt", [P, 4, NCOL])
        rden = sb("rden", [P, NCOL, 2])
        spare_i = sb("spare_i", [P, NCOL], I32)
        spare = sb("spare", [P, NCOL])
        start_i = sb("start_i", [P, NCOL], I32)
        end_i = sb("end_i", [P, NCOL], I32)
        onesn = sb("onesn", [P, NCOL])
        before = sb("before", [P, 1])
        dst0_i = sb("dst0_i", [P, 1], I32)
        prev_i = sb("prev_i", [P, 1], I32)
        prev_f = sb("prev_f", [P, 1])
        cont = sb("cont", [P, 1])
        cmask = sb("cmask", [P, 1])
        wmask = sb("wmask", [P, ROW])
        pt = sb("pt", [P, 4])
        row0_i = sb("row0_i", [P, 1], I32)
        fe_i = sb("fe_i", [P, 1], I32)
        x0 = sb("x0", [P, D])
        a0 = sb("a0", [P, 2])
        tot = sb("tot", [P, 1])
        viol = sb("viol", [P, 1])
        mrep = sb("mrep", [P, ROW])
        wm_t = sb("wm_t", [ROW, P])
        m_t = sb("m_t", [ROW, P])
        mi_t = sb("mi_t", [ROW, P + 1])
        si_t = sb("si_t", [ROW, P + 1])
        te_in = sb("te_in", [ROW, 2, P])
        te = sb("te", [ROW, 2, P])
        fix = sb("fix", [P, ROW])
        fo = sb("fo", [P, ROW])
        cs = sb("cs", [P, ROW])
        cm = sb("cm", [P, 2])
        vm = sb("vm", [P, 2])
        fe_in = sb("fe_in", [P, 2, 2])
        fe = sb("fe", [P, 2, 2])
        ident = sb("ident", [P, P])
        upper = sb("upper", [P, P])
        iota_i = sb("iota_i", [P, P], I32)
        iota_b = sb("iota_b", [P, P], BF16)
        w1_sb = sb("w1_sb", [3 * D, HID])
        w2_sb = sb("w2_sb", [2 * HID, 2 * D])
        b1_sb = sb("b1_sb", [2 * HID, 1])
        b2_sb = sb("b2_sb", [P, D])
        bg_sb = sb("bg_sb", [P, 3, D])
        gw_sb = sb("gw_sb", [D, 3, D])
        pick = sb("pick", [D, 3, KD])
        wc_sb = sb("wc_sb", [D, 3, KD])
        wd_sb = sb("wd_sb", [P, 3, 4 * KD])
        ea_sb = sb("ea_sb", [P, 1])
        sc = sb("sc", [P, 4])
        sc_out = sb("sc_out", [P, 1])

        psum = ctx.enter_context(nc.psum_tensor("psum", [P, 8 * 512], F32))
        t_ps = [psum[:, k * 512:(k + 1) * 512] for k in range(2)]
        h_ps = [psum[:, (2 + k) * 512:(3 + k) * 512] for k in range(2)]
        v_ps = psum[:, 4 * 512:8 * 512].rearrange("p (j f) -> p j f", f=D)
        count_ps = psum[:, 4 * 512:4 * 512 + NCOL]
        before_ps = psum[:, 5 * 512:5 * 512 + 1]
        sel_ps = [psum[:, (2 + i) * 512:(2 + i) * 512 + C1 * FG] for i in range(RS)]
        oht_ps = [psum[:, (6 + i) * 512:(7 + i) * 512].bitcast(BF16)[:, 0:C2 * P] for i in range(2)]
        flag_ps = psum[0:1, 5 * 512 + 8:5 * 512 + 9]
        total_ps = psum[:, 0:2 * P]
        rank_ps = psum[:, 512:512 + P]
        add_ps = psum[:, 1024:1024 + P]
        wc_ps = psum[0:D, 6 * 512:6 * 512 + 3 * KD].rearrange("p (l k) -> p l k", l=3)

        s_src = sem("s_src")
        s_dst = sem("s_dst")
        s_prev = sem("s_prev")
        s_viol = sem("s_viol")
        s_violp = sem("s_violp")
        s_flag = sem("s_flag")
        s_srt = sem("s_srt")
        s_dig = sem("s_dig")
        s_srp = [sem(f"s_srp{m}") for m in range(2)]
        s_recs = sem("s_recs")
        s_recd = sem("s_recd")
        s_cntd = sem("s_cntd")
        s_totd = sem("s_totd")
        s_rec = [sem(f"s_rec{m}") for m in range(3)]
        s_ohs = sem("s_ohs")
        s_rank = sem("s_rank")
        s_pos = sem("s_pos")
        s_put = [sem(f"s_put{m}") for m in range(2)]
        s_eid = sem("s_eid")
        s_erow = sem("s_erow")
        s_erowd = sem("s_erowd")
        s_back = sem("s_back")
        s_sorted = sem("s_sorted")
        s_sbegun = sem("s_sbegun")
        s_past = sem("s_past")
        s_x = sem("s_x")
        s_w = sem("s_w")
        s_pads = sem("s_pads")
        s_zs = sem("s_zs")
        s_zero = sem("s_zero")
        s_const = sem("s_const")
        s_pool = sem("s_pool")
        s_index = sem("s_index")
        s_begun = sem("s_begun")
        s_wc = sem("s_wc")
        s_wcs = sem("s_wcs")
        s_wd = sem("s_wd")
        s_wz = sem("s_wz")
        s_v = sem("s_v")
        s_oh = sem("s_oh")
        s_ohd = sem("s_ohd")
        s_fs = sem("s_fs")
        s_ms = sem("s_ms")
        s_own = sem("s_own")
        s_cnt = sem("s_cnt")
        s_tot = sem("s_tot")
        s_bef = sem("s_bef")
        s_idx = sem("s_idx")
        s_xs = [sem(f"s_xs{k}") for k in range(2)]
        s_xst = [sem(f"s_xst{k}") for k in range(2)]
        s_xl = [sem(f"s_xl{k}") for k in range(2)]
        s_xd = [sem(f"s_xd{k}") for k in range(2)]
        s_ed = [sem(f"s_ed{k}") for k in range(2)]
        s_st0 = [sem(f"s_st_max{k}") for k in range(2)]
        s_xscat = sem("s_xscat")
        s_x0 = sem("s_x0")
        s_xrow = sem("s_xrow")
        s_fill = sem("s_fill")
        s_t = sem("s_t")
        s_tc = sem("s_tc")
        s_h = sem("s_h")
        s_hr = sem("s_hr")
        s_vp = sem("s_vp")
        s_max = sem("s_max")
        s_g = [[sem(f"s_g{l}_{k}") for k in range(2)] for l in range(3)]
        s_st = [[sem(f"s_st{l}_{k}") for k in range(2)] for l in range(3)]
        s_exin = sem("s_exin")
        s_ex = sem("s_ex")
        s_sum = sem("s_sum")
        s_keys = sem("s_keys")
        s_ohe = sem("s_ohe")
        s_oht = sem("s_oht")
        s_ohc = sem("s_ohc")
        s_sel = sem("s_sel")
        s_pick = sem("s_pick")
        s_row = sem("s_row")
        s_tail = sem("s_tail")
        s_tailt = sem("s_tailt")
        s_tein = sem("s_tein")
        s_te = sem("s_te")
        s_car = sem("s_car")
        s_cart = sem("s_cart")
        s_fein = sem("s_fein")
        s_fe = sem("s_fe")
        s_fixg = sem("s_fixg")
        s_fixv = sem("s_fixv")
        s_fixs = sem("s_fixs")
        s_nd = [sem(f"s_nd{q}") for q in range(len(QUARTERS))]
        s_ain = sem("s_ain")
        s_aout = sem("s_aout")
        s_node = sem("s_node")
        s_nt = sem("s_nt")
        s_ntc = sem("s_ntc")
        s_np = sem("s_np")
        s_npc = sem("s_npc")
        s_tab = sem("s_tab")
        s_tabd = sem("s_tabd")
        s_adnd = sem("s_adnd")
        s_ascat = sem("s_ascat")
        s_a0 = sem("s_a0")
        s_arow = sem("s_arow")
        s_adf = sem("s_adf")
        s_fin = sem("s_fin")
        s_out = sem("s_out")

        block = ctx.enter_context(nc.Block())

        def split_rows(ap, per, real):
            whole = ap[0:(P - 1) * per].rearrange("(p j) -> p j", j=per)
            last = ap[(P - 1) * per:(P - 1) * per + real].rearrange("(p j) -> p j", p=1)
            return ((slice(0, 112), per, whole[0:112, :]), (slice(112, P - 1), per, whole[112:P - 1, :]),
                    (slice(P - 1, P), real, last))

        @block.sync
        def _(sp):
            sp.wait_ge(s_pads, 1)
            for rows, n, part in split_rows(dst, COLS, REAL):
                sp.dma_start(hi_f.bitcast(I32)[rows, 0:n], part).then_inc(s_dst, 16)
            for rows, n, part in split_rows(src, COLS, REAL):
                sp.dma_start(src_i[rows, 0:n], part).then_inc(s_src, 16)
            sp.dma_start(prev_i[1:P, :], dst[COLS - 1:E:COLS].unsqueeze(1),
                         allow_slow_non_contiguous=True).then_inc(s_prev, 16)
            xn_flat = xn.rearrange("p c f -> p (c f)")
            for rows, n, part in split_rows(x.rearrange("n f -> (n f)"), NCOL * D, NREAL * D):
                sp.dma_start(xn_flat[rows, 0:n], part).then_inc(s_x, 16)
            sp.wait_ge(s_flag, 1)
            unsorted = sp.value_load(flag_i[0:1, 0:1], min_val=0, max_val=1)
            with sp.If(unsorted > 0):
                sp.wait_ge(s_recs, 2)
                sp.dma_start(recs_d[0].rearrange("(p j) r -> p j r", p=P), recs).then_inc(s_recd, 16)
                sp.wait_ge(s_recd, 16)
                for m in range(2):
                    with sp.Fori(0, COLS) as t:
                        sp.dma_start(rec[:, :], recs_d[m][bass.ds(t * P, P), :]).then_inc(s_rec[m], 16)
                        sp.wait_ge(s_put[m], (t + 1) * 16)
                        sp.sem_inc(s_past, 1)
                with sp.Fori(0, COLS) as t:
                    sp.dma_start(rec[:, :], recs_d[2][bass.ds(t * P, P), :]).then_inc(s_rec[2], 16)
                    sp.wait_ge(s_erow, (t + 1) * 16)
                    sp.dma_start(edge_s[bass.ds(t * P, P), :], erow).then_inc(s_erowd, 16)
                    sp.wait_ge(s_erowd, (t + 1) * 16)
                    sp.sem_inc(s_past, 1)
                sp.dma_start(recs, recs_d[2].rearrange("(p j) r -> p j r", p=P)).then_inc(s_back, 16)
                sp.dma_start(prev_f[1:P, :], recs_d[2][COLS - 1:EP - 1:COLS, 0:1],
                             allow_slow_non_contiguous=True).then_inc(s_back, 16)
                sp.wait_ge(s_sorted, 1)

            sp.wait_ge(s_wcs, 1)
            sp.wait_ge(s_wz, 1)
            for l in range(3):
                for q in range(4):
                    sp.dma_start(wd_sb[q * D:(q + 1) * D, l, q * KD:(q + 1) * KD], wc_sb[:, l, :]).then_inc(s_wd, 16)

            def from_edges(load):
                with sp.If(unsorted > 0):
                    load(edge_s)
                with sp.If(unsorted < 1):
                    load(edge)

            def load_edges(b, k, j0):
                from_edges(lambda table: load_parts(table, b, k, j0))

            def load_parts(edge, b, k, j0):
                n = CB if b < NB else TAIL
                for rows in (slice(0, 112), slice(112, P - 1)):
                    flat = edge[0:(P - 1) * COLS, :].rearrange("(p j) f -> p j f", j=COLS)
                    sp.dma_start(slot0[k][rows, 0:n, 2 * D:3 * D], flat[rows, j0:j0 + n, :]).then_inc(s_ed[k], 16)
                real = min(max(REAL - j0, 0), n)
                if real:
                    first = (P - 1) * COLS + j0
                    sp.dma_start(slot0[k][P - 1:P, 0:real, 2 * D:3 * D],
                                 edge[first:first + real, :].rearrange("(p j) f -> p j f", p=1)).then_inc(s_ed[k], 16)

            def load_spread(k, j0, n):
                sp.dma_start(spread[k][:, 0:n, :], xd_v[:, bass.ds(j0, n), :]).then_inc(s_xd[k], 16)

            def load_sources(k, j0, n, stored):
                sp.wait_ge(s_xst[k], stored)
                sp.dma_start(slot0[k][:, 0:n, 0:D], xs_v[:, bass.ds(j0, n), :]).then_inc(s_xl[k], 16)

            def whole_columns(table):
                return bass.AP(tensor=table.tensor, offset=0, ap=[[COLS * D, P], [D, (NB - 1) * CB], [1, D]])

            def load_whole(k, j0):
                from_edges(lambda table: sp.dma_start(slot0[k][:, :, 2 * D:3 * D], whole_columns(table)[:, bass.ds(j0, CB), :])
                           .then_inc(s_ed[k], 16))

            def store_max(k, j0, n, done):
                sp.wait_ge(s_max, done)
                sp.dma_start(scan0_v[:, bass.ds(j0, n), :], spread[k][:, 0:n, :]).then_inc(s_st0[k], 16)

            load_whole(0, 0)
            load_whole(1, CB)
            sp.wait_ge(s_xscat, 16 * NCOL)
            sp.wait_ge(s_x0, 16)
            sp.dma_start(xd_v[:, 0, :], x0[:, :]).then_inc(s_xrow, 16)
            sp.wait_ge(s_xrow, 16)
            for k in range(2):
                load_spread(k, k * CB, CB)
                load_sources(k, k * CB, CB, 16)
            store_max(0, 0, CB, 1)
            with sp.Fori(1, ROUNDS - 1) as r:
                for k in range(2):
                    sp.wait_ge(s_t, (r * 2 + (k - 1)) * GB)
                    sp.sem_inc(s_past, 1)
                    load_whole(k, r * (2 * CB) + k * CB)
                    sp.wait_ge(s_st0[k], r * 16)
                    load_spread(k, r * (2 * CB) + k * CB, CB)
                    load_sources(k, r * (2 * CB) + k * CB, CB, (r + 1) * 16)
                    store_max(1 - k, r * (2 * CB) + (k - 1) * CB, CB, r * 2 + k)
            for b in range(NB - 2, NB + 1):
                k = b % 2
                n = CB if b < NB else TAIL
                sp.wait_ge(s_t, (b - 1) * GB)
                if b == NB - 2:
                    load_whole(k, b * CB)
                else:
                    load_edges(b, k, b * CB)
                sp.wait_ge(s_st0[k], b // 2 * 16)
                load_spread(k, b * CB, n)
                load_sources(k, b * CB, n, (b // 2 + 1) * 16)
                store_max(1 - k, (b - 1) * CB, CB, b)
            store_max(NB % 2, NB * CB, TAIL, NB + 1)

            for l in range(3):
                for q, (c0, c1) in enumerate(QUARTERS):
                    sp.wait_ge(s_tab, l * len(QUARTERS) + q + 1)
                    sp.dma_start(table_d.rearrange("(p c) f -> p c f", p=P)[:, c0:c1, :],
                                 tab[:, c0:c1, :]).then_inc(s_tabd, 16)
                    sp.dma_start(adn_d.rearrange("(p c) f -> p c f", p=P)[:, c0:c1, :],
                                 adt[:, c0:c1, :]).then_inc(s_adnd, 16)
                sp.wait_ge(s_ascat, 16 * NCOL * (l + 1))
                sp.wait_ge(s_a0, 16 * (l + 1))
                sp.dma_start(ad_v[:, 0, :], a0[:, :]).then_inc(s_arow, 16)
                sp.wait_ge(s_arow, 16 * (l + 1))
                sp.dma_start(adf[:, :, :], ad_v).then_inc(s_adf, 16)

                done = l * (NB + 1)

                def store_sum(k, j0, n, blocks):
                    sp.wait_ge(s_sum, blocks)
                    sp.dma_start(scan_v[:, bass.ds(j0, n), :], slotg[k][:, 0:n, :]).then_inc(s_st[l][k], 16)

                with sp.Fori(0, ROUNDS) as r:
                    for k in range(2):
                        store_sum(k, r * (2 * CB) + k * CB, CB, r * 2 + (done + k + 1))
                store_sum(NB % 2, NB * CB, TAIL, done + NB + 1)
            sp.wait_ge(s_fin, len(QUARTERS))
            o_flat = work2[:, 0:NCOL, :].rearrange("p c f -> p (c f)")
            for rows, n, part in split_rows(out.rearrange("n f -> (n f)"), NCOL * D, NREAL * D):
                sp.dma_start(part, o_flat[rows, 0:n]).then_inc(s_out, 16)
            sp.wait_ge(s_out, 48)

        @block.gpsimd
        def _(pool):
            steps = [0]

            def step(ins):
                steps[0] += 1
                ins.then_inc(s_pool, 1)
                pool.wait_ge(s_pool, steps[0])

            step(pool.memset(ident[:, :], 0.0))
            step(pool.affine_select(out=ident[:, :], in_=ident[:, :], compare_op=ALU.not_equal, fill=1.0,
                                    base=0, pattern=[[-1, P]], channel_multiplier=1))
            step(pool.memset(upper[:, :], 1.0))
            step(pool.affine_select(out=upper[:, :], in_=upper[:, :], compare_op=ALU.is_gt, fill=0.0,
                                    base=0, pattern=[[1, P]], channel_multiplier=-1))
            step(pool.iota(iota_i[:, :], pattern=[[1, P]], base=0, channel_multiplier=0))
            step(pool.iota(spare_i[:, :], pattern=[[1, NCOL]], base=EP, channel_multiplier=NCOL))
            step(pool.iota(iota_ki, pattern=[[1, C2 * P]], base=0, channel_multiplier=0))
            step(pool.iota(row0_i[:, :], pattern=[[1, 1]], base=0, channel_multiplier=COLS))
            step(pool.memset(pick[:, :, :], 0.0))
            step(pool.memset(w2_sb[:, :], 0.0))
            for l in range(3):
                for h in range(2):
                    part = pick[:, l, h * HW + 1:h * HW + 17]
                    step(pool.affine_select(out=part, in_=part, compare_op=ALU.not_equal, fill=1.0,
                                            base=-16 * h, pattern=[[-1, 16]], channel_multiplier=1))
            pool.memset(wd_sb[:, :, :], 0.0).then_inc(s_wz, 1)
            pool.engine_nop().then_inc(s_const, 1)

            step(pool.memset(ones_f[:, :], 1.0))
            pool.wait_ge(s_flag, 1)
            unsorted = pool.value_load(flag_i[0:1, 0:1], min_val=0, max_val=1)
            with pool.If(unsorted > 0):
                pool.iota(lo_f.bitcast(I32), pattern=[[1, COLS]], base=0, channel_multiplier=COLS).then_inc(s_recs, 1)
                for m in range(2):
                    with pool.Fori(0, COLS) as t:
                        pool.wait_ge(s_pos, t + (m * COLS + 1))
                        pool.sem_inc(s_sbegun, 1)
                        pool.indirect_dma_start(
                            out=recs_d[m + 1], out_offset=bass.IndirectOffsetOnAxis(ap=pos_i[:, :], axis=0),
                            in_=rec[:, :], in_offset=None).then_inc(s_put[m], 16)
                with pool.Fori(0, COLS) as t:
                    pool.wait_ge(s_eid, t + 1)
                    pool.sem_inc(s_sbegun, 1)
                    pool.indirect_dma_start(
                        out=erow, out_offset=None, in_=edge,
                        in_offset=bass.IndirectOffsetOnAxis(ap=pos_i[:, :], axis=0)).then_inc(s_erow, 16)
                pool.wait_ge(s_sorted, 1)

            def gather(table, k, j0, n, blocks, row, signal, meanwhile=None):
                pool.tensor_copy(index[:, k, 0:n], src_i[:, bass.ds(j0, n)]).then_inc(s_index, 1)
                pool.wait_ge(s_index, blocks + 1)
                pool.sem_inc(s_begun, 1)
                for j in range(n):
                    if j == 4 and meanwhile is not None:
                        meanwhile()
                    gather_one(row(j), table, index[:, k, j:j + 1], signal)

            def gather_one(rows, table, index, signal):
                pool.indirect_dma_start(out=rows, out_offset=None, in_=table,
                                        in_offset=bass.IndirectOffsetOnAxis(ap=index, axis=0)).then_inc(signal, 16)

            def scatter_one(table, index, rows, signal):
                pool.indirect_dma_start(out=table, out_offset=bass.IndirectOffsetOnAxis(ap=index, axis=0),
                                        in_=rows, in_offset=None).then_inc(signal, 16)

            def join_and_fetch(n_fix, scanned, width):
                gather_one(fix[:, 0:width], scanned, fe_i[:, :], s_fixg)
                pool.wait_ge(s_fixv, n_fix)
                scatter_one(scanned, fe_i[:, :], fo[:, 0:width], s_fixs)
                pool.wait_ge(s_fixs, 16 * n_fix)
                for q, (c0, c1) in enumerate(QUARTERS):
                    for c in range(c0, c1):
                        gather_one(nd[:, c, 0:width], scanned, end_i[:, c:c + 1], s_nd[q])

            def put_away(k, j0, n, gathered):
                pool.wait_ge(s_xs[k], gathered)
                pool.sem_inc(s_begun, 1)
                pool.dma_start(xs_v[:, bass.ds(j0, n), :], stage[k][:, 0:n, :]).then_inc(s_xst[k], 16)

            def fetch(k, j0, n, blocks, gathered, stored):
                if stored is not None:
                    pool.wait_ge(s_xst[k], stored)
                gather(x, k, j0, n, blocks, lambda j: stage[k][:, j, :], s_xs[k],
                       None if gathered is None else lambda: put_away(1 - k, j0 - CB, CB, gathered))

            pool.wait_ge(s_src, 48)
            fetch(0, 0, CB, 0, None, None)
            fetch(1, CB, CB, 1, None, None)
            put_away(0, 0, CB, 16 * CB)

            def rounds(first, last):
                with pool.Fori(first, last) as r:
                    fetch(0, r * (2 * CB), CB, r * 2, r * (16 * CB), r * 16)
                    fetch(1, r * (2 * CB) + CB, CB, r * 2 + 1, (r + 1) * (16 * CB), r * 16)

            rounds(1, EARLY // 2)
            pool.wait_ge(s_x, 48)
            pool.wait_ge(s_idx, 1)
            pool.wait_ge(s_zero, 32)
            for c in range(NCOL):
                scatter_one(xd_d, start_i[:, c:c + 1], xn[:, c, :], s_xscat)
            gather_one(x0[:, :], x, dst0_i[:, :], s_x0)
            rounds(EARLY // 2, ROUNDS)
            fetch(0, NB * CB, TAIL, NB, ROUNDS * 16 * CB, ROUNDS * 16)
            put_away(0, NB * CB, TAIL, ROUNDS * 16 * CB + 16 * TAIL)
            pool.wait_ge(s_st0[0], 16 * (ROUNDS + 1))
            pool.wait_ge(s_st0[1], 16 * ROUNDS)
            join_and_fetch(1, scan0_d, D)

            for l in range(3):
                done = (l + 1) * (NB + 1)
                for q, (c0, c1) in enumerate(QUARTERS):
                    pool.wait_ge(s_tab, l * len(QUARTERS) + q + 1)
                    for c in range(c0, c1):
                        scatter_one(ad_d, start_i[:, c:c + 1], adt[:, c, :], s_ascat)
                pool.wait_ge(s_adnd, 16 * len(QUARTERS) * (l + 1))
                gather_one(a0[:, :], adn_d, dst0_i[:, :], s_a0)
                pool.wait_ge(s_tabd, 16 * len(QUARTERS) * (l + 1))
                for k in range(2):
                    gather(table_d, k, k * CB, PG, done + k, lambda j: slotg[k][:, j, :], s_g[l][k])
                with pool.Fori(1, ROUNDS) as r:
                    for k in range(2):
                        pool.wait_ge(s_st[l][k], r * 16)
                        gather(table_d, k, r * (2 * CB) + k * CB, PG, r * 2 + (done + k),
                               lambda j: slotg[k][:, j, :], s_g[l][k])
                pool.wait_ge(s_st[l][0], 16 * ROUNDS)
                gather(table_d, 0, NB * CB, TAIL, done + NB, lambda j: slotg[0][:, j, :], s_g[l][0])
                pool.wait_ge(s_st[l][0], 16 * (ROUNDS + 1))
                pool.wait_ge(s_st[l][1], 16 * ROUNDS)
                join_and_fetch(l + 2, scan_d, ROW)

        @block.tensor
        def _(pe):
            pe.wait_ge(s_const, 1)
            pe.wait_ge(s_viol, 1)
            pe.matmul(flag_ps, viol[:, :], onesn[:, 0:1], start=True, stop=True).then_inc(s_violp, 1)
            pe.wait_ge(s_flag, 1)
            unsorted = pe.value_load(flag_i[0:1, 0:1], min_val=0, max_val=1)
            with pe.If(unsorted > 0):
                pe.wait_ge(s_cntd, 1)
                pe.matmul(total_ps, ones_f[:, :], cnt, start=True, stop=True).then_inc(s_totd, 1)
                for m in range(2):
                    with pe.Fori(0, COLS) as t:
                        pe.wait_ge(s_ohs, t + (m * COLS + 1))
                        pe.matmul(rank_ps, upper_b, oh_s, start=True, stop=True)
                        pe.matmul(add_ps, ones_b, oh_s, start=True, stop=True).then_inc(s_rank, 1)
            pe.wait_ge(s_w, 16 * LOADS)
            for l in range(3):
                last = pe.matmul(wc_ps[:, l, :], gw_sb[:, l, :], pick[:, l, :], start=True, stop=True)
            last.then_inc(s_wc, 1)
            def count(m, k, n, first=False, final=False):
                pe.wait_ge(s_oh, m)
                for j in range(n):
                    last = pe.matmul(count_ps, oh_hi[k][:, j, :], oh_lo[k][:, j, :],
                                     start=first and j == 0, stop=final and j == n - 1, skip_group_check=True)
                last.then_inc(s_cnt, 1)

            count(1, 0, OH, first=True)
            count(2, 1, OH)
            with pe.Fori(1, OHN // 2) as r:
                for k in range(2):
                    count(r * 2 + (k + 1), k, OH)
            for m in range(OHN - OHN % 2, OHN):
                count(m + 1, m % 2, OH)
            count(OHN + 1, OHN % 2, OHT, final=True)
            pe.wait_ge(s_tot, 1)
            pe.matmul(before_ps, upper[:, :], tot[:, :], start=True, stop=True).then_inc(s_bef, 1)

            def block0(k, use, base, blocks, n, attrs=None):
                groups = -(-n // GW)
                pe.wait_ge(s_xl[k], use)
                pe.wait_ge(s_ed[k], use if attrs is None else attrs)
                pe.wait_ge(s_fill, blocks + 1)
                for i in range(groups + 2):
                    if i < groups:
                        if base is not None:
                            pe.wait_ge(s_tc, base + (i - 1))
                        elif i >= 2:
                            pe.wait_ge(s_tc, i - 1)
                        for q, j in enumerate((0, 2, 1, 3)):
                            last = pe.transpose(t_ps[i % 2][0:3 * D, q * P:(q + 1) * P],
                                                slot0[k][:, GW * i + j, :], ident[:, :])
                        last.then_inc(s_t, 1)
                    if 1 <= i <= groups:
                        g = i - 1
                        pe.wait_ge(s_tc, (0 if base is None else base) + (g + 1))
                        if base is not None:
                            pe.wait_ge(s_hr, base + (g - 1))
                        elif g >= 2:
                            pe.wait_ge(s_hr, g - 1)
                        for h in range(2):
                            last = pe.matmul(h_ps[g % 2][h * HID:(h + 1) * HID, 0:2 * P], w1_sb[:, :],
                                             xt_sb[0:3 * D, g % 2, 2 * h * P:2 * (h + 1) * P], start=True, stop=True)
                        last.then_inc(s_h, 1)
                    if i >= 2:
                        g = i - 2
                        pe.wait_ge(s_hr, (0 if base is None else base) + (g + 1))
                        if g == 0 and base is not None:
                            pe.wait_ge(s_max, blocks)
                        for q in range(2):
                            j = GW * g + 2 * q
                            last = pe.matmul(v_ps[:, j:j + 2, :], h_sb[:, g % 2, q * P:(q + 1) * P], w2_sb[:, :],
                                             start=True, stop=True)
                        last.then_inc(s_vp, 1)

            block0(0, 16, None, 0, CB)
            block0(1, 16, GB, 1, CB)
            with pe.Fori(1, ROUNDS - 1) as r:
                for k in range(2):
                    block0(k, (r + 1) * 16, r * (2 * GB) + k * GB, r * 2 + k, CB)
            block0(0, ROUNDS * 16, (NB - 2) * GB, NB - 2, CB)
            block0(1, ROUNDS * 16, (NB - 1) * GB, NB - 1, CB, (ROUNDS - 1) * 16 + 48)
            block0(0, (ROUNDS + 1) * 16, NB * GB, NB, TAIL, ROUNDS * 16 + 32)

            def tails(n):
                pe.wait_ge(s_tail, n)
                pe.transpose(t_ps[0][0:ROW, 0:P], (maxc if n == 1 else sumc)[:, :], ident[:, :])
                last = pe.transpose(t_ps[0][0:ROW, P:2 * P], wmask[:, :], ident[:, :])
                if n > 1:
                    last = pe.transpose(t_ps[0][0:ROW, 2 * P:3 * P], mrep[:, :], ident[:, :])
                last.then_inc(s_tailt, 1)
                pe.wait_ge(s_car, n)
                last = pe.transpose(t_ps[1][:, 0:ROW], si_t[:, 0:P], ident[0:ROW, 0:ROW])
                if n > 1:
                    last = pe.transpose(t_ps[1][:, 64:64 + ROW], mi_t[:, 0:P], ident[0:ROW, 0:ROW])
                last.then_inc(s_cart, 1)

            def table(l, q):
                feats = x1 if l == 0 else work
                pe.wait_ge(s_node, l * len(QUARTERS) + q + 1)
                c0, c1 = QUARTERS[q]
                groups = range(c0 // 4, -(-c1 // 4))
                for i in [*groups, groups[-1] + 1]:
                    n = l * NQ + i
                    if i in groups:
                        if n >= 2:
                            pe.wait_ge(s_ntc, n - 1)
                        pe.transpose(t_ps[n % 2][:, 0:P], feats[:, 4 * i:4 * i + 4, :], ident[:, :]).then_inc(s_nt, 1)
                    if i - 1 in groups:
                        n -= 1
                        pe.wait_ge(s_ntc, n + 1)
                        if n >= 2:
                            pe.wait_ge(s_npc, n - 1)
                        pe.matmul(h_ps[n % 2][:, 0:4 * KD], xt_sb[:, n % 2, 0:P], wd_sb[:, l, :],
                                  start=True, stop=True).then_inc(s_np, 1)

            def fetch_block(n0):
                def transposes(i):
                    pe.wait_ge(s_ohe, n0 + (i + 1))
                    past = before_reuse(i, n0, RT)
                    if past is not None:
                        pe.wait_ge(s_ohc, past)
                    for c in range(C2):
                        last = pe.transpose(oht_ps[i % RT][:, c * P:(c + 1) * P],
                                            onehot_e[i % RE][:, c * P:(c + 1) * P], ident_b[:, :])
                    last.then_inc(s_oht, 1)

                transposes(0)
                for i in range(KG):
                    if i + 1 < KG:
                        transposes(i + 1)
                    pe.wait_ge(s_ohc, n0 + (i + 1))
                    past = before_reuse(i, n0, RS)
                    if past is not None:
                        pe.wait_ge(s_pick, past)
                    for c in range(C2):
                        for part in range(2):
                            last = pe.matmul(sel_ps[i % RS], onehot_t[i % RT][:, c * P:(c + 1) * P],
                                             parts[:, part, c * C1 * FG:(c + 1) * C1 * FG],
                                             start=c + part == 0, stop=c + part == C2)
                    last.then_inc(s_sel, 1)

            tails(1)
            pe.wait_ge(s_wd, 16 * 12)
            for l in range(3):
                for q in range(len(QUARTERS)):
                    table(l, q)
                first = l * NB * KG
                fetch_block(first)
                fetch_block(first + KG)
                with pe.Fori(1, ROUNDS) as r:
                    for k in range(2):
                        fetch_block(r * (2 * KG) + (first + k * KG))
                tails(l + 2)

        @block.scalar
        def _(act):
            act.wait_ge(s_wz, 1)
            act.wait_ge(s_const, 1)
            act.dma_start(w1_sb[:, :], w1).then_inc(s_w, 16)
            for h in range(2):
                half = slice(h * HID, (h + 1) * HID)
                act.dma_start(w2_sb[half, h * D:(h + 1) * D], w2).then_inc(s_w, 16)
                act.dma_start(b1_sb[half, :], b1.unsqueeze(1), allow_slow_non_contiguous=True).then_inc(s_w, 16)
            act.dma_start(b2_sb[:, :], b2.partition_broadcast(P)).then_inc(s_w, 16)
            act.dma_start(ea_sb[:, :], ea1.partition_broadcast(P)).then_inc(s_w, 16)
            for l, (w, att_s, att_d, b) in enumerate(gat):
                act.dma_start(gw_sb[:, l, :], w).then_inc(s_w, 16)
                act.dma_start(bg_sb[:, l, :], b.partition_broadcast(P)).then_inc(s_w, 16)
                heads = att_s.shape[0]
                for h in range(2):
                    rows = slice(16 * h, 16 * h + 16) if heads == 2 else slice(0, D)
                    head = h if heads == 2 else 0
                    for column, att in ((h * HW + HW - 1, att_s), (ROW + h, att_d)):
                        act.dma_start(pick[rows, l, column:column + 1], att[head, :].unsqueeze(1),
                                          allow_slow_non_contiguous=True).then_inc(s_w, 16)
            act.wait_ge(s_zs, 1)
            act.dma_start(xd_v.rearrange("p (a j) f -> p a (j f)", j=11),
                          zeros[:, 0:11 * D].unsqueeze(1).broadcast_to([P, COLS // 11, 11 * D])).then_inc(s_zero, 16)
            act.dma_start(ad_v.rearrange("p j h -> p (j h)").rearrange("p (a z) -> p a z", z=ZW),
                          zeros.unsqueeze(1).broadcast_to([P, 11, ZW])).then_inc(s_zero, 16)

            def block0(base, n):
                groups = -(-n // GW)
                for i in range(groups + 1):
                    if i < groups:
                        act.wait_ge(s_t, (0 if base is None else base) + (i + 1))
                        if base is not None:
                            act.wait_ge(s_h, base + (i - 1))
                        elif i >= 2:
                            act.wait_ge(s_h, i - 1)
                        act.activation(xt_sb[0:3 * D, i % 2, :], t_ps[i % 2][0:3 * D, :], ACT.Copy).then_inc(s_tc, 1)
                    if i >= 1:
                        g = i - 1
                        act.wait_ge(s_h, (0 if base is None else base) + (g + 1))
                        if base is not None:
                            act.wait_ge(s_vp, base + (g - 1))
                        elif g >= 2:
                            act.wait_ge(s_vp, g - 1)
                        act.activation(h_sb[:, g % 2, :], h_ps[g % 2][:, 0:2 * P], ACT.Relu,
                                       bias=b1_sb[:, 0:1]).then_inc(s_hr, 1)

            act.wait_ge(s_w, 16 * LOADS)
            act.activation(sc_out[:, :], ea_sb[:, :], ACT.Tanh).then_inc(s_te, 1)
            block0(None, CB)
            block0(GB, CB)
            with act.Fori(1, ROUNDS) as r:
                for k in range(2):
                    block0(r * (2 * GB) + k * GB, CB)
            block0(NB * GB, TAIL)

            asked = [0]

            def serve(out_ap, in_ap, what):
                asked[0] += 1
                act.wait_ge(s_ain, asked[0])
                act.activation(out_ap, in_ap, what).then_inc(s_aout, 1)

            def norm_parts(c0, c1):
                serve(work[:, c0:c1, :], work2[:, c0:c1, :], ACT.Square)
                serve(nt[:, 2, c0:c1], nt[:, 1, c0:c1], ACT.Sqrt)

            def copy_nodes(l, q):
                c0, c1 = QUARTERS[q]
                for i in range(c0 // 4, -(-c1 // 4)):
                    n = l * NQ + i
                    act.wait_ge(s_nt, n + 1)
                    if n >= 2:
                        act.wait_ge(s_np, n - 1)
                    act.activation(xt_sb[:, n % 2, 0:P], t_ps[n % 2][:, 0:P], ACT.Copy).then_inc(s_ntc, 1)

            for l in range(3):
                for q, (c0, c1) in enumerate(QUARTERS):
                    if l == 0:
                        norm_parts(c0, c1)
                    else:
                        serve(work2[:, c0:c1, :], work2[:, c0:c1, :], ACT.Exp)
                    if q:
                        copy_nodes(l, q - 1)
                copy_nodes(l, len(QUARTERS) - 1)
                done = l * (NB + 1)

                def exps(blocks, n):
                    act.wait_ge(s_exin, blocks)
                    act.activation(ex[:, :, :, 0:n], ex_in[:, :, :, 0:n], ACT.Exp).then_inc(s_ex, 1)

                def copies(n0, columns):
                    for i in columns:
                        act.wait_ge(s_oht, n0 + (i + 1))
                        past = before_reuse(i, n0, RT)
                        if past is not None:
                            act.wait_ge(s_sel, past)
                        act.activation(onehot_t[i % RT], oht_ps[i % RT], ACT.Copy).then_inc(s_ohc, 1)

                first = l * NB * KG
                copies(first, range(KG))
                for b in range(2):
                    copies(first + (b + 1) * KG, range(3))
                    exps(done + b + 1, CB)
                    copies(first + (b + 1) * KG, range(3, KG))
                with act.Fori(1, ROUNDS - 1) as r:
                    for k in range(2):
                        copies(r * (2 * KG) + (first + (k + 1) * KG), range(3))
                        exps(r * 2 + (done + k + 1), CB)
                        copies(r * (2 * KG) + (first + (k + 1) * KG), range(3, KG))
                copies(first + (NB - 1) * KG, range(3))
                exps(done + NB - 1, CB)
                copies(first + (NB - 1) * KG, range(3, KG))
                exps(done + NB, CB)
                exps(done + NB + 1, TAIL)
                act.wait_ge(s_tein, l + 1)
                act.activation(te[:, :, :], te_in[:, :, :], ACT.Exp).then_inc(s_te, 1)
                act.wait_ge(s_fein, l + 1)
                act.activation(fe[:, :, :], fe_in[:, :, :], ACT.Exp).then_inc(s_fe, 1)
            for c0, c1 in QUARTERS:
                norm_parts(c0, c1)

        @block.vector
        def _(dve):
            count = [0]

            def mark(ins):
                count[0] += 1
                ins.then_inc(s_v, 1)

            def link(ins):
                mark(ins)
                dve.wait_ge(s_v, count[0])

            tt, ts, stt = dve.tensor_tensor, dve.tensor_scalar, dve.scalar_tensor_tensor

            hi_i = hi_f.bitcast(I32)
            link(dve.memset(hi_i[96:P, REAL:COLS], N))
            link(dve.memset(src_i[96:P, REAL:COLS], 0))
            link(dve.memset(xn[96:P, NREAL:NCOL, :], 0.0))
            dve.memset(prev_i[:, :], -1).then_inc(s_pads, 1)
            dve.memset(zeros, 0.0).then_inc(s_zs, 1)
            mark(dve.memset(onesn[:, :], 1.0))
            mark(dve.memset(x1[:, NCOL:4 * NQ, :], 0.0))
            mark(dve.memset(fillc[:, :], 0.0))
            mark(dve.memset(maxc[:, :], 0.0))
            mark(dve.memset(si_t[:, 0:1], 0.0))
            mark(dve.memset(mi_t[:, 0:1], 0.0))

            dve.wait_ge(s_dst, 48)
            dve.wait_ge(s_prev, 16)
            mark(dve.tensor_copy(prev_f[:, :], prev_i[:, :]))
            link(dve.tensor_copy(dst_f[:, :], hi_i))
            mark(tt(same[:, 1:COLS], dst_f[:, 1:COLS], dst_f[:, 0:COLS - 1], ALU.is_lt))
            link(tt(same[:, 0:1], dst_f[:, 0:1], prev_f[:, :], ALU.is_lt))
            dve.reduce_sum(viol[:, :], same[:, :], X).then_inc(s_viol, 1)
            dve.wait_ge(s_violp, 1)
            ts(flag_i[:, :], flag_ps, 1.0, None, ALU.min).then_inc(s_flag, 1)
            dve.wait_ge(s_flag, 1)
            unsorted = dve.value_load(flag_i[0:1, 0:1], min_val=0, max_val=1)
            dve.wait_ge(s_const, 1)
            link(dve.tensor_copy(iota_b[:, :], iota_i[:, :]))

            own_s = [0]

            def srt(ins):
                own_s[0] += 1
                ins.then_inc(s_srt, 1)
                dve.wait_ge(s_srt, own_s[0])

            def digit(out_hi, out_lo, values, run, radix=NCOL):
                run(ts(out_hi, values, 0.5, 1.0 / radix, ALU.add, ALU.mult))
                run(ts(out_hi, out_hi, -0.5, None, ALU.add))
                run(ts(out_hi, out_hi, ROUND, None, ALU.add))
                run(ts(out_hi, out_hi, -ROUND, None, ALU.add))
                run(stt(out_lo, out_hi, -float(radix), values, ALU.mult, ALU.add))

            with dve.If(unsorted > 0):
                dve.wait_ge(s_src, 48)
                srt(dve.tensor_copy(recs[:, :, 0], dst_f[:, :]))
                srt(dve.tensor_copy(recs[:, :, 1], src_i[:, :]))
                dve.wait_ge(s_recs, 1)
                srt(dve.tensor_copy(reset[:, :], lo_f.bitcast(I32)))
                ts(recs[:, :, 2], reset[:, :], float(E - 1), None, ALU.min).then_inc(s_recs, 1)
                dve.wait_ge(s_recs, 2)
                srt(dve.memset(cnt, 0.0))
                srt(dve.tensor_copy(upper_b, upper[:, :]))
                srt(dve.memset(ones_b, 1.0))
                digit(hi_f, lo_f, dst_f[:, :], srt)
                for m, (digits_m, values) in enumerate(((lo_f, NCOL), (hi_f, P))):
                    with dve.Fori(0, values) as d:
                        dve.tensor_copy(key[:, 0:1], iota_b[:, bass.ds(d, 1)]).then_inc(s_dig, 1)
                        dve.wait_ge(s_dig, d * 3 + (m * NCOL * 3 + 1))
                        ts(reset[:, :], digits_m, key[:, 0:1], None, ALU.is_equal).then_inc(s_dig, 1)
                        dve.wait_ge(s_dig, d * 3 + (m * NCOL * 3 + 2))
                        dve.reduce_sum(cnt[:, m, bass.ds(d, 1)], reset[:, :], X).then_inc(s_dig, 1)
                        dve.wait_ge(s_dig, d * 3 + (m * NCOL * 3 + 3))
                dve.engine_nop().then_inc(s_cntd, 1)
                dve.wait_ge(s_totd, 1)
                srt(dve.tensor_copy(cnt, total_ps.rearrange("p (m d) -> p m d", m=2)))
                for m in range(2):
                    srt(dve.tensor_tensor_scan(base[:, m, :], ones_f[:, :], cnt[:, m, :], 0.0, ALU.mult, ALU.add))
                srt(tt(base, base, cnt, ALU.subtract))
                STEP = 9
                for m in range(2):
                    with dve.Fori(0, COLS) as t:
                        own = [0]

                        def run(ins):
                            own[0] += 1
                            ins.then_inc(s_srp[m], 1)
                            dve.wait_ge(s_srp[m], t * STEP + own[0])

                        dve.wait_ge(s_rec[m], (t + 1) * 16)
                        digit(key[:, 0:1], key[:, 1:2], rec[:, 0:1], run)
                        of = key[:, 1:2] if m == 0 else key[:, 0:1]
                        ts(oh_s, iota_b[:, :], of, None, ALU.is_equal).then_inc(s_ohs, 1)
                        dve.wait_ge(s_rank, t + (m * COLS + 1))
                        run(tt(places, rank_ps, base[:, m, :], ALU.add))
                        run(tt(places, places, oh_s, ALU.mult))
                        run(dve.reduce_sum(key[:, 2:3], places, X))
                        run(tt(base[:, m, :], base[:, m, :], add_ps, ALU.add))
                        assert own[0] == STEP
                        dve.tensor_copy(pos_i[:, :], key[:, 2:3]).then_inc(s_pos, 1)
                with dve.Fori(0, COLS) as t:
                    dve.wait_ge(s_rec[2], (t + 1) * 16)
                    dve.tensor_copy(pos_i[:, :], rec[:, 2:3]).then_inc(s_eid, 1)
                dve.wait_ge(s_back, 32)
                srt(dve.tensor_copy(dst_f[:, :], recs[:, :, 0]))
                srt(dve.tensor_copy(src_i[:, :], recs[:, :, 1]))
                dve.engine_nop().then_inc(s_sorted, 1)

            mark(dve.memset(same[:, 0:1], 0.0))
            mark(dve.tensor_copy(dst0_i[:, :], dst_f[:, 0:1]))
            digit(hi_f, lo_f, dst_f[:, :], link)
            def onehots(m, k, j0, n, wait):
                if wait is not None:
                    dve.wait_ge(s_cnt, wait)
                dve.tensor_copy(digits[:, 0, 0:n], hi_f[:, bass.ds(j0, n)])
                dve.tensor_copy(digits[:, 1, 0:n], lo_f[:, bass.ds(j0, n)]).then_inc(s_ohd, 1)
                dve.wait_ge(s_ohd, m)
                for d, (rows, values) in enumerate(((oh_hi[k], P), (oh_lo[k], NCOL))):
                    last = tt(rows[:, 0:n, :], iota_b[:, 0:values].unsqueeze(1).broadcast_to([P, n, values]),
                              digits[:, d, 0:n].unsqueeze(2).broadcast_to([P, n, values]), ALU.is_equal)
                last.then_inc(s_oh, 1)
                dve.wait_ge(s_oh, m)

            onehots(1, 0, 0, OH, None)
            onehots(2, 1, OH, OH, None)
            with dve.Fori(1, OHN // 2) as r:
                for k in range(2):
                    onehots(r * 2 + (k + 1), k, r * (2 * OH) + k * OH, OH, r * 2 + (k - 1))
            for m in range(OHN - OHN % 2, OHN + 1):
                onehots(m + 1, m % 2, m * OH, OH if m < OHN else OHT, m - 1)

            dve.wait_ge(s_cnt, OHN + 1)
            link(dve.tensor_copy(deg[:, :], count_ps))
            link(dve.tensor_tensor_scan(cum[:, :], onesn[:, :], deg[:, :], 0.0, ALU.mult, ALU.add))
            dve.tensor_copy(tot[:, :], cum[:, NCOL - 1:NCOL]).then_inc(s_tot, 1)
            mark(ts(has[:, :], deg[:, :], 0.5, None, ALU.is_gt))
            link(dve.tensor_copy(spare[:, :], spare_i[:, :]))
            link(ts(pen[:, :], has[:, :], -1.0, -LOW, ALU.add, ALU.mult))
            dve.wait_ge(s_bef, 1)
            link(dve.tensor_copy(before[:, :], before_ps))
            link(ts(cum[:, :], cum[:, :], before[:, 0:1], None, ALU.add))
            link(tt(nt[:, 0, :], cum[:, :], deg[:, :], ALU.subtract))
            link(tt(nt[:, 0, :], nt[:, 0, :], spare[:, :], ALU.subtract))
            link(tt(nt[:, 0, :], nt[:, 0, :], has[:, :], ALU.mult))
            link(tt(nt[:, 0, :], nt[:, 0, :], spare[:, :], ALU.add))
            mark(dve.tensor_copy(start_i[:, :], nt[:, 0, :]))
            link(ts(nt[:, 1, :], cum[:, :], -1.0, 0.0, ALU.add, ALU.max))
            link(dve.tensor_copy(end_i[:, :], nt[:, 1, :]))

            link(tt(same[:, 1:COLS], dst_f[:, 1:COLS], dst_f[:, 0:COLS - 1], ALU.is_equal))
            link(ts(reset[:, :], same[:, :], -1.0, -LOW, ALU.add, ALU.mult))
            link(tt(cont[:, :], prev_f[:, :], dst_f[:, 0:1], ALU.is_equal))
            link(ts(cmask[:, :], cont[:, :], -1.0, -LOW, ALU.add, ALU.mult))
            link(tt(pt[:, 0:1], dst_f[:, 0:1], dst_f[:, COLS - 1:COLS], ALU.is_equal))
            link(tt(pt[:, 0:1], pt[:, 0:1], cont[:, :], ALU.mult))
            link(ts(pt[:, 0:1], pt[:, 0:1], -1.0, -LOW, ALU.add, ALU.mult))
            link(dve.tensor_copy(wmask[:, :], pt[:, 0:1].broadcast_to([P, ROW])))
            link(ts(hi_f, dst_f[:, :], dst_f[:, 0:1], None, ALU.is_equal))
            link(dve.reduce_sum(pt[:, 1:2], hi_f, X))
            link(dve.tensor_copy(pt[:, 2:3], row0_i[:, :]))
            link(tt(pt[:, 1:2], pt[:, 1:2], pt[:, 2:3], ALU.add))
            link(ts(pt[:, 1:2], pt[:, 1:2], -1.0, None, ALU.add))
            dve.tensor_copy(fe_i[:, :], pt[:, 1:2]).then_inc(s_idx, 1)
            dve.wait_ge(s_src, 48)
            flat = [dst_f[:, i * NB * KG:(i + 1) * NB * KG] for i in range(3)]
            src_v = src_i[:, 0:NB * CB].rearrange("p (b j) -> p b j", j=CB)[:, :, PG:CB]
            link(dve.tensor_copy(flat[0].rearrange("p (b j) -> p b j", j=KG), src_v))
            digit(flat[1], flat[2], flat[0], link)
            digit(flat[0], c1s[:, :, :].rearrange("p b j -> p (b j)"), flat[2], link, C1)
            link(stt(keys[:, :, :].rearrange("p b j -> p (b j)"), flat[0], float(P), flat[1], ALU.mult, ALU.add))
            mark(dve.tensor_copy(iota_key[:, :], iota_ki))
            mark(dve.tensor_copy(iota_c1[:, :], iota_i[:, 0:C1]))
            mark(dve.tensor_copy(ident_b[:, :], ident[:, :]))
            dve.wait_ge(s_wc, 1)
            dve.tensor_copy(wc_sb[:, :, :], wc_ps).then_inc(s_wcs, 1)
            dve.wait_ge(s_te, 1)
            link(ts(sc[:, 0:1], sc_out[:, :], 0.1, None, ALU.is_lt))
            link(ts(sc[:, 1:2], sc[:, 0:1], -1.0, 1.0, ALU.mult, ALU.add))
            link(tt(sc[:, 2:3], sc_out[:, :], sc[:, 1:2], ALU.mult))
            link(tt(sc[:, 2:3], sc[:, 2:3], sc[:, 0:1], ALU.add))

            def fill(k, j0, n, use, blocks):
                dve.wait_ge(s_xd[k], use)
                dve.tensor_copy(same_b[:, 0:n], same[:, bass.ds(j0, n)]).then_inc(s_fs, 1)
                dve.wait_ge(s_fs, blocks * 2 + 1)
                for f in range(D):
                    last = dve.tensor_tensor_scan(slot0[k][:, 0:n, D + f], same_b[:, 0:n], spread[k][:, 0:n, f],
                                                  fillc[:, f:f + 1], ALU.mult, ALU.add)
                last.then_inc(s_fill, 1)
                dve.wait_ge(s_fill, blocks + 1)
                dve.tensor_copy(fillc[:, :], slot0[k][:, n - 1, D:2 * D]).then_inc(s_fs, 1)
                dve.wait_ge(s_fs, blocks * 2 + 2)

            def maxima(k, j0, n, groups, blocks):
                dve.tensor_copy(reset_b[:, 0:n], reset[:, bass.ds(j0, n)]).then_inc(s_ms, 1)
                dve.wait_ge(s_ms, blocks * 2 + 1)
                dve.wait_ge(s_vp, groups)
                for f in range(D):
                    last = dve.tensor_tensor_scan(spread[k][:, 0:n, f], reset_b[:, 0:n], v_ps[:, 0:n, f],
                                                  maxc[:, f:f + 1], ALU.add, ALU.max)
                last.then_inc(s_ms, 1)
                dve.wait_ge(s_ms, blocks * 2 + 2)
                dve.tensor_copy(maxc[:, 0:D], spread[k][:, n - 1, :]).then_inc(s_max, 1)
                dve.wait_ge(s_max, blocks + 1)

            fill(0, 0, CB, 16, 0)
            with dve.Fori(0, ROUNDS - 1) as r:
                for k in range(2):
                    fill(1 - k, r * (2 * CB) + (k + 1) * CB, CB, (r + (k + 1)) * 16, r * 2 + (k + 1))
                    maxima(k, r * (2 * CB) + k * CB, CB, r * (2 * GB) + (k + 1) * GB, r * 2 + k)
            fill(1, (NB - 1) * CB, CB, ROUNDS * 16, NB - 1)
            maxima(0, (NB - 2) * CB, CB, (NB - 1) * GB, NB - 2)
            fill(0, NB * CB, TAIL, (ROUNDS + 1) * 16, NB)
            maxima(1, (NB - 1) * CB, CB, NB * GB, NB - 1)
            maxima(0, NB * CB, TAIL, NB * GB + GT, NB)

            dve.engine_nop().then_inc(s_tail, 1)
            dve.wait_ge(s_tailt, 1)
            link(dve.tensor_copy(wm_t[:, :], t_ps[0][0:ROW, P:2 * P]))
            link(dve.tensor_tensor_scan(si_t[:, 1:P + 1], wm_t[:, :], t_ps[0][0:ROW, 0:P], 0.0, ALU.add, ALU.max))
            dve.engine_nop().then_inc(s_car, 1)
            dve.wait_ge(s_cart, 1)
            link(ts(cs[:, :], t_ps[1][:, 0:ROW], cmask[:, 0:1], None, ALU.add))
            dve.wait_ge(s_fixg, 16)
            tt(fo[:, 0:D], fix[:, 0:D], cs[:, 0:D], ALU.max).then_inc(s_fixv, 1)

            def per_node(v, f=D):
                return v.unsqueeze(2).broadcast_to([P, v.shape[1], f])

            def per_feature(v, n):
                return v.unsqueeze(1).broadcast_to([P, n, D])

            asked = [0]

            def ask(ins):
                asked[0] += 1
                ins.then_inc(s_ain, 1)
                dve.wait_ge(s_aout, asked[0])

            def norm(c0, c1, result):
                wk, wk2 = work[:, c0:c1, :], work2[:, c0:c1, :]
                mean, var, sd, inv = (nt[:, i, c0:c1] for i in range(4))
                link(dve.reduce_sum(mean, wk, X))
                link(ts(mean, mean, 1.0 / D, None, ALU.mult))
                ask(tt(wk2, wk, per_node(mean), ALU.subtract))
                link(dve.reduce_sum(var, wk, X))
                ask(ts(var, var, 1.0 / D, 1e-5, ALU.mult, ALU.add))
                link(dve.reciprocal(inv, sd))
                return tt(result[:, c0:c1, :], wk2, per_node(inv), ALU.mult)

            def finish0(q):
                c0, c1 = QUARTERS[q]
                wk = work[:, c0:c1, :]
                dve.wait_ge(s_nd[q], 16 * (c1 - c0))
                link(tt(wk, nd[:, c0:c1, 0:D], per_feature(b2_sb[:, :], c1 - c0), ALU.add))
                link(tt(wk, wk, per_node(pen[:, c0:c1]), ALU.add))
                link(tt(wk, wk, x1[:, c0:c1, :], ALU.max))
                link(tt(wk, wk, x1[:, c0:c1, :], ALU.add))
                norm(c0, c1, x1).then_inc(s_node, 1)

            def finish(l, q):
                c0, c1 = QUARTERS[q]
                n = c1 - c0
                wk, wk2, rd = work[:, c0:c1, :], work2[:, c0:c1, :], rden[:, c0:c1, :]
                dve.wait_ge(s_nd[q], 16 * n * (l + 2))
                link(ts(rd, nd[:, c0:c1, 0:ROW:HW], 1e-16, None, ALU.add))
                link(dve.reciprocal(rd, rd))
                link(tt(rd, rd, per_node(has[:, c0:c1], 2), ALU.mult))
                link(tt(wk.rearrange("p c (h k) -> p c h k", h=2),
                        nd[:, c0:c1, :].rearrange("p c (h k) -> p c h k", h=2)[:, :, :, 1:17],
                        rd.unsqueeze(3).broadcast_to([P, n, 2, 16]), ALU.mult))
                link(tt(wk, wk, per_feature(bg_sb[:, l, :], n), ALU.add))
                if l == 0:
                    link(ts(wk, wk, sc[:, 2:3], None, ALU.mult))
                    link(stt(wk, wk, 0.05, wk, ALU.mult, ALU.add))
                if l < 2:
                    ask(ts(wk2, wk, 0.0, None, ALU.min))
                    link(ts(wk, wk, 0.0, None, ALU.max))
                    link(stt(wk, wk2, -1.0, wk, ALU.add, ALU.add))
                    if c1 == NCOL:
                        mark(dve.memset(work[:, NCOL:4 * NQ, :], 0.0))
                    ts(wk, wk, -3.0, 3.0, ALU.max, ALU.min).then_inc(s_node, 1)
                else:
                    link(tt(wk, wk, x1[:, c0:c1, :], ALU.add))
                    norm(c0, c1, work2).then_inc(s_fin, 1)

            def take_table(l, q):
                c0, c1 = QUARTERS[q]
                for g in range(c0 // 4, -(-c1 // 4)):
                    n = l * NQ + g
                    dve.wait_ge(s_np, n + 1)
                    prod = h_ps[n % 2][:, 0:4 * KD].rearrange("p (c k) -> p c k", k=KD)
                    dve.tensor_copy(tab[:, 4 * g:4 * g + 4, :], prod[:, :, 0:ROW])
                    dve.tensor_copy(adt[:, 4 * g:4 * g + 4, :], prod[:, :, ROW:KD]).then_inc(s_npc, 1)
                dve.wait_ge(s_npc, n + 1)
                dve.memset(tab[:, c0:c1, 0:ROW:HW], 1.0).then_inc(s_tab, 1)

            for l in range(3):
                for q in range(len(QUARTERS)):
                    if l == 0:
                        finish0(q)
                    else:
                        finish(l - 1, q)
                    if q:
                        take_table(l, q - 1)
                take_table(l, len(QUARTERS) - 1)
                mark(dve.memset(mx[:, :, 0:1], 0.0))
                link(dve.memset(sumc[:, :], 0.0))

                heads = [t.rearrange("p (c k) -> p c k", k=HW - 1) for t in (parts[:, 0, :], parts[:, 1, :])]
                features = tab[:, 0:NCOL, :].rearrange("p c (h k) -> p (c h) k", h=2)[:, :, 1:HW]
                cut = nd_all[:, 0:NCOL * FG].rearrange("p (c k) -> p c k", k=HW - 1)
                link(ts(cut.bitcast(I32), features.bitcast(I32), -(1 << 12), None, ALU.bitwise_and))
                link(dve.tensor_copy(heads[0], cut))
                link(tt(heads[1], features, heads[0].bitcast(F32), ALU.subtract))

                dve.wait_ge(s_adf, 16 * (l + 1))
                for h in range(2):
                    mark(dve.tensor_tensor_scan(adf[:, :, h], same[:, :], adf[:, :, h], 0.0, ALU.mult, ALU.add))
                dve.wait_ge(s_v, count[0])
                done = l * (NB + 1)
                STEPS = 7
                SPACE = 5

                first = l * NB * KG
                def ohe(n0, m, i):
                    past = before_reuse(i, n0, RE)
                    if past is not None:
                        dve.wait_ge(s_oht, past)
                    ts(onehot_e[i % RE], iota_key[:, :], key_b[:, m, i:i + 1], None,
                       ALU.is_equal).then_inc(s_ohe, 1)

                def one_block(v, b):
                    if isinstance(b, int):
                        return v[:, b, :]
                    return v[:, bass.ds(b, 1), :].rearrange("p b j -> p (b j)")

                def keys_of(b, m):
                    dve.tensor_copy(key_b[:, m, :], one_block(keys, b)).then_inc(s_keys, 1)
                    tt(onehot_c1[:, m, :, :], iota_c1[:, :].unsqueeze(1).broadcast_to([P, KG, C1]),
                       one_block(c1s, b).unsqueeze(2).broadcast_to([P, KG, C1]), ALU.is_equal).then_inc(s_keys, 1)
                    dve.wait_ge(s_keys, (b + l * NB) * 2 + 2)

                def columns(n0, k, wanted, ahead=True):
                    for i in wanted:
                        dve.wait_ge(s_sel, n0 + (i + 1))
                        past = before_reuse(i, n0, 2)
                        if past is not None:
                            dve.wait_ge(s_row, past)
                        prod = sel_ps[i % RS].rearrange("p (c f) -> p c f", f=FG)
                        mine = picked[:, i % 2, :].rearrange("p (c f) -> p c f", f=FG)
                        tt(mine, prod, onehot_c1[:, k, i, :].unsqueeze(2).broadcast_to([P, C1, FG]),
                           ALU.mult).then_inc(s_pick, 1)
                        if i + RE < KG:
                            ohe(n0, k, i + RE)
                        elif ahead:
                            ohe(n0 + KG, 1 - k, i + RE - KG)
                        dve.wait_ge(s_pick, n0 + (i + 1))
                        dve.reduce_sum(slotg[k][:, PG + i, :].rearrange("p (h k) -> p h k", h=2)[:, :, 1:HW],
                                       picked[:, i % 2, :].rearrange("p (c h k) -> p h k c", c=C1, h=2),
                                       X).then_inc(s_row, 1)

                def blockg(k, j0, n, use, blocks, rows_in=None, meanwhile=None):
                    own = [0]

                    def chain(ins):
                        own[0] += 1
                        ins.then_inc(s_own, 1)
                        dve.wait_ge(s_own, blocks * STEPS + own[0])

                    rows = slotg[k][:, 0:n, :]
                    logit = rows[:, :, HW - 1:ROW:HW].rearrange("p j h -> p h j")
                    if meanwhile is not None:
                        meanwhile([0])
                    dve.wait_ge(s_g[l][k], use)
                    if rows_in is not None:
                        dve.wait_ge(s_row, rows_in)
                    chain(tt(lg[:, :, 0:n], logit, adf[:, bass.ds(j0, n), :].rearrange("p j h -> p h j"), ALU.add))
                    chain(stt(lg[:, :, 0:n], lg[:, :, 0:n], SLOPES[l], lg[:, :, 0:n], ALU.mult, ALU.max))
                    dve.tensor_copy(reset_b[:, 0:n], reset[:, bass.ds(j0, n)]).then_inc(s_own, 1)
                    own[0] += 1
                    dve.wait_ge(s_own, blocks * STEPS + own[0])
                    for h in range(2):
                        last = dve.tensor_tensor_scan(mx[:, h, 1:n + 1], reset_b[:, 0:n], lg[:, h, 0:n],
                                                      mx[:, h, 0:1], ALU.add, ALU.max)
                    chain(last)
                    tt(ex_in[:, 1, :, 0:n], lg[:, :, 0:n], mx[:, :, 1:n + 1], ALU.subtract)
                    dve.tensor_copy(rows[:, :, HW - 1:ROW:HW].rearrange("p j h -> p h j"), mx[:, :, 1:n + 1])
                    chain(tt(ex_in[:, 0, :, 0:n], mx[:, :, 0:n],
                             reset_b[:, 0:n].unsqueeze(1).broadcast_to([P, 2, n]), ALU.add))
                    tt(ex_in[:, 0, :, 0:n], ex_in[:, 0, :, 0:n], mx[:, :, 1:n + 1], ALU.subtract).then_inc(s_exin, 1)
                    if meanwhile is not None:
                        meanwhile([1])
                    dve.wait_ge(s_ex, blocks + 1)
                    parts = rows.rearrange("p j (h k) -> p j h k", h=2)[:, :, :, 0:HW - 1]
                    weights = ex[:, 1, :, 0:n].rearrange("p h j -> p j h").unsqueeze(3).broadcast_to([P, n, 2, HW - 1])
                    chain(tt(parts, parts, weights, ALU.mult))
                    sums = [(h, h * HW + c) for h in range(2) for c in range(HW - 1)]
                    for i, (h, c) in enumerate(sums):
                        if meanwhile is not None and i and i % SPACE == 0:
                            meanwhile([1 + i // SPACE])
                        last = dve.tensor_tensor_scan(rows[:, :, c], ex[:, 0, h, 0:n], rows[:, :, c],
                                                      sumc[:, c:c + 1], ALU.mult, ALU.add)
                    chain(last)
                    assert own[0] == STEPS
                    dve.tensor_copy(mx[:, :, 0:1], mx[:, :, n:n + 1])
                    dve.tensor_copy(sumc[:, :], rows[:, n - 1, :]).then_inc(s_sum, 1)
                    dve.wait_ge(s_sum, blocks + 1)

                def window(r, k, ahead=True):
                    n1 = r * (2 * KG) + (first + (k + 1) * KG)
                    if ahead:
                        keys_of(r * 2 + (k + 2), k)
                    if not (isinstance(r, int) and r + k == 0):
                        dve.wait_ge(s_st[l][1 - k], (r + k) * 16)
                    dve.memset(slotg[1 - k][:, PG:CB, 0:ROW:HW], 1.0)
                    blockg(k, r * (2 * CB) + k * CB, CB, (r + 1) * (16 * PG), r * 2 + (done + k), n1,
                           lambda wanted: columns(n1, 1 - k, wanted, ahead))
                    columns(n1, 1 - k, range(1 + -(-2 * (HW - 1) // SPACE), KG), ahead)

                keys_of(0, 0)
                keys_of(1, 1)
                for i in range(RE):
                    ohe(first, 0, i)
                dve.memset(slotg[0][:, PG:CB, 0:ROW:HW], 1.0)
                columns(first, 0, range(KG))
                window(0, 0)
                window(0, 1)
                with dve.Fori(1, ROUNDS - 1) as r:
                    for k in range(2):
                        window(r, k)
                window(ROUNDS - 1, 0, ahead=False)
                blockg(1, (NB - 1) * CB, CB, ROUNDS * 16 * PG, done + NB - 1, first + NB * KG)
                blockg(0, NB * CB, TAIL, ROUNDS * 16 * PG + 16 * TAIL, done + NB)

                dve.tensor_copy(mrep[:, :].rearrange("p (h k) -> p h k", h=2),
                                sumc[:, HW - 1:ROW:HW].unsqueeze(2).broadcast_to([P, 2, HW])).then_inc(s_tail, 1)
                dve.wait_ge(s_tailt, l + 2)
                mark(dve.tensor_copy(wm_t[:, :], t_ps[0][0:ROW, P:2 * P]))
                link(dve.tensor_copy(m_t[:, :], t_ps[0][0:ROW, 2 * P:3 * P]))
                link(dve.tensor_tensor_scan(mi_t[:, 1:P + 1], wm_t[:, :], m_t[:, :], 0.0, ALU.add, ALU.max))
                mark(tt(te_in[:, 0, :], mi_t[:, 0:P], wm_t[:, :], ALU.add))
                link(tt(te_in[:, 1, :], m_t[:, :], mi_t[:, 1:P + 1], ALU.subtract))
                tt(te_in[:, 0, :], te_in[:, 0, :], mi_t[:, 1:P + 1], ALU.subtract).then_inc(s_tein, 1)
                dve.wait_ge(s_te, l + 2)
                link(tt(m_t[:, :], te[:, 1, :], t_ps[0][0:ROW, 0:P], ALU.mult))
                dve.tensor_tensor_scan(si_t[:, 1:P + 1], te[:, 0, :], m_t[:, :], 0.0, ALU.mult, ALU.add).then_inc(s_car, 1)
                dve.wait_ge(s_cart, l + 2)
                dve.wait_ge(s_fixg, 16 * (l + 2))
                mark(dve.tensor_copy(cs[:, :], t_ps[1][:, 0:ROW]))
                link(ts(cm[:, :], t_ps[1][:, 64 + HW - 1:64 + ROW:HW], cmask[:, 0:1], None, ALU.add))
                link(tt(vm[:, :], cm[:, :], fix[:, HW - 1:ROW:HW], ALU.max))
                mark(tt(fe_in[:, 0, :], fix[:, HW - 1:ROW:HW], vm[:, :], ALU.subtract))
                tt(fe_in[:, 1, :], cm[:, :], vm[:, :], ALU.subtract).then_inc(s_fein, 1)
                dve.wait_ge(s_fe, l + 1)
                both = [t[:, :].rearrange("p (h k) -> p h k", h=2) for t in (fix, cs, fo)]
                mark(tt(both[0], both[0], fe[:, 0, :].unsqueeze(2).broadcast_to([P, 2, HW]), ALU.mult))
                link(tt(both[1], both[1], fe[:, 1, :].unsqueeze(2).broadcast_to([P, 2, HW]), ALU.mult))
                tt(both[2], both[0], both[1], ALU.add).then_inc(s_fixv, 1)

            for q in range(len(QUARTERS)):
                finish(2, q)


_INS = ['x', 'src', 'dst', 'edge_attr_32', 'L0_gnn_W1', 'L0_gnn_b1', 'L0_gnn_W2', 'L0_gnn_b2', 'L1_gnn_W1',
        'L1_gnn_att_s1', 'L1_gnn_att_d1', 'L1_gnn_b1', 'L1_gnn_ea1', 'L1_gnn_W2', 'L1_gnn_att_s2',
        'L1_gnn_att_d2', 'L1_gnn_b2', 'L1_gnn_W3', 'L1_gnn_att_s3', 'L1_gnn_att_d3', 'L1_gnn_b3']


def kernel(**inputs):
    import numpy as _np
    import concourse.bacc as _bacc
    from concourse import mybir as _mybir
    from concourse.bass_utils import run_bass_kernel_spmd as _run

    nc = _bacc.Bacc("TRN2", target_bir_lowering=False, num_devices=1)
    arrays, a = {}, {}
    for name in _INS:
        v = _np.ascontiguousarray(inputs[name])
        arrays[f"in_{name}"] = v
        a[name] = nc.dram_tensor(f"in_{name}", v.shape, _mybir.dt.from_np(v.dtype), kind="ExternalInput").ap()
    out = nc.dram_tensor("out_0", a['x'].shape, _mybir.dt.float32, kind="ExternalOutput").ap()
    gat = [tuple(a[f'L1_gnn_{n}{i}'] for n in ('W', 'att_s', 'att_d', 'b')) for i in (1, 2, 3)]
    gnn_program(nc, a['x'], a['src'], a['dst'], a['edge_attr_32'], a['L0_gnn_W1'], a['L0_gnn_b1'],
                a['L0_gnn_W2'], a['L0_gnn_b2'], gat, a['L1_gnn_ea1'], out)
    r = _run(nc, [arrays], core_ids=[0])
    return r.results[0]["out_0"]
```
